# Optimizing a Trainium2 kernel written in Bass

```python
import numpy as np
import jax
import jax.numpy as jnp

def _softmax(x, axis=-1):
    return jax.nn.softmax(x, axis=axis)

def _gelu(x):
    return jax.nn.gelu(x, approximate=True)

def _silu(x):
    return jax.nn.silu(x)

def _sigmoid(x):
    return jax.nn.sigmoid(x)

def _layernorm(x, axis=-1, eps=1e-05):
    m = jnp.mean(x, axis=axis, keepdims=True)
    v = jnp.var(x, axis=axis, keepdims=True)
    return (x - m) / jnp.sqrt(v + eps)

def _scatter_add(tgt, idx, src, axis=0):
    return tgt.at[idx].add(src)

def _segment_sum(src, seg, n):
    return jax.ops.segment_sum(src, seg, n)
kernel_name = 'mk_adj_ffn_d1_adj_r2_bfab72'

def setup_inputs(seed: int=0):
    np.random.seed(seed)
    _w = jnp.asarray

    def _rec_inputs():
        import jax
        import jax.numpy as jnp
        _gk = jax.random.key(seed)
        x = -0.0002422 + 1 * jax.random.normal(jax.random.fold_in(_gk, 1), (16, 512, 512), jnp.float32)
        _a = jax.random.bernoulli(jax.random.fold_in(_gk, 2), 0.00390625, (16, 512, 512))
        adj = _a.astype(jnp.int32)
        return (x, adj)
    x, adj = _rec_inputs()

    def _L0_gnn_setup():
        import jax, jax.numpy as jnp
        import numpy as np
        IN_DIM = 512
        OUT_DIM = 512
        BATCH = 128
        NUM_OBJS = 100
        key = jax.random.key(seed)
        k1, k2, k3, k4, k5 = jax.random.split(key, 5)
        stdv = 1.0 / np.sqrt(OUT_DIM)
        feature = jax.random.normal(k1, (BATCH, NUM_OBJS, IN_DIM), dtype=jnp.float32)
        graph = jax.random.randint(k2, (BATCH, NUM_OBJS, NUM_OBJS), 0, 2, dtype=jnp.int32)
        weight = jax.random.uniform(k3, (IN_DIM, OUT_DIM), dtype=jnp.float32, minval=-stdv, maxval=stdv)
        wq = jax.random.uniform(k4, (IN_DIM, OUT_DIM), dtype=jnp.float32, minval=-stdv, maxval=stdv)
        wk = jax.random.uniform(k5, (IN_DIM, OUT_DIM), dtype=jnp.float32, minval=-stdv, maxval=stdv)
        return {'feature': feature, 'graph': graph, 'weight': weight, 'wq': wq, 'wk': wk}
    _L0_gnn_all = _L0_gnn_setup()
    _L0_gnn_in = {k: v for k, v in _L0_gnn_all.items() if k in ('weight', 'wq', 'wk')}
    del _L0_gnn_all

    def _L0_ffn_setup():
        import jax, jax.numpy as jnp
        import numpy as np
        D_MODEL = 512
        N_EXPERTS = 8
        CAPACITY = 256
        TOP_K = 2
        BATCH, SEQ = (4, 1024)
        key = jax.random.key(seed)
        k1, k2, k3, k4 = jax.random.split(key, 4)
        x = jax.random.normal(k1, (BATCH, SEQ, D_MODEL), dtype=jnp.float32)
        Wg = jax.random.normal(k2, (D_MODEL, N_EXPERTS), dtype=jnp.float32) * 0.02
        W1 = jax.random.normal(k3, (N_EXPERTS, D_MODEL, CAPACITY), dtype=jnp.float32) * 0.02
        W2 = jax.random.normal(k4, (N_EXPERTS, CAPACITY, D_MODEL), dtype=jnp.float32) * 0.02
        return {'x': x, 'Wg': Wg, 'W1': W1, 'W2': W2}
    _L0_ffn_all = _L0_ffn_setup()
    _L0_ffn_in = {k: v for k, v in _L0_ffn_all.items() if k in ('Wg', 'W1', 'W2')}
    del _L0_ffn_all
    return {'x': x, 'adj': adj, 'L0_gnn_weight': _L0_gnn_in['weight'], 'L0_gnn_wq': _L0_gnn_in['wq'], 'L0_gnn_wk': _L0_gnn_in['wk'], 'L0_ffn_Wg': _L0_ffn_in['Wg'], 'L0_ffn_W1': _L0_ffn_in['W1'], 'L0_ffn_W2': _L0_ffn_in['W2']}

def reference(x, adj, L0_gnn_weight, L0_gnn_wq, L0_gnn_wk, L0_ffn_Wg, L0_ffn_W1, L0_ffn_W2):
    import jax
    import jax.numpy as jnp

    def _L0_gnn_ref(feature, graph, weight, wq, wk):
        import jax, jax.numpy as jnp
        import numpy as np
        IN_DIM = 512
        OUT_DIM = 512
        BATCH = 128
        NUM_OBJS = 100
        output = jnp.einsum('bni,io->bno', feature, weight)
        q = jnp.einsum('bni,io->bno', feature, wq)
        k = jnp.einsum('bni,io->bno', feature, wk)
        alpha = jnp.einsum('bno,bmo->bnm', q, k)
        alpha = jnp.maximum(alpha, 0.0) * (graph != 0).astype(alpha.dtype)
        alpha = jax.nn.softmax(alpha, axis=1)
        return jnp.einsum('bnm,bmo->bno', alpha, output)

    def _L0_ffn_ref(x, Wg, W1, W2):
        import jax, jax.numpy as jnp
        import numpy as np
        D_MODEL = 512
        N_EXPERTS = 8
        CAPACITY = 256
        TOP_K = 2
        BATCH, SEQ = (4, 1024)
        B, S, D = x.shape
        T = B * S
        E = W1.shape[0]
        xf = x.reshape(T, D)
        logits = xf @ Wg
        topk_scores, topk_idx = jax.lax.top_k(logits, TOP_K)
        probs = jax.nn.softmax(topk_scores, axis=-1)
        combine = jnp.zeros((T, E), dtype=x.dtype)
        combine = combine.at[jnp.arange(T)[:, None], topk_idx].add(probs)
        h = jax.nn.relu(jnp.einsum('td,edc->etc', xf, W1))
        y = jnp.einsum('etc,ecd->etd', h, W2)
        out = jnp.einsum('te,etd->td', combine, y)
        return out.reshape(B, S, D)
    x = x + _L0_gnn_ref(_layernorm(x, axis=-1), adj, L0_gnn_weight, L0_gnn_wq, L0_gnn_wk)
    x = x + _L0_ffn_ref(_layernorm(x, axis=-1), L0_ffn_Wg, L0_ffn_W1, L0_ffn_W2)
    return x

_drawn_inputs = setup_inputs


def setup_inputs(seed=0):
    import zlib

    import numpy as np

    out = dict(_drawn_inputs(seed))
    spreads = {}
    factors = {}
    for name, (base, spread) in spreads.items():
        noise = np.random.default_rng([zlib.crc32(name.encode()), seed]).standard_normal(out[name].shape)
        drawn = base * np.exp(spread * noise) if base else spread * noise
        out[name] = jnp.asarray(drawn.astype(out[name].dtype))
    for name, factor in factors.items():
        out[name] = (out[name] * factor).astype(out[name].dtype)
    return out
```

```python
from contextlib import ExitStack

import concourse.bass as bass
from concourse import mybir

F32 = mybir.dt.float32
F16 = mybir.dt.float16
I32 = mybir.dt.int32
U32 = mybir.dt.uint32
ALU = mybir.AluOpType
ACT = mybir.ActivationFunctionType
AX = mybir.AxisListType.X
RMAX = bass.bass_isa.ReduceOp.max

P = 128
EPS = 1e-5
SX = 2.0 ** 8
SW = 2.0 ** 8
TO32 = 2.0 ** -11
TO_Y = 1.0 / (32.0 * SW)
SPROB = 2.0 ** 14
SX2 = 2.0 ** 3
SW1 = 2.0 ** 2


def build_program(nc, x, adj, weight, wq, wk, Wg, W1, W2, out):
    B, N, D = x.shape
    E, _, C = W1.shape
    JT = N // P
    KT = D // P
    CT = C // P
    T = B * N
    TILES = B * JT
    ROWS = 256
    SUB = ROWS // P
    REGION = T + ROWS
    MAXT = (2 * T + E * (ROWS - 1)) // ROWS
    NT = MAXT + MAXT % 2
    assert JT == 4 and KT == 4 and CT == 2 and E == 8 and B % 2 == 0

    sorted_x = nc.dram_tensor("sorted_x", [E * REGION, 2 * D], F16).ap()
    sorted_y = nc.dram_tensor("sorted_y", [NT * ROWS, D], F32).ap()
    x1_dram = nc.dram_tensor("x1_dram", [B, P, JT * D], F32).ap()

    x_v = x.rearrange("b (p j) d -> b p (j d)", j=JT)
    adj_v = adj.rearrange("b (p j) m -> b p (j m)", j=JT)
    out_v = out.rearrange("b (p j) d -> b p (j d)", j=JT)
    w1_v = W1.rearrange("e (k p) c -> e p k c", p=P)
    w2_v = W2.rearrange("e (k p) d -> e p k d", p=P)

    with ExitStack() as ctx:
        def sb(name, shape, dt):
            return ctx.enter_context(nc.sbuf_tensor(name, shape, dt))

        def pb(name, shape, dt):
            return ctx.enter_context(nc.psum_tensor(name, shape, dt))

        def sem(name):
            return ctx.enter_context(nc.semaphore(name))

        ident = sb("ident", [P, P], F32)
        ident16 = sb("ident16", [P, P], F16)
        before = sb("before", [P, P], F16)
        ones16 = sb("ones16", [P, P], F16)
        minus_half = sb("minus_half", [P, JT], F32)
        expert_iota = sb("expert_iota", [P, E], F32)
        WM = sb("WM", [P, 2, KT, D], F16)
        WV = sb("WV", [P, 2, KT, D], F16)
        WG = sb("WG", [P, 2, KT, E], F16)
        W1H = sb("W1H", [P, E, KT * C], F16)
        W1L = sb("W1L", [P, E, KT * C], F16)
        W2H = sb("W2H", [P, E, CT * D], F16)
        W2L = sb("W2L", [P, E, CT * D], F16)
        wraw = sb("wraw", [P, KT * C], F32)
        wg_raw = sb("wg_raw", [P, KT * E], F32)
        X = sb("X", [P, 2, JT * D], F32)
        ADJ = sb("ADJ", [P, JT * N], I32)
        MK = sb("MK", [P, JT * N], F16)
        MKT = sb("MKT", [P, JT, N], F16)
        XN = sb("XN", [P, JT, D], F32)
        XTH = sb("XTH", [P, 2, KT, N], F16)
        XTL = sb("XTL", [P, 2, KT, N], F16)
        TT = sb("TT", [P, 2, KT, N], F16)
        VV = sb("VV", [P, 2, JT, D], F16)
        PR = sb("PR", [P, 2, JT, N], F16)
        RL = sb("RL", [P, 2, N], F32)
        EX = sb("EX", [P, 2, N], F32)
        XN2 = sb("XN2", [P, 2, D], F32)
        X2S = sb("X2S", [P, 2, JT, 2 * D], F16)
        X2T = sb("X2T", [P, 2, 2 * KT, P], F16)
        OHA = sb("OHA", [P, 2, TILES, E], F16)
        DL = sb("DL", [P, TILES], F32)
        SLOT = sb("SLOT", [P, 2, TILES], F32)
        YROW = sb("YROW", [P, 2, TILES], I32)
        to_y = sb("to_y", [P, E], F32)
        LG = sb("LG", [P, JT, E], F32)
        top = sb("top", [P, JT, E], F32)
        tix = sb("tix", [P, JT, E], U32)
        tixf = sb("tixf", [P, 2, JT], F32)
        OH = sb("OH", [P, 2, JT, E], F32)
        OHS = sb("OHS", [P, JT, E], F16)
        row_of = sb("row_of", [P, JT, E], F32)
        picked = sb("picked", [P, 2, JT, E], F32)
        slot = sb("slot", [P, 2, 2, JT], I32)
        slotf = sb("slotf", [P, 2, JT], F32)
        R = sb("R", [P, E], F32)
        base = sb("base", [P, E], F32)
        earlier = sb("earlier", [P, E, E], F32)
        cnt = sb("cnt", [P, E], F32)
        cnti = sb("cnti", [P, E], I32)
        ntile = sb("ntile", [P, E], F32)
        tend = sb("tend", [P, E], F32)
        tstart = sb("tstart", [P, E], F32)
        tile_iota = sb("tile_iota", [P, NT], F32)
        TAB = sb("TAB", [P, 2, NT], I32)
        padrow = sb("padrow", [P, 2, E], I32)
        iota_p = sb("iota_p", [P, 2, E], F32)
        inv12 = sb("inv12", [P, E], F32)
        gx = sb("gx", [P, TILES], F32)
        gd = sb("gd", [P, TILES], F32)
        gr = sb("gr", [P, TILES], F32)
        GE = sb("GE", [P, 2, TILES], F32)
        F12 = sb("F12", [P, 2, TILES], F32)
        gidx = sb("gidx", [P, 2, 2, JT], I32)
        k_gate = sb("k_gate", [P, 1], F32)
        bs = sb("bs", [P, 2, JT, 6], F32)
        mv = sb("mv", [P, 2, JT, 2], F32)
        ve = sb("ve", [P, 2, JT], F32)
        rs = sb("rs", [P, 2, JT], F32)
        rr = sb("rr", [P, 2, JT], F32)
        nm = sb("nm", [P, 2, JT], F32)
        nb = sb("nb", [P, 2, JT], F32)
        smax = sb("smax", [P, JT], F32)
        sbias = sb("sbias", [P, JT], F32)
        ssum = sb("ssum", [P, JT], F32)
        srec = sb("srec", [P, JT], F32)
        srs = sb("srs", [P, JT], F32)
        mxp = sb("mxp", [P, KT], F32)
        mx = sb("mx", [P, 3], F32)
        mxa = sb("mxa", [P, 3], F32)
        ebits = sb("ebits", [P, 3], I32)
        ibits = sb("ibits", [P, 3], I32)
        wsc = sb("wsc", [P, 3], F32)
        k_pos = sb("k_pos", [P, 1], F32)
        k_neg = sb("k_neg", [P, 1], F32)
        g_res = sb("g_res", [P, 1], F32)
        emx = sb("emx", [P, 1], F32)
        emxa = sb("emxa", [P, 1], F32)
        eebits = sb("eebits", [P, 2 * E], I32)
        eibits = sb("eibits", [P, 1], I32)
        esc = sb("esc", [P, 1], F32)

        ACC = [pb(f"ACC{j}", [P, 512], F32) for j in range(4)]
        TX = [pb(f"TX{j}", [P, 512], F32) for j in range(2)]
        MT = pb("MT", [P, 512], F32)
        RB = pb("RB", [P, 512], F32)

        s_const = sem("s_const")
        s_passed = sem("s_passed")
        s_wq = sem("s_wq")
        s_wk = sem("s_wk")
        s_wv = sem("s_wv")
        s_wg = sem("s_wg")
        s_wtp = sem("s_wtp")
        s_wta = sem("s_wta")
        s_wtd = sem("s_wtd")
        s_m = sem("s_m")
        s_pmx = sem("s_pmx")
        s_mxa = sem("s_mxa")
        s_sc = sem("s_sc")
        s_whi = sem("s_whi")
        s_wlo = sem("s_wlo")
        s_x = [sem(f"s_x{i}") for i in range(2)]
        s_adj = sem("s_adj")
        s_wr = sem("s_wr")
        s_bn = sem("s_bn")
        s_mv = sem("s_mv")
        s_lna = sem("s_ln")
        s_nba = sem("s_nb")
        s_xn = sem("s_xn")
        s_xtp = sem("s_xtp")
        s_xth = sem("s_xth")
        s_xtl = sem("s_xtl")
        s_mk = sem("s_mk")
        s_mtp = sem("s_mtp")
        s_mkt = sem("s_mkt")
        s_tp = sem("s_tp")
        s_th = sem("s_th")
        s_tl = sem("s_tl")
        s_sp = sem("s_sp")
        s_rl = sem("s_rl")
        s_z = sem("s_z")
        s_sb = sem("s_sb")
        s_ex = sem("s_ex")
        s_rec = sem("s_rec")
        s_srs = sem("s_srs")
        s_ph = sem("s_ph")
        s_pl = sem("s_pl")
        s_vp = sem("s_vp")
        s_vh = sem("s_vh")
        s_vl = sem("s_vl")
        s_op = sem("s_op")
        s_res = sem("s_res")
        s_x1 = sem("s_x1_stored")
        s_bn2 = sem("s_bn2")
        s_mv2 = sem("s_mv2")
        s_ln2 = sem("s_ln2")
        s_nb2 = sem("s_nb2")
        s_xn2 = sem("s_xn2")
        s_x2h = sem("s_x2h")
        s_x2l = sem("s_x2l")
        s_x2p = sem("s_x2p")
        s_x2t = sem("s_x2t")
        s_lg = sem("s_lg")
        s_lgc = sem("s_lgc")
        s_top = sem("s_top")
        s_tix = sem("s_tix")
        s_txf = sem("s_txf")
        s_oh = sem("s_oh")
        s_ohs = sem("s_ohs")
        s_dl = sem("s_dl")
        s_pos = sem("s_pos")
        s_row = sem("s_row")
        s_pick = sem("s_pick")
        s_slot = sem("s_slot")
        s_sc2 = [sem(f"s_scat{i}") for i in range(2)]
        s_tab = sem("s_tab")
        s_pad = sem("s_pad")
        s_xf = [sem(f"s_xf{i}") for i in range(2)]
        s_fp = sem("s_fp")
        s_fh = sem("s_fh")
        s_fl = sem("s_fl")
        s_hp = sem("s_hp")
        s_hh = sem("s_hh")
        s_hl = sem("s_hl")
        s_yp = sem("s_yp")
        s_y0 = sem("s_y0")
        s_y1 = sem("s_y1")
        s_ys = [sem(f"s_ys{i}") for i in range(2)]
        s_fac = sem("s_fac")
        s_gexp = sem("s_gexp")
        s_gi = sem("s_gi")
        s_ga = [sem(f"s_ga{i}") for i in range(2)]
        s_xo = [sem(f"s_xo{i}") for i in range(2)]
        s_c1 = sem("s_c1")
        s_c2 = sem("s_c2")
        s_out = sem("s_out")
        s_ea = sem("s_ea")
        s_eg = sem("s_eg")
        s_es = sem("s_es")
        s_eh = sem("s_eh")
        s_el = sem("s_el")

        WQR = PR[:, :, :, :].rearrange("p a j n -> p (a j n)").bitcast(F32)
        WKR = TT[:, :, :, :].rearrange("p a j n -> p (a j n)").bitcast(F32)
        WVR = VV[:, :, :, :].rearrange("p a j n -> p (a j n)").bitcast(F32)
        WQT = W2H[:, E - 4:E, :].rearrange("p e n -> p (e n)").bitcast(F32)
        WKT = W2L[:, E - 4:E, :].rearrange("p e n -> p (e n)").bitcast(F32)
        BANKS = ACC + TX
        XF = ADJ[:, :].bitcast(F16).rearrange("p (b s n) -> p b s n", b=2, s=SUB)
        XFT = XN[:, :, :].rearrange("p j d -> p (j d)").bitcast(F16).rearrange(
            "p (b a k n) -> p b a k n", b=2, a=2, k=KT)
        HH = RL[:, :, :].rearrange("p a n -> p (a n)").bitcast(F16).rearrange("p (b a n) -> p b a n", b=2, a=2)
        YF = XTH[:, :, :, :].rearrange("p a j n -> p (a j n)").bitcast(F32).rearrange(
            "p (b s d) -> p b s d", b=2, s=SUB)
        FT = [TX[a][:, :].bitcast(F16) for a in range(2)]
        HB = [ACC[0], ACC[1]]
        YB = [[ACC[2], ACC[3]], [MT, RB]]
        zeros = EX[:, :, :].rearrange("p a n -> p (a n)").bitcast(F16)[:, 0:2 * D]
        scratch = WM[:, :, :, :].rearrange("p a k n -> p (a k n)").bitcast(F32)
        past, pastn = [scratch[:, a * NT * E:(a + 1) * NT * E].rearrange("p (t e) -> p t e", e=E) for a in range(2)]
        tin, tex, tst, trow, tdif = [scratch[:, (2 * E + a) * NT:(2 * E + a + 1) * NT] for a in range(5)]
        tmpee = scratch[:, (2 * E + 6) * NT:(2 * E + 6) * NT + E * E].rearrange("p (a b) -> p a b", b=E)
        Y1 = [t[:, :, :, :].rearrange("p a j n -> p (a j n)").bitcast(F32) for t in (TT, VV)]
        Y2 = [PR[:, :, :, :].rearrange("p a j n -> p (a j n)").bitcast(F32),
              XN[:, :, :].rearrange("p j d -> p (j d)")]
        MASKB = [MT[:, :].bitcast(F16), TX[0][:, :].bitcast(F16)]

        N_FAC = 12
        N_TAB = 20

        block = ctx.enter_context(nc.Block())

        def settle(engine):
            engine.sem_inc(s_passed, 1)

        def Xt(par, j):
            return X[:, par, j * D:(j + 1) * D]

        @block.sync
        def _(sp):
            def load_x(b, par, first=False):
                if not first:
                    sp.wait_ge(s_x2h, 4 * (b - 1))
                    settle(sp)
                    sp.wait_ge(s_xn2, 4 * (b - 1))
                    settle(sp)
                    sp.wait_ge(s_x1, 16 * (b - 1))
                    settle(sp)
                sp.dma_start(X[:, par, :], x_v[b]).then_inc(s_x[par], 16)

            def load_adj(b, first=False):
                if not first:
                    sp.wait_ge(s_mk, b)
                    settle(sp)
                sp.dma_start(ADJ[:, :], adj_v[b]).then_inc(s_adj, 16)

            load_x(0, 0, first=True)
            sp.dma_start(WQR.rearrange("p (k o) -> p k o", k=KT),
                         wq.rearrange("(k p) o -> p k o", p=P)).then_inc(s_wq, 16)
            sp.dma_start(WKR.rearrange("p (k o) -> p k o", k=KT),
                         wk.rearrange("(k p) o -> p k o", p=P)).then_inc(s_wk, 16)
            sp.dma_start(WVR.rearrange("p (k o) -> p k o", k=KT),
                         weight.rearrange("(k p) o -> p k o", p=P)).then_inc(s_wv, 16)
            sp.dma_start(wg_raw[:, :].rearrange("p (k e) -> p k e", k=KT),
                         Wg.rearrange("(k p) e -> p k e", p=P)).then_inc(s_wg, 16)
            load_adj(0, first=True)
            load_x(1, 1, first=True)

            def graph(i, par, last=False):
                b = 2 * i + par
                if not (last and par == 1) and not (isinstance(b, int) and b == 0):
                    load_x(b + 1, 1 - par)
                sp.wait_ge(s_el, b)
                settle(sp)
                if par == 0:
                    sp.dma_start(wraw[:, :].rearrange("p (k c) -> p k c", k=KT), w1_v[i]).then_inc(s_wr, 16)
                else:
                    sp.dma_start(wraw[:, :].rearrange("p (k c) -> p k c", k=CT), w2_v[i]).then_inc(s_wr, 16)
                if not (last and par == 1):
                    load_adj(b + 1)
                sp.wait_ge(s_res, 4 * (b + 1))
                settle(sp)
                sp.dma_start(x1_dram[b], X[:, par, :]).then_inc(s_x1, 16)

            graph(0, 0)
            graph(0, 1)
            graph(1, 0)
            graph(1, 1)
            with sp.Fori(2, B // 2 - 1) as i:
                graph(i, 0)
                graph(i, 1)
            graph(B // 2 - 1, 0, last=True)
            graph(B // 2 - 1, 1, last=True)
            def load_rows(n, par, free=True):
                row = sp.value_load(TAB[0:1, 1, bass.ds(n, 1)], min_val=0, max_val=E * REGION - ROWS)
                if free:
                    sp.wait_ge(s_fp, n - 1)
                    settle(sp)
                src = sorted_x[bass.ds(row, ROWS), :].rearrange("(p s) n -> p s n", s=SUB)
                sp.dma_start(XF[:, par], src).then_inc(s_xf[par], 16)

            for par in range(2):
                sp.wait_ge(s_sc2[par], 2 * JT * 16 * (B // 2))
            sp.wait_ge(s_pad, 2 * E * 16)
            sp.wait_ge(s_tab, N_TAB)
            load_rows(0, 0, free=False)
            load_rows(1, 1, free=False)
            with sp.Fori(1, NT // 2) as i:
                load_rows(2 * i, 0)
                load_rows(2 * i + 1, 1)

            for par in range(2):
                sp.wait_ge(s_x1, 16 * B)
                sp.dma_start(X[:, par, :], x1_dram[par]).then_inc(s_xo[par], 16)

            def store_out(i, par, again=True):
                b = 2 * i + par
                sp.wait_ge(s_c2, JT * (b + 1))
                settle(sp)
                sp.dma_start(out_v[b], X[:, par, :]).then_inc(s_out, 16)
                if again:
                    sp.wait_ge(s_out, 16 * (b + 1))
                    settle(sp)
                    sp.dma_start(X[:, par, :], x1_dram[b + 2]).then_inc(s_xo[par], 16)

            with sp.Fori(0, B // 2 - 1) as i:
                store_out(i, 0)
                store_out(i, 1)
            store_out(B // 2 - 1, 0, again=False)
            store_out(B // 2 - 1, 1, again=False)
            sp.wait_ge(s_out, 16 * B)

        @block.gpsimd
        def _(pool):
            pool.memset(ident[:, :], 0.0).then_inc(s_const, 1)
            pool.memset(ones16[:, :], 1.0).then_inc(s_const, 1)
            pool.memset(minus_half[:, :], -0.5).then_inc(s_const, 1)
            pool.iota(expert_iota[:, :], pattern=[[1, E]], base=0, channel_multiplier=0,
                      allow_small_or_imprecise_dtypes=True).then_inc(s_const, 1)
            pool.iota(R[:, :], pattern=[[REGION, E]], base=0, channel_multiplier=0,
                      allow_small_or_imprecise_dtypes=True).then_inc(s_const, 1)
            pool.iota(base[:, :], pattern=[[REGION, E]], base=0, channel_multiplier=0,
                      allow_small_or_imprecise_dtypes=True).then_inc(s_const, 1)
            pool.iota(tile_iota[:, :], pattern=[[1, NT]], base=0, channel_multiplier=0,
                      allow_small_or_imprecise_dtypes=True).then_inc(s_const, 1)
            pool.iota(iota_p[:, :, :], pattern=[[P, 2], [0, E]], base=0, channel_multiplier=1,
                      allow_small_or_imprecise_dtypes=True).then_inc(s_const, 1)
            pool.memset(earlier[:, :, :], 1.0).then_inc(s_const, 1)
            pool.wait_ge(s_const, 9)
            pool.affine_select(out=earlier[:, :, :], in_=earlier[:, :, :], compare_op=ALU.is_gt, fill=0.0, base=0,
                               pattern=[[1, E], [-1, E]], channel_multiplier=0).then_inc(s_const, 1)
            pool.affine_select(out=ident[:, :], in_=ident[:, :], compare_op=ALU.not_equal, fill=1.0, base=0,
                               pattern=[[-1, P]], channel_multiplier=1).then_inc(s_const, 1)
            pool.affine_select(out=before[:, :], in_=ones16[:, :], compare_op=ALU.is_gt, fill=0.0, base=0,
                               pattern=[[1, P]], channel_multiplier=-1).then_inc(s_const, 1)
            pool.wait_ge(s_const, 12)
            pool.tensor_copy(ident16[:, :], ident[:, :]).then_inc(s_const, 1)

            def layernorm_scale(b, q):
                s_m_v, s_ln, s_nb, scale = ((s_mv, s_lna, s_nba, SX), (s_mv2, s_ln2, s_nb2, SX2))[q]
                n_ln = 3 * b
                pool.wait_ge(s_m_v, 4 * (b + 1))
                settle(pool)
                pool.tensor_scalar(ve[:, q, :], mv[:, q, :, 1], 1.0, EPS, ALU.mult, ALU.add).then_inc(s_ln, 1)
                pool.tensor_scalar(nm[:, q, :], mv[:, q, :, 0], -scale, 0.0, ALU.mult, ALU.add).then_inc(s_ln, 1)
                pool.wait_ge(s_ln, n_ln + 2)
                pool.tensor_tensor(rs[:, q, :], ve[:, q, :], minus_half[:, :], ALU.pow).then_inc(s_ln, 1)
                pool.wait_ge(s_ln, n_ln + 3)
                settle(pool)
                pool.tensor_scalar(rr[:, q, :], rs[:, q, :], scale, 0.0, ALU.mult, ALU.add).then_inc(s_nb, 1)
                pool.tensor_tensor(nb[:, q, :], nm[:, q, :], rs[:, q, :], ALU.mult).then_inc(s_nb, 1)

            layernorm_scale(0, 0)
            pool.wait_ge(s_pmx, 7)
            pool.partition_all_reduce(mxa[:, :], mx[:, :], P, RMAX).then_inc(s_mxa, 1)

            def rows(r, par, turn):
                pool.wait_ge(s_nb2, 2 * (r + 1))
                if not isinstance(r, int) or r >= 2:
                    pool.wait_ge(s_sc2[par], 2 * JT * 16 * turn)
                    pool.wait_ge(s_x2p, 4 * (r - 1))
                settle(pool)
                for j in range(JT):
                    if not isinstance(r, int) or r > 0 or j >= 2:
                        pool.wait_ge(s_x2l, 4 * r + j - 1)
                        settle(pool)
                    pool.tensor_scalar(XN2[:, j % 2, :], Xt(par, j), rr[:, 1, j:j + 1], nb[:, 1, j:j + 1],
                                       ALU.mult, ALU.add).then_inc(s_xn2, 1)
                    pool.tensor_scalar(X2S[:, par, j, 0:D], Xt(par, j), rr[:, 1, j:j + 1], nb[:, 1, j:j + 1],
                                       ALU.mult, ALU.add).then_inc(s_x2h, 1)
                    pool.wait_ge(s_xn2, 4 * r + j + 1)
                    pool.wait_ge(s_x2h, 4 * r + j + 1)
                    pool.tensor_tensor(X2S[:, par, j, D:2 * D], XN2[:, j % 2, :], X2S[:, par, j, 0:D],
                                       ALU.subtract).then_inc(s_x2l, 1)

            def scatter(r, par):
                pool.wait_ge(s_slot, 2 * (r + 1))
                settle(pool)
                for j in range(JT):
                    for c in range(2):
                        pool.indirect_dma_start(
                            out=sorted_x, out_offset=bass.IndirectOffsetOnAxis(ap=slot[:, par, c, j:j + 1], axis=0),
                            in_=X2S[:, par, j, :], in_offset=None).then_inc(s_sc2[par], 16)

            def graph(i, par, last=False):
                b = 2 * i + par
                r = b - 1
                static = isinstance(b, int)
                if not static or b > 0:
                    layernorm_scale(r, 1)
                    rows(r, 1 - par, i - 1 + par)
                if not (last and par == 1):
                    layernorm_scale(b + 1, 0)
                pool.wait_ge(s_ea, b + 1)
                settle(pool)
                pool.partition_all_reduce(emxa[:, :], emx[:, :], P, RMAX).then_inc(s_eg, 1)
                if not static or b > 0:
                    scatter(r, 1 - par)

            graph(0, 0)
            graph(0, 1)
            graph(1, 0)
            graph(1, 1)
            with pool.Fori(2, B // 2 - 1) as i:
                graph(i, 0)
                graph(i, 1)
            graph(B // 2 - 1, 0, last=True)
            graph(B // 2 - 1, 1, last=True)

            layernorm_scale(B - 1, 1)
            rows(B - 1, 1, B // 2 - 1)
            scatter(B - 1, 1)
            pool.memset(zeros, 0.0).then_inc(s_const, 1)
            pool.wait_ge(s_const, 14)
            pool.wait_ge(s_tab, 2)
            for h in range(2):
                for e in range(E):
                    pool.indirect_dma_start(
                        out=sorted_x, out_offset=bass.IndirectOffsetOnAxis(ap=padrow[:, h, e:e + 1], axis=0),
                        in_=zeros, in_offset=None).then_inc(s_pad, 16)

            def store_rows(n, par):
                pool.wait_ge(s_y0, n + 1)
                pool.wait_ge(s_y1, n + 1)
                settle(pool)
                dst = sorted_y[bass.ds(n * ROWS, ROWS), :].rearrange("(p s) d -> p s d", s=SUB)
                pool.dma_start(dst, YF[:, par]).then_inc(s_ys[par], 16)

            with pool.Fori(0, NT // 2) as i:
                store_rows(2 * i, 0)
                store_rows(2 * i + 1, 1)

            pool.wait_ge(s_fac, N_FAC)
            for par in range(2):
                pool.wait_ge(s_ys[par], 16 * (NT // 2))

            def gather(i, par, first=False):
                b = 2 * i + par
                if not first:
                    pool.wait_ge(s_c2, JT * (b - 1))
                    settle(pool)
                pool.tensor_copy(gidx[:, par, :, :], YROW[:, :, bass.ds(JT * b, JT)]).then_inc(s_gi, 1)
                pool.wait_ge(s_gi, b + 1)
                settle(pool)
                for j in range(JT):
                    for c, Y in enumerate((Y1, Y2)):
                        pool.indirect_dma_start(
                            out=Y[par][:, j * D:(j + 1) * D], out_offset=None, in_=sorted_y,
                            in_offset=bass.IndirectOffsetOnAxis(ap=gidx[:, par, c, j:j + 1], axis=0)
                        ).then_inc(s_ga[par], 16)

            gather(0, 0, first=True)
            gather(0, 1, first=True)
            with pool.Fori(1, B // 2) as i:
                gather(i, 0)
                gather(i, 1)

        @block.scalar
        def _(act):
            for t in range(0, 8, 2):
                act.wait_ge(s_wtp, t + 1)
                dst = (WQT if t < 4 else WKT)[:, (t % 4) * D:(t % 4 + 1) * D]
                act.activation(dst, BANKS[t % 6][:, :], ACT.Copy).then_inc(s_wta, 1)

            def xn_tiles(b, par, tiles=range(JT)):
                act.wait_ge(s_nba, 2 * (b + 1))
                for j in tiles:
                    if j == 0 and not isinstance(b, int):
                        act.wait_ge(s_xtp, 4 * b)
                    elif j == 0 and b > 0:
                        act.wait_ge(s_xtp, 4 * b)
                    act.activation(XN[:, j, :], Xt(par, j), ACT.Identity, scale=rr[:, 0, j:j + 1],
                                   bias=nb[:, 0, j:j + 1]).then_inc(s_xn, 1)

            def xt_high(b, par, tiles=range(JT)):
                for j in tiles:
                    act.wait_ge(s_xtp, 4 * b + j + 1)
                    act.activation(XTH[:, par, :, j * P:(j + 1) * P],
                                   TX[j % 2][:, :].rearrange("p (k n) -> p k n", k=KT), ACT.Copy).then_inc(s_xth, 1)

            def mask_t(b, halves=range(2)):
                for h in halves:
                    act.wait_ge(s_mtp, 2 * b + h + 1)
                    act.activation(MKT[:, 2 * h:2 * h + 2, :].rearrange("p j n -> p (j n)"), MASKB[h],
                                   ACT.Copy).then_inc(s_mkt, 1)

            def x2_t(r, j):
                act.wait_ge(s_x2p, 4 * r + j + 1)
                if not isinstance(r, int) or r > 0 or j >= 2:
                    act.wait_ge(s_lg, 4 * r + j - 1)
                act.activation(X2T[:, j % 2, :, :].rearrange("p k n -> p (k n)"), TX[j % 2][:, :].bitcast(F16),
                               ACT.Copy).then_inc(s_x2t, 1)

            xn_tiles(0, 0)
            act.wait_ge(s_sc, 4)
            for k in range(KT):
                act.activation(WM[:, 0, k, :], ACC[k][:, :], ACT.Copy, scale=wsc[:, 0:1]).then_inc(s_whi, 1)
            for k in range(KT):
                act.activation(WV[:, 0, k, :], WVR[:, k * D:(k + 1) * D], ACT.Copy, scale=wsc[:, 1:2]).then_inc(s_whi, 1)
            act.activation(WG[:, 0, :, :].rearrange("p k e -> p (k e)"), wg_raw[:, :], ACT.Copy,
                           scale=wsc[:, 2:3]).then_inc(s_whi, 1)
            xt_high(0, 0)
            mask_t(0)

            def graph(i, par, last=False):
                b = 2 * i + par
                front = not (last and par == 1)

                def t_high(j):
                    act.wait_ge(s_tp, 4 * b + j + 1)
                    act.activation(TT[:, 0, j, :], ACC[j][:, :], ACT.Copy, scale=TO32).then_inc(s_th, 1)

                for j in range(JT):
                    t_high(j)

                def relu(j):
                    act.wait_ge(s_sp, 4 * b + j + 1)
                    act.activation(RL[:, j % 2, :], ACC[j][:, :], ACT.Relu).then_inc(s_rl, 1)

                def exp_and_high(j):
                    act.wait_ge(s_sb, 4 * b + j + 1)
                    act.activation(EX[:, j % 2, :], RL[:, j % 2, :], ACT.Exp, scale=k_pos[:, 0:1],
                                   bias=sbias[:, j:j + 1], accum_out=ssum[:, j:j + 1]).then_inc(s_ex, 1)
                    act.wait_ge(s_srs, 4 * b + j + 1)
                    act.activation(PR[:, 0, j, :], EX[:, j % 2, :], ACT.Copy, scale=srs[:, j:j + 1]).then_inc(s_ph, 1)

                relu(0)
                relu(1)
                for j in range(JT):
                    exp_and_high(j)
                    if j + 2 < JT:
                        relu(j + 2)
                for j in range(JT):
                    if j < 2 and (not isinstance(b, int) or b > 0):
                        x2_t(b - 1, 2 * j)
                        x2_t(b - 1, 2 * j + 1)
                    act.wait_ge(s_vp, 4 * b + j + 1)
                    act.activation(VV[:, 0, j, :], ACC[j][:, :], ACT.Copy, scale=TO32).then_inc(s_vh, 1)
                    if front:
                        if j == 0:
                            xn_tiles(b + 1, 1 - par, [0])
                        if j == 1:
                            xn_tiles(b + 1, 1 - par, [1, 2, 3])
                        if j == 2:
                            xt_high(b + 1, 1 - par, [0, 1])
                        if j == 3:
                            mask_t(b + 1, [0])
                            xt_high(b + 1, 1 - par, [2, 3])
                            mask_t(b + 1, [1])
                act.wait_ge(s_es, 4 * (b + 1))
                settle(act)
                hi = (W1H if par == 0 else W2H)[:, bass.ds(i, 1), :].rearrange("p o n -> p (o n)")
                act.activation(hi, wraw[:, :], ACT.Copy, scale=esc[:, 0:1]).then_inc(s_eh, 1)

            graph(0, 0)
            graph(0, 1)
            graph(1, 0)
            graph(1, 1)
            with act.Fori(2, B // 2 - 1) as i:
                graph(i, 0)
                graph(i, 1)
            graph(B // 2 - 1, 0, last=True)
            graph(B // 2 - 1, 1, last=True)

            for j in range(JT):
                x2_t(B - 1, j)

            act.wait_ge(s_fac, 1)
            act.activation(gx[:, :], DL[:, :], ACT.Exp, scale=k_gate[:, 0:1]).then_inc(s_gexp, 1)

            def expert_tile(n, par, transposed=True):
                act.wait_ge(s_hp, n + 1)
                act.activation(HH[:, par, 0, :], HB[par][:, :], ACT.Relu).then_inc(s_hh, 1)
                if transposed:
                    act.wait_ge(s_fp, n + 2)
                    act.activation(XFT[:, 1 - par, 0].rearrange("p k n -> p (k n)"), FT[0], ACT.Copy).then_inc(s_fh, 1)

            def result(n, par, again=True):
                if again:
                    act.wait_ge(s_ys[par], 8 * (n - par))
                act.wait_ge(s_yp, 2 * n + 1)
                act.activation(YF[:, par, 0, :], YB[par][0][:, :], ACT.Copy, scale=TO_Y).then_inc(s_y0, 1)

            act.wait_ge(s_fp, 1)
            act.activation(XFT[:, 0, 0].rearrange("p k n -> p (k n)"), FT[0], ACT.Copy).then_inc(s_fh, 1)
            expert_tile(0, 0)
            expert_tile(1, 1)
            result(0, 0, again=False)
            expert_tile(2, 0)
            result(1, 1, again=False)
            with act.Fori(1, NT // 2 - 1) as i:
                expert_tile(2 * i + 1, 1)
                result(2 * i, 0)
                expert_tile(2 * i + 2, 0)
                result(2 * i + 1, 1)
            expert_tile(NT - 1, 1, transposed=False)
            result(NT - 2, 0)
            result(NT - 1, 1)

        @block.vector
        def _(dve):
            def statistics(b, par, q):
                s_b, s_m_v = ((s_bn, s_mv), (s_bn2, s_mv2))[q]
                for j in range(JT):
                    if q:
                        dve.wait_ge(s_res, 4 * b + j + 1)
                    dve.bn_stats(bs[:, q, j, :], Xt(par, j)).then_inc(s_b, 1)
                dve.wait_ge(s_b, 4 * (b + 1))
                settle(dve)
                for j in range(JT):
                    dve.bn_aggr(mv[:, q, j, :], bs[:, q, j, :]).then_inc(s_m_v, 1)

            def route(r):
                dve.wait_ge(s_lg, 4 * (r + 1))
                dve.tensor_copy(LG[:, :, :], RB[:, 0:JT * E].rearrange("p (j e) -> p j e", j=JT)).then_inc(s_lgc, 1)
                dve.wait_ge(s_lgc, r + 1)
                settle(dve)
                for j in range(JT):
                    dve.max(top[:, j, :], LG[:, j, :]).then_inc(s_top, 1)
                dve.wait_ge(s_top, 4 * (r + 1))
                settle(dve)
                for j in range(JT):
                    dve.max_index(tix[:, j, :], top[:, j, :], LG[:, j, :]).then_inc(s_tix, 1)
                dve.tensor_tensor(DL[:, bass.ds(JT * r, JT)], top[:, :, 1], top[:, :, 0], ALU.subtract).then_inc(s_dl, 1)
                dve.wait_ge(s_tix, 4 * (r + 1))
                dve.tensor_copy(tixf[:, :, :], tix[:, :, 0:2].rearrange("p j c -> p c j")).then_inc(s_txf, 1)
                dve.wait_ge(s_txf, r + 1)
                for c in range(2):
                    dve.tensor_tensor(OH[:, c, :, :], tixf[:, c, :].unsqueeze(2).broadcast_to([P, JT, E]),
                                      expert_iota[:, :].unsqueeze(1).broadcast_to([P, JT, E]),
                                      ALU.is_equal).then_inc(s_oh, 1)
                dve.wait_ge(s_oh, 2 * (r + 1))
                dve.tensor_tensor(OHS[:, :, :], OH[:, 0, :, :], OH[:, 1, :, :], ALU.add).then_inc(s_ohs, 1)
                dve.tensor_copy(OHA[:, :, bass.ds(JT * r, JT), :].rearrange("p c j e -> p c (j e)"),
                                OH[:, :, :, :].rearrange("p c j e -> p c (j e)")).then_inc(s_dl, 1)

            def place(r, par, turn):
                dve.wait_ge(s_pos, r + 1)
                counts = RB[:, 64:64 + (JT + 1) * E].rearrange("p (j e) -> p j e", e=E)
                dve.tensor_tensor(row_of[:, :, :], counts[:, 0:JT, :], R[:, :].unsqueeze(1).broadcast_to([P, JT, E]),
                                  ALU.add).then_inc(s_row, 1)
                dve.wait_ge(s_row, 2 * r + 1)
                dve.tensor_tensor(R[:, :], R[:, :], counts[:, JT, :], ALU.add).then_inc(s_row, 1)
                for c in range(2):
                    dve.tensor_tensor(picked[:, c, :, :], OH[:, c, :, :], row_of[:, :, :], ALU.mult).then_inc(s_pick, 1)
                dve.wait_ge(s_pick, 3 * r + 2)
                dve.tensor_reduce(slotf[:, :, :], picked[:, :, :, :], AX, ALU.add).then_inc(s_pick, 1)
                dve.wait_ge(s_pick, 3 * r + 3)
                if not isinstance(r, int) or r >= 2:
                    dve.wait_ge(s_sc2[par], 2 * JT * 16 * turn)
                settle(dve)
                dve.tensor_copy(slot[:, par, :, :], slotf[:, :, :]).then_inc(s_slot, 1)
                dve.tensor_copy(SLOT[:, :, bass.ds(JT * r, JT)], slotf[:, :, :]).then_inc(s_slot, 1)

            def mask(b):
                dve.wait_ge(s_adj, 16 * (b + 1))
                if not (isinstance(b, int) and b == 0):
                    dve.wait_ge(s_mtp, 2 * b)
                dve.tensor_scalar(MK[:, :], ADJ[:, :], 0.0, None, ALU.not_equal).then_inc(s_mk, 1)

            def xt_low(b, par, tiles=range(JT)):
                for j in tiles:
                    dve.wait_ge(s_xth, 4 * b + j + 1)
                    dve.tensor_tensor(XTL[:, par, :, j * P:(j + 1) * P],
                                      TX[j % 2][:, :].rearrange("p (k n) -> p k n", k=KT),
                                      XTH[:, par, :, j * P:(j + 1) * P], ALU.subtract).then_inc(s_xtl, 1)

            dve.wait_ge(s_x[0], 16)
            statistics(0, 0, 0)
            for t in range(1, 8, 2):
                dve.wait_ge(s_wtp, t + 1)
                dst = (WQT if t < 4 else WKT)[:, (t % 4) * D:(t % 4 + 1) * D]
                dve.tensor_copy(dst, BANKS[t % 6][:, :]).then_inc(s_wtd, 1)
            dve.wait_ge(s_wv, 16)
            dve.tensor_reduce(mx[:, 1:2], WVR, AX, ALU.max, apply_absolute_value=True).then_inc(s_pmx, 1)
            dve.wait_ge(s_wg, 16)
            dve.tensor_reduce(mx[:, 2:3], wg_raw[:, :], AX, ALU.max, apply_absolute_value=True).then_inc(s_pmx, 1)
            mask(0)
            for k in range(KT):
                dve.wait_ge(s_m, k + 1)
                dve.tensor_reduce(mxp[:, k:k + 1], ACC[k][:, :], AX, ALU.max,
                                  apply_absolute_value=True).then_inc(s_pmx, 1)
            dve.wait_ge(s_pmx, 6)
            dve.tensor_reduce(mx[:, 0:1], mxp[:, :], AX, ALU.max).then_inc(s_pmx, 1)

            dve.wait_ge(s_mxa, 1)
            dve.tensor_scalar(mx[:, :], mxa[:, :], 2.0 ** -90, 2.0 ** 90, ALU.max, ALU.min).then_inc(s_sc, 1)
            dve.wait_ge(s_sc, 1)
            dve.tensor_scalar(ebits[:, :], mx[:, :].bitcast(I32), 0x7F800000, None, ALU.bitwise_and).then_inc(s_sc, 1)
            dve.wait_ge(s_sc, 2)
            dve.tensor_scalar(ibits[:, :], ebits[:, :], -1.0, float(254 << 23), ALU.mult, ALU.add).then_inc(s_sc, 1)
            dve.wait_ge(s_sc, 3)
            dve.tensor_scalar(wsc[:, :], ibits[:, :].bitcast(F32), SW, None, ALU.mult).then_inc(s_sc, 1)
            ef = ebits[:, :].bitcast(F32)
            dve.tensor_scalar(k_pos[:, :], ef[:, 0:1], 1.0 / (SX * 32.0), None, ALU.mult).then_inc(s_sc, 1)
            dve.tensor_scalar(k_neg[:, :], ef[:, 0:1], -1.0 / (SX * 32.0), None, ALU.mult).then_inc(s_sc, 1)
            dve.tensor_scalar(g_res[:, :], ef[:, 1:2], 1.0 / (SPROB * 32.0), None, ALU.mult).then_inc(s_sc, 1)
            dve.tensor_scalar(k_gate[:, :], ef[:, 2:3], 1.0 / (SX2 * SW), None, ALU.mult).then_inc(s_sc, 1)
            for k in range(KT):
                dve.wait_ge(s_whi, k + 1)
                if k == 0:
                    dve.wait_ge(s_sc, 8)
                dve.scalar_tensor_tensor(out=WM[:, 1, k, :], in0=ACC[k][:, :], scalar=wsc[:, 0:1],
                                         in1=WM[:, 0, k, :], op0=ALU.mult, op1=ALU.subtract).then_inc(s_wlo, 1)
            for k in range(KT):
                dve.wait_ge(s_whi, KT + k + 1)
                dve.scalar_tensor_tensor(out=WV[:, 1, k, :], in0=WVR[:, k * D:(k + 1) * D], scalar=wsc[:, 1:2],
                                         in1=WV[:, 0, k, :], op0=ALU.mult, op1=ALU.subtract).then_inc(s_wlo, 1)
            dve.wait_ge(s_whi, 2 * KT + 1)
            dve.scalar_tensor_tensor(out=WG[:, 1, :, :].rearrange("p k e -> p (k e)"), in0=wg_raw[:, :],
                                     scalar=wsc[:, 2:3], in1=WG[:, 0, :, :].rearrange("p k e -> p (k e)"),
                                     op0=ALU.mult, op1=ALU.subtract).then_inc(s_wlo, 1)
            xt_low(0, 0)

            def graph(i, par, last=False):
                b = 2 * i + par
                front = not (last and par == 1)
                for j in range(JT):
                    dve.wait_ge(s_th, 4 * b + j + 1)
                    dve.scalar_tensor_tensor(out=TT[:, 1, j, :], in0=ACC[j][:, :], scalar=TO32, in1=TT[:, 0, j, :],
                                             op0=ALU.mult, op1=ALU.subtract).then_inc(s_tl, 1)
                def masked_max(j):
                    dve.wait_ge(s_rl, 4 * b + j + 1)
                    if j == 0:
                        dve.wait_ge(s_mkt, 2 * (b + 1))
                    settle(dve)
                    rl = RL[:, j % 2, :]
                    dve.tensor_tensor_reduce(rl, rl, MKT[:, j, :], 1.0, 0.0, ALU.mult, ALU.max,
                                             smax[:, j:j + 1]).then_inc(s_z, 1)
                    dve.wait_ge(s_z, 4 * b + j + 1)
                    dve.tensor_scalar(sbias[:, j:j + 1], smax[:, j:j + 1], k_neg[:, 0:1], None,
                                      ALU.mult).then_inc(s_sb, 1)

                def inverse_sum(j):
                    dve.wait_ge(s_ex, 4 * b + j + 1)
                    dve.reciprocal(srec[:, j:j + 1], ssum[:, j:j + 1]).then_inc(s_rec, 1)
                    dve.wait_ge(s_rec, 4 * b + j + 1)
                    dve.tensor_scalar(srs[:, j:j + 1], srec[:, j:j + 1], SPROB, None, ALU.mult).then_inc(s_srs, 1)

                def prob_low(j):
                    dve.wait_ge(s_ph, 4 * b + j + 1)
                    dve.scalar_tensor_tensor(out=PR[:, 1, j, :], in0=EX[:, j % 2, :], scalar=srs[:, j:j + 1],
                                             in1=PR[:, 0, j, :], op0=ALU.mult, op1=ALU.subtract).then_inc(s_pl, 1)

                masked_max(0)
                masked_max(1)
                for j in range(JT):
                    inverse_sum(j)
                    prob_low(j)
                    if j + 2 < JT:
                        masked_max(j + 2)

                if front:
                    dve.wait_ge(s_x[1 - par], 16 * (i + 1 + par))
                    statistics(b + 1, 1 - par, 0)
                routed = not isinstance(b, int) or b > 0
                dve.wait_ge(s_wr, 16 * (b + 1))
                dve.tensor_reduce(emx[:, :], wraw[:, :], AX, ALU.max, apply_absolute_value=True).then_inc(s_ea, 1)
                for j in range(JT):
                    dve.wait_ge(s_vh, 4 * b + j + 1)
                    dve.scalar_tensor_tensor(out=VV[:, 1, j, :], in0=ACC[j][:, :], scalar=TO32, in1=VV[:, 0, j, :],
                                             op0=ALU.mult, op1=ALU.subtract).then_inc(s_vl, 1)
                    if j == 0:
                        dve.wait_ge(s_eg, b + 1)
                        dve.tensor_scalar(emx[:, :], emxa[:, :], 2.0 ** -60, 2.0 ** 60, ALU.max,
                                          ALU.min).then_inc(s_es, 1)
                        dve.wait_ge(s_es, 4 * b + 1)
                        eb = eebits[:, bass.ds(i + E * par, 1)]
                        dve.tensor_scalar(eb, emx[:, :].bitcast(I32), 0x7F800000, None,
                                          ALU.bitwise_and).then_inc(s_es, 1)
                        dve.wait_ge(s_es, 4 * b + 2)
                        dve.tensor_scalar(eibits[:, :], eb, -1.0, float(254 << 23), ALU.mult,
                                          ALU.add).then_inc(s_es, 1)
                        dve.wait_ge(s_es, 4 * b + 3)
                        dve.tensor_scalar(esc[:, :], eibits[:, :].bitcast(F32), SW if par else SW1, None,
                                          ALU.mult).then_inc(s_es, 1)
                    if front:
                        if j == 1:
                            mask(b + 1)
                        if j == 2:
                            xt_low(b + 1, 1 - par, [0, 1])
                        if j == 3:
                            xt_low(b + 1, 1 - par, [2, 3])
                if routed:
                    route(b - 1)
                dve.wait_ge(s_eh, b + 1)
                settle(dve)
                sl = bass.ds(i, 1)
                hi, lo = (W1H, W1L) if par == 0 else (W2H, W2L)
                dve.scalar_tensor_tensor(out=lo[:, sl, :].rearrange("p o n -> p (o n)"), in0=wraw[:, :],
                                         scalar=esc[:, 0:1], in1=hi[:, sl, :].rearrange("p o n -> p (o n)"),
                                         op0=ALU.mult, op1=ALU.subtract).then_inc(s_el, 1)
                for j in range(JT):
                    dve.wait_ge(s_op, 4 * b + j + 1)
                    dve.scalar_tensor_tensor(out=Xt(par, j), in0=ACC[j][:, :], scalar=g_res[:, 0:1], in1=Xt(par, j),
                                             op0=ALU.mult, op1=ALU.add).then_inc(s_res, 1)
                    if j == 2 and routed:
                        place(b - 1, 1 - par, i - 1 + par)
                statistics(b, par, 1)

            graph(0, 0)
            graph(0, 1)
            graph(1, 0)
            graph(1, 1)
            with dve.Fori(2, B // 2 - 1) as i:
                graph(i, 0)
                graph(i, 1)
            graph(B // 2 - 1, 0, last=True)
            graph(B // 2 - 1, 1, last=True)

            route(B - 1)
            place(B - 1, 1, B // 2 - 1)

            steps = [0]

            def step(instruction):
                steps[0] += 1
                instruction.then_inc(s_tab, 1)
                dve.wait_ge(s_tab, steps[0])

            dve.wait_ge(s_row, 2 * B)
            dve.wait_ge(s_slot, 2 * B)
            step(dve.tensor_tensor(past[:, 0:2, :], iota_p[:, :, :], R[:, :].unsqueeze(1).broadcast_to([P, 2, E]),
                                   ALU.add))
            step(dve.tensor_copy(padrow[:, :, :], past[:, 0:2, :]))
            step(dve.scalar_tensor_tensor(out=cnt[:, :], in0=R[:, :], scalar=float(ROWS - 1), in1=base[:, :],
                                          op0=ALU.add, op1=ALU.subtract))
            step(dve.tensor_copy(cnti[:, :], cnt[:, :]))
            step(dve.tensor_scalar(cnti[:, :], cnti[:, :], ROWS.bit_length() - 1, None, ALU.logical_shift_right))
            step(dve.tensor_copy(ntile[:, :], cnti[:, :]))
            step(dve.tensor_tensor(tmpee[:, :, :], earlier[:, :, :], ntile[:, :].unsqueeze(1).broadcast_to([P, E, E]),
                                   ALU.mult))
            step(dve.tensor_reduce(tstart[:, :], tmpee[:, :, :], AX, ALU.add))
            step(dve.tensor_tensor(tend[:, :], tstart[:, :], ntile[:, :], ALU.add))
            step(dve.tensor_scalar(tdif[:, 0:1], tend[:, E - 1:E], -1.0, None, ALU.add))
            step(dve.tensor_scalar(tin[:, :], tile_iota[:, :], tdif[:, 0:1], None, ALU.min))
            step(dve.tensor_tensor(past[:, :, :], tin[:, :].unsqueeze(2).broadcast_to([P, NT, E]),
                                   tend[:, :].unsqueeze(1).broadcast_to([P, NT, E]), ALU.is_ge))
            step(dve.tensor_tensor(pastn[:, :, :], past[:, :, :], ntile[:, :].unsqueeze(1).broadcast_to([P, NT, E]),
                                   ALU.mult))
            step(dve.tensor_reduce(tex[:, :], past[:, :, :], AX, ALU.add))
            step(dve.tensor_reduce(tst[:, :], pastn[:, :, :], AX, ALU.add))
            step(dve.tensor_tensor(trow[:, :], tin[:, :], tst[:, :], ALU.subtract))
            step(dve.tensor_scalar(trow[:, :], trow[:, :], float(ROWS), None, ALU.mult))
            step(dve.scalar_tensor_tensor(out=trow[:, :], in0=tex[:, :], scalar=float(REGION), in1=trow[:, :],
                                          op0=ALU.mult, op1=ALU.add))
            step(dve.tensor_copy(TAB[:, 0, :], tex[:, :]))
            step(dve.tensor_copy(TAB[:, 1, :], trow[:, :]))
            assert steps[0] == N_TAB

            fsteps = [0]

            def fstep(instruction):
                fsteps[0] += 1
                instruction.then_inc(s_fac, 1)
                dve.wait_ge(s_fac, fsteps[0])

            dve.wait_ge(s_dl, 2 * B)
            ef = eebits[:, :].bitcast(F32)
            fstep(dve.tensor_tensor(inv12[:, :], ef[:, 0:E], ef[:, E:2 * E], ALU.mult))
            flat = OHA[:, :, :, :].rearrange("p c t e -> p (c t) e")
            prod = WM[:, :, :, :].rearrange("p a k n -> p (a k n)").bitcast(F32)[:, 0:2 * TILES * E].rearrange(
                "p (t e) -> p t e", e=E)
            fstep(dve.tensor_tensor(prod, flat, inv12[:, :].unsqueeze(1).broadcast_to([P, 2 * TILES, E]), ALU.mult))
            fstep(dve.tensor_reduce(GE[:, :, :].rearrange("p c t -> p (c t)"), prod, AX, ALU.add))
            fstep(dve.scalar_tensor_tensor(out=to_y[:, :], in0=tstart[:, :], scalar=float(ROWS), in1=base[:, :],
                                           op0=ALU.mult, op1=ALU.subtract))
            fstep(dve.tensor_tensor(prod, flat, to_y[:, :].unsqueeze(1).broadcast_to([P, 2 * TILES, E]), ALU.mult))
            slots = SLOT[:, :, :].rearrange("p c t -> p (c t)")
            fstep(dve.tensor_reduce(F12[:, :, :].rearrange("p c t -> p (c t)"), prod, AX, ALU.add))
            fstep(dve.tensor_tensor(YROW[:, :, :].rearrange("p c t -> p (c t)"), slots,
                                    F12[:, :, :].rearrange("p c t -> p (c t)"), ALU.add))
            dve.wait_ge(s_gexp, 1)
            fstep(dve.tensor_scalar(gd[:, :], gx[:, :], 1.0, None, ALU.add))
            fstep(dve.reciprocal(gr[:, :], gd[:, :]))
            fstep(dve.tensor_tensor(gx[:, :], gx[:, :], gr[:, :], ALU.mult))
            fstep(dve.tensor_tensor(F12[:, 0, :], gr[:, :], GE[:, 0, :], ALU.mult))
            fstep(dve.tensor_tensor(F12[:, 1, :], gx[:, :], GE[:, 1, :], ALU.mult))

            def expert_tile(n, par, transposed=True):
                dve.wait_ge(s_hh, n + 1)
                dve.scalar_tensor_tensor(out=HH[:, par, 1, :], in0=HB[par][:, :], scalar=0.0, in1=HH[:, par, 0, :],
                                         op0=ALU.max, op1=ALU.subtract).then_inc(s_hl, 1)
                if transposed:
                    dve.wait_ge(s_fp, n + 2)
                    dve.tensor_copy(XFT[:, 1 - par, 1].rearrange("p k n -> p (k n)"), FT[1]).then_inc(s_fl, 1)

            def result(n, par, again=True):
                if again:
                    dve.wait_ge(s_ys[par], 8 * (n - par))
                dve.wait_ge(s_yp, 2 * n + 2)
                dve.tensor_scalar(YF[:, par, 1, :], YB[par][1][:, :], TO_Y, None, ALU.mult).then_inc(s_y1, 1)

            dve.wait_ge(s_fp, 1)
            dve.tensor_copy(XFT[:, 0, 1].rearrange("p k n -> p (k n)"), FT[1]).then_inc(s_fl, 1)
            expert_tile(0, 0)
            expert_tile(1, 1)
            result(0, 0, again=False)
            expert_tile(2, 0)
            result(1, 1, again=False)
            with dve.Fori(1, NT // 2 - 1) as i:
                expert_tile(2 * i + 1, 1)
                result(2 * i, 0)
                expert_tile(2 * i + 2, 0)
                result(2 * i + 1, 1)
            expert_tile(NT - 1, 1, transposed=False)
            result(NT - 2, 0)
            result(NT - 1, 1)

            assert fsteps[0] == N_FAC

            def combine(i, par):
                b = 2 * i + par
                dve.wait_ge(s_xo[par], 16 * (i + 1))
                dve.wait_ge(s_ga[par], 2 * JT * 16 * (i + 1))
                for j in range(JT):
                    dve.scalar_tensor_tensor(out=Xt(par, j), in0=Y1[par][:, j * D:(j + 1) * D],
                                             scalar=F12[:, 0, bass.ds(JT * b + j, 1)], in1=Xt(par, j),
                                             op0=ALU.mult, op1=ALU.add).then_inc(s_c1, 1)
                for j in range(JT):
                    dve.wait_ge(s_c1, JT * b + j + 1)
                    dve.scalar_tensor_tensor(out=Xt(par, j), in0=Y2[par][:, j * D:(j + 1) * D],
                                             scalar=F12[:, 1, bass.ds(JT * b + j, 1)], in1=Xt(par, j),
                                             op0=ALU.mult, op1=ALU.add).then_inc(s_c2, 1)

            with dve.Fori(0, B // 2) as i:
                combine(i, 0)
                combine(i, 1)

        @block.tensor
        def _(pe):
            def product(bank, left, right, terms, arrive=None):
                last = None
                for k in range(terms):
                    if arrive is not None:
                        arrive(k)
                    for n, (a, c) in enumerate(((0, 0), (0, 1), (1, 0))):
                        last = pe.matmul(bank, left(a, k), right(c, k), start=(k == 0 and n == 0),
                                         stop=(k == terms - 1 and n == 2))
                return last

            pe.wait_ge(s_const, 13)
            for t in range(8):
                if t == 0:
                    pe.wait_ge(s_wq, 16)
                if t == 4:
                    pe.wait_ge(s_wk, 16)
                if t >= 6:
                    pe.wait_ge(s_wta, 1)
                    pe.wait_ge(s_wtd, 1)
                raw = WQR if t < 4 else WKR
                for k in range(KT):
                    o = k * D + (t % 4) * P
                    mm = pe.transpose(BANKS[t % 6][:, k * P:(k + 1) * P], raw[:, o:o + P], ident[:, :])
                mm.then_inc(s_wtp, 1)
            pe.wait_ge(s_wta, 4)
            pe.wait_ge(s_wtd, 4)
            for m in range(KT):
                for k in range(KT):
                    mm = pe.matmul(ACC[m][:, :], WQT[:, k * D + m * P:k * D + (m + 1) * P],
                                   WKT[:, k * D:(k + 1) * D], start=(k == 0), stop=(k == KT - 1))
                mm.then_inc(s_m, 1)

            def xt(b, tiles=range(JT)):
                for j in tiles:
                    pe.wait_ge(s_xn, 4 * b + j + 1)
                    if not isinstance(b, int) or b > 0 or j >= 2:
                        pe.wait_ge(s_xtl, 4 * b + j - 1)
                    if j == 0 and not (isinstance(b, int) and b == 0):
                        pe.wait_ge(s_mkt, 2 * b)
                    if j < 2 and not (isinstance(b, int) and b < 2):
                        pe.wait_ge(s_x2t, 4 * (b - 1))
                    for k in range(KT):
                        mm = pe.transpose(TX[j % 2][:, k * P:(k + 1) * P], XN[:, j, k * P:(k + 1) * P], ident[:, :])
                    mm.then_inc(s_xtp, 1)

            def mask_t(b, halves=range(2)):
                pe.wait_ge(s_mk, b + 1)
                cols = MK[:, :].rearrange("p (n m j) -> p n j m", n=JT, j=JT)
                for h in halves:
                    if h == 1:
                        pe.wait_ge(s_xtl, 4 * (b + 1))
                    for j in range(2):
                        for n in range(JT):
                            o = j * N + n * P
                            mm = pe.transpose(MASKB[h][:, o:o + P], cols[:, n, 2 * h + j, :], ident16[:, :])
                    mm.then_inc(s_mtp, 1)

            def x2_t(r, par, j, b=None):
                pe.wait_ge(s_x2h, 4 * r + j + 1)
                pe.wait_ge(s_x2l, 4 * r + j + 1)
                if j >= 2:
                    pe.wait_ge(s_x2t, 4 * r + j - 1)
                elif b is not None:
                    pe.wait_ge(s_xtl, 4 * b + 3 + j)
                    if j == 0:
                        pe.wait_ge(s_mkt, 2 * (b + 1))
                else:
                    pe.wait_ge(s_mkt, 2 * B)
                view = TX[j % 2][:, :].bitcast(F16)
                for k in range(2 * KT):
                    mm = pe.transpose(view[:, k * P:(k + 1) * P], X2S[:, par, j, k * P:(k + 1) * P], ident16[:, :])
                mm.then_inc(s_x2p, 1)

            def logits(r, j):
                pe.wait_ge(s_x2t, 4 * r + j + 1)
                if j == 0 and (not isinstance(r, int) or r > 0):
                    pe.wait_ge(s_lgc, r)
                    pe.wait_ge(s_row, 2 * r)
                product(RB[:, j * E:(j + 1) * E], lambda a, k: X2T[:, j % 2, a * KT + k, :],
                        lambda c, k: WG[:, c, k, :], KT).then_inc(s_lg, 1)

            def positions(r):
                pe.wait_ge(s_ohs, r + 1)
                out0 = 64
                pe.matmul(RB[:, out0:out0 + JT * E], before[:, :], OHS[:, :, :].rearrange("p j e -> p (j e)"),
                          start=True, stop=False, skip_group_check=True)
                for j in range(JT):
                    for later in range(j + 1, JT + 1):
                        mm = pe.matmul(RB[:, out0 + later * E:out0 + (later + 1) * E], ones16[:, :], OHS[:, j, :],
                                       start=False, stop=(j == JT - 1), skip_group_check=True)
                mm.then_inc(s_pos, 1)

            xt(0)
            mask_t(0)
            pe.wait_ge(s_wlo, 2 * KT + 1)

            def graph(i, par, last=False):
                b = 2 * i + par
                front = not (last and par == 1)
                XA = (XTH[:, par], XTL[:, par])

                pe.wait_ge(s_xtl, 4 * (b + 1))
                for j in range(JT):
                    if isinstance(b, int) and b == 0:
                        pass
                    else:
                        pe.wait_ge(s_res, 4 * b - 3 + j)
                    product(ACC[j][:, :], lambda a, k: WM[:, a, k, j * P:(j + 1) * P],
                            lambda c, k: XA[c][:, k, :], KT).then_inc(s_tp, 1)
                for j in range(JT):
                    product(ACC[j][:, :], lambda a, k: XA[a][:, k, j * P:(j + 1) * P],
                            lambda c, k: TT[:, c, k, :], KT,
                            lambda k: pe.wait_ge(s_tl, 4 * b + k + 1) if j == 0 else None).then_inc(s_sp, 1)
                routed = not isinstance(b, int) or b > 0
                for j in range(JT):
                    if routed and j < 2:
                        x2_t(b - 1, 1 - par, 2 * j, b)
                        x2_t(b - 1, 1 - par, 2 * j + 1, b)
                    pe.wait_ge(s_rl, 4 * b + j + 1)
                    product(ACC[j][:, :], lambda a, k: XA[a][:, k, j * P:(j + 1) * P],
                            lambda c, k: WV[:, c, k, :], KT).then_inc(s_vp, 1)
                    if routed and j < 2:
                        logits(b - 1, 2 * j)
                        logits(b - 1, 2 * j + 1)
                    if front and j == 2:
                        xt(b + 1, [0, 1])
                if front:
                    mask_t(b + 1, [0])
                    xt(b + 1, [2, 3])
                pe.wait_ge(s_pl, 4 * (b + 1))
                for j in range(JT):
                    product(ACC[j][:, :], lambda a, k: PR[:, a, k, j * P:(j + 1) * P],
                            lambda c, k: VV[:, c, k, :], JT,
                            lambda k: pe.wait_ge(s_vl, 4 * b + k + 1) if j == 0 else None).then_inc(s_op, 1)
                    if front and j == 0:
                        mask_t(b + 1, [1])
                    if j == 2 and routed:
                        positions(b - 1)

            graph(0, 0)
            graph(0, 1)
            graph(1, 0)
            graph(1, 1)
            with pe.Fori(2, B // 2 - 1) as i:
                graph(i, 0)
                graph(i, 1)
            graph(B // 2 - 1, 0, last=True)
            graph(B // 2 - 1, 1, last=True)
            for j in range(JT):
                x2_t(B - 1, 1, j)
                logits(B - 1, j)
            positions(B - 1)

            pe.wait_ge(s_x2t, 4 * B)
            pe.wait_ge(s_el, B)
            pe.wait_ge(s_row, 2 * B)
            pe.wait_ge(s_tab, N_TAB)

            def rows_t(n, par, turn):
                pe.wait_ge(s_xf[par], turn)
                if not isinstance(n, int) or n > 0:
                    pe.wait_ge(s_fh, n)
                    pe.wait_ge(s_fl, n)
                for a in range(2):
                    for k in range(KT):
                        for s in range(SUB):
                            o = k * ROWS + s * P
                            mm = pe.transpose(FT[a][:, o:o + P], XF[:, par, s, a * D + k * P:a * D + (k + 1) * P],
                                              ident16[:, :])
                mm.then_inc(s_fp, 1)

            def hidden(n, par, e):
                pe.wait_ge(s_fh, n + 1)
                pe.wait_ge(s_fl, n + 1)
                if not isinstance(n, int) or n > 1:
                    pe.wait_ge(s_hl, n - 1)
                settle(pe)
                W = (W1H, W1L)
                w = e * (KT * C)
                for m in range(CT):
                    mm = product(HB[par][:, m * ROWS:(m + 1) * ROWS],
                                 lambda a, k: W[a][:, :, :].rearrange("p e n -> p (e n)")[
                                     :, bass.ds(w + (k * C + m * P), P)],
                                 lambda c, k: XFT[:, par, c, k, :], KT)
                mm.then_inc(s_hp, 1)

            def expert_out(n, par, e):
                pe.wait_ge(s_hh, n + 1)
                pe.wait_ge(s_hl, n + 1)
                W = (W2H, W2L)
                w = e * (CT * D)
                for s in range(SUB):
                    if not isinstance(n, int) or n > 1:
                        pe.wait_ge((s_y0, s_y1)[s], n - 1)
                    product(YB[par][s][:, :],
                            lambda a, m: HH[:, par, a, m * ROWS + s * P:m * ROWS + (s + 1) * P],
                            lambda c, m: W[c][:, :, :].rearrange("p e n -> p (e n)")[:, bass.ds(w + m * D, D)],
                            CT).then_inc(s_yp, 1)

            def expert(n):
                return pe.value_load(TAB[0:1, 0, bass.ds(n, 1)], min_val=0, max_val=E - 1)

            e0 = expert(0)
            rows_t(0, 0, 16)
            hidden(0, 0, e0)
            rows_t(1, 1, 16)
            e1 = expert(1)
            hidden(1, 1, e1)
            rows_t(2, 0, 32)
            expert_out(0, 0, e0)
            def pair(i, last=False):
                a, c, d = expert(2 * i - 1), expert(2 * i), expert(2 * i + 1)
                hidden(2 * i, 0, c)
                rows_t(2 * i + 1, 1, 16 * (i + 1))
                expert_out(2 * i - 1, 1, a)
                hidden(2 * i + 1, 1, d)
                if not last:
                    rows_t(2 * i + 2, 0, 16 * (i + 2))
                expert_out(2 * i, 0, c)
                return d

            with pe.Fori(1, NT // 2 - 1) as i:
                pair(i)
            d = pair(NT // 2 - 1, last=True)
            expert_out(NT - 1, 1, d)


_INS = ['x', 'adj', 'L0_gnn_weight', 'L0_gnn_wq', 'L0_gnn_wk', 'L0_ffn_Wg', 'L0_ffn_W1', 'L0_ffn_W2']
_OUTS = [((16, 512, 512), 'float32')]


def kernel(**inputs):
    import numpy as _np
    import concourse.bacc as _bacc
    from concourse import mybir as _mybir
    from concourse.bass_utils import run_bass_kernel_spmd as _run

    nc = _bacc.Bacc("TRN2", target_bir_lowering=False, num_devices=1)
    arrays, args = {}, []
    for name in _INS:
        a = _np.ascontiguousarray(inputs[name])
        arrays[f"in_{name}_dram"] = a
        args.append(nc.dram_tensor(f"in_{name}_dram", a.shape, _mybir.dt.from_np(a.dtype), kind="ExternalInput").ap())
    for i, (shape, dtype) in enumerate(_OUTS):
        dt = _mybir.dt.from_np(_np.dtype(dtype))
        args.append(nc.dram_tensor(f"out_{i}_dram", shape, dt, kind="ExternalOutput").ap())
    build_program(nc, *args)
    r = _run(nc, [arrays], core_ids=[0])
    got = tuple(r.results[0][f"out_{i}_dram"] for i in range(len(_OUTS)))
    return got[0]
```

```python
from contextlib import ExitStack

import concourse.bass as bass
from concourse import mybir

F32 = mybir.dt.float32
F16 = mybir.dt.float16
I32 = mybir.dt.int32
U32 = mybir.dt.uint32
ALU = mybir.AluOpType
ACT = mybir.ActivationFunctionType
AX = mybir.AxisListType.X
RMAX = bass.bass_isa.ReduceOp.max

P = 128
EPS = 1e-5
SX = 2.0 ** 8
SW = 2.0 ** 8
TO32 = 2.0 ** -11
TO_Y = 1.0 / (32.0 * SW)
SPROB = 2.0 ** 14
SX2 = 2.0 ** 3
SW1 = 2.0 ** 2


def build_program(nc, x, adj, weight, wq, wk, Wg, W1, W2, out):
    B, N, D = x.shape
    E, _, C = W1.shape
    JT = N // P
    KT = D // P
    CT = C // P
    T = B * N
    TILES = B * JT
    ROWS = 256
    SUB = ROWS // P
    REGION = T + ROWS
    NF = 2 * T // ROWS
    NT = NF + E
    RING = 4
    META = 16
    WIDE = D + META
    assert JT == 4 and KT == 4 and CT == 2 and E == 8 and B % 2 == 0 and NF % RING == 0 and E % RING == 0

    sorted_x = nc.dram_tensor("sorted_x", [E * REGION + P, WIDE], F32).ap()

    x_v = x.rearrange("b (p j) d -> b p (j d)", j=JT)
    adj_v = adj.rearrange("b (p j) m -> b p (j m)", j=JT)
    out_v = out.rearrange("b (p j) d -> b p (j d)", j=JT)
    out_rows = out.rearrange("b n d -> (b n) d")
    w1_v = W1.rearrange("e (k p) c -> e p k c", p=P)
    w2_v = W2.rearrange("e (k p) d -> e p k d", p=P)

    with ExitStack() as ctx:
        def sb(name, shape, dt):
            return ctx.enter_context(nc.sbuf_tensor(name, shape, dt))

        def pb(name, shape, dt):
            return ctx.enter_context(nc.psum_tensor(name, shape, dt))

        def sem(name):
            return ctx.enter_context(nc.semaphore(name))

        ident = sb("ident", [P, P], F32)
        ident16 = sb("ident16", [P, P], F16)
        before = sb("before", [P, P], F16)
        ones16 = sb("ones16", [P, P], F16)
        minus_half = sb("minus_half", [P, JT], F32)
        expert_iota = sb("expert_iota", [P, E], F32)
        WM = sb("WM", [P, 2, KT, D], F16)
        WV = sb("WV", [P, 2, KT, D], F16)
        WG = sb("WG", [P, 2, KT, E], F16)
        W1H = sb("W1H", [P, E, KT * C], F16)
        W1L = sb("W1L", [P, E, KT * C], F16)
        W2H = sb("W2H", [P, E, CT * D], F16)
        W2L = sb("W2L", [P, E, CT * D], F16)
        wraw = sb("wraw", [P, KT * C], F32)
        wg_raw = sb("wg_raw", [P, KT * E], F32)
        XBUF = sb("XBUF", [P, RING * SUB * WIDE], F32)
        ADJ = sb("ADJ", [P, JT * N], I32)
        MK = sb("MK", [P, JT * N], F16)
        MKT = sb("MKT", [P, JT, N], F16)
        XN = sb("XN", [P, JT, D], F32)
        XTH = sb("XTH", [P, 2, KT, N], F16)
        XTL = sb("XTL", [P, 2, KT, N], F16)
        TT = sb("TT", [P, 2, KT, N], F16)
        VV = sb("VV", [P, 2, JT, D], F16)
        PR = sb("PR", [P, 2, JT, N], F16)
        RL = sb("RL", [P, 2, N], F32)
        EX = sb("EX", [P, 2, N], F32)
        X2S = sb("X2S", [P, 2, JT, WIDE], F32)
        X2T = sb("X2T", [P, 2, 2 * KT, P], F16)
        LG = sb("LG", [P, JT, E], F32)
        top = sb("top", [P, JT, E], F32)
        tix = sb("tix", [P, JT, E], U32)
        tixf = sb("tixf", [P, 2, JT], F32)
        OH = sb("OH", [P, 2, JT, E], F32)
        OHS = sb("OHS", [P, JT, E], F16)
        row_of = sb("row_of", [P, JT, E], F32)
        picked = sb("picked", [P, 2, JT, E], F32)
        slot = sb("slot", [P, 2, 2, JT], I32)
        DL = sb("DL", [P, JT], F32)
        gx = sb("gx", [P, JT], F32)
        gd = sb("gd", [P, JT], F32)
        gates = sb("gates", [P, 2, JT], F32)
        gated = sb("gated", [P, 2, JT, E], F32)
        slotf = sb("slotf", [P, 2, JT], F32)
        R = sb("R", [P, E], F32)
        base = sb("base", [P, E], F32)
        earlier = sb("earlier", [P, E, E], F32)
        cnt = sb("cnt", [P, E], F32)
        few = sb("few", [P, E], F32)
        oh0 = sb("oh0", [P, 2, E], F32)
        cex0 = sb("cex0", [P, 2, E], F32)
        dump = sb("dump", [P, 1], F32)
        pos0 = sb("pos0", [P, 2, E], F32)
        dpos = sb("dpos", [P, 2, E], F32)
        bad = sb("bad", [P, 2, E], F32)
        total1 = sb("total1", [P, 1], F32)
        cnti = sb("cnti", [P, E], I32)
        ntile = sb("ntile", [P, E], F32)
        tend = sb("tend", [P, E], F32)
        tstart = sb("tstart", [P, E], F32)
        tile_iota = sb("tile_iota", [P, NF], F32)
        TAB = sb("TAB", [P, 2, NT], I32)
        padrow = sb("padrow", [P, 2, E], I32)
        iota_p = sb("iota_p", [P, 2, E], F32)
        pad_rows = sb("pad_rows", [P, 2, WIDE], F32)
        token = sb("token", [P, RING, SUB], I32)
        gsel = sb("gsel", [P, RING, SUB, E], F32)
        to_y = sb("to_y", [P, E], F32)
        fr = sb("fr", [P, RING, SUB], F32)
        k_gate = sb("k_gate", [P, 1], F32)
        bs = sb("bs", [P, 2, JT, 6], F32)
        mv = sb("mv", [P, 2, JT, 2], F32)
        ve = sb("ve", [P, 2, JT], F32)
        rs = sb("rs", [P, 2, JT], F32)
        rr = sb("rr", [P, 2, JT], F32)
        nm = sb("nm", [P, 2, JT], F32)
        nb = sb("nb", [P, 2, JT], F32)
        smax = sb("smax", [P, JT], F32)
        sbias = sb("sbias", [P, JT], F32)
        ssum = sb("ssum", [P, JT], F32)
        srec = sb("srec", [P, JT], F32)
        srs = sb("srs", [P, JT], F32)
        mxp = sb("mxp", [P, KT], F32)
        mx = sb("mx", [P, 3], F32)
        mxa = sb("mxa", [P, 3], F32)
        ebits = sb("ebits", [P, 3], I32)
        ibits = sb("ibits", [P, 3], I32)
        wsc = sb("wsc", [P, 3], F32)
        k_pos = sb("k_pos", [P, 1], F32)
        k_neg = sb("k_neg", [P, 1], F32)
        g_res = sb("g_res", [P, 1], F32)
        emx = sb("emx", [P, 1], F32)
        emxa = sb("emxa", [P, 1], F32)
        eebits = sb("eebits", [P, 2 * E], I32)
        eibits = sb("eibits", [P, 1], I32)
        esc = sb("esc", [P, 1], F32)

        ACC = [pb(f"ACC{j}", [P, 512], F32) for j in range(4)]
        TX = [pb(f"TX{j}", [P, 512], F32) for j in range(2)]
        MT = pb("MT", [P, 512], F32)
        RB = pb("RB", [P, 512], F32)

        s_const = sem("s_const")
        s_passed = sem("s_passed")
        s_wq = sem("s_wq")
        s_wk = sem("s_wk")
        s_wv = sem("s_wv")
        s_wg = sem("s_wg")
        s_wtp = sem("s_wtp")
        s_wta = sem("s_wta")
        s_wtd = sem("s_wtd")
        s_m = sem("s_m")
        s_pmx = sem("s_pmx")
        s_mxa = sem("s_mxa")
        s_sc = sem("s_sc")
        s_whi = sem("s_whi")
        s_wlo = sem("s_wlo")
        s_x = [sem(f"s_x{i}") for i in range(2)]
        s_adj = sem("s_adj")
        s_wr = sem("s_wr")
        s_bn = sem("s_bn")
        s_mv = sem("s_mv")
        s_lna = sem("s_ln")
        s_nba = sem("s_nb")
        s_xn = sem("s_xn")
        s_xtp = sem("s_xtp")
        s_xth = sem("s_xth")
        s_xtl = sem("s_xtl")
        s_mk = sem("s_mk")
        s_mtp = sem("s_mtp")
        s_mkt = sem("s_mkt")
        s_tp = sem("s_tp")
        s_th = sem("s_th")
        s_tl = sem("s_tl")
        s_sp = sem("s_sp")
        s_rl = sem("s_rl")
        s_z = sem("s_z")
        s_sb = sem("s_sb")
        s_ex = sem("s_ex")
        s_rec = sem("s_rec")
        s_srs = sem("s_srs")
        s_ph = sem("s_ph")
        s_pl = sem("s_pl")
        s_vp = sem("s_vp")
        s_vh = sem("s_vh")
        s_vl = sem("s_vl")
        s_op = sem("s_op")
        s_res = sem("s_res")
        s_x1 = sem("s_x1_stored")
        s_bn2 = sem("s_bn2")
        s_mv2 = sem("s_mv2")
        s_ln2 = sem("s_ln2")
        s_nb2 = sem("s_nb2")
        s_x2h = sem("s_x2h")
        s_x2p = sem("s_x2p")
        s_x2t = sem("s_x2t")
        s_x2l = sem("s_x2l")
        s_lg = sem("s_lg")
        s_lgc = sem("s_lgc")
        s_top = sem("s_top")
        s_tix = sem("s_tix")
        s_txf = sem("s_txf")
        s_oh = sem("s_oh")
        s_ohs = sem("s_ohs")
        s_dl = sem("s_dl")
        s_pos = sem("s_pos")
        s_row = sem("s_row")
        s_pick = sem("s_pick")
        s_slot = sem("s_slot")
        s_sc2 = [sem(f"s_scat{i}") for i in range(2)]
        s_tab = sem("s_tab")
        s_pad = sem("s_pad")
        s_pad_at = sem("s_pad_at")
        s_xf = [sem(f"s_xf{i}") for i in range(RING)]
        s_fp = sem("s_fp")
        s_fh = sem("s_fh")
        s_fl = sem("s_fl")
        s_wx = sem("s_wx")
        s_fr = sem("s_fr")
        s_hp = sem("s_hp")
        s_hh = sem("s_hh")
        s_hl = sem("s_hl")
        s_yp = sem("s_yp")
        s_y0 = sem("s_y0")
        s_y1 = sem("s_y1")
        s_add = [sem(f"s_add{i}") for i in range(2)]
        s_gexp = sem("s_gexp")
        s_gate = sem("s_gate")
        s_g0 = sem("s_g0")
        s_ea = sem("s_ea")
        s_eg = sem("s_eg")
        s_es = sem("s_es")
        s_eh = sem("s_eh")
        s_el = sem("s_el")

        WQR = PR[:, :, :, :].rearrange("p a j n -> p (a j n)").bitcast(F32)
        WKR = TT[:, :, :, :].rearrange("p a j n -> p (a j n)").bitcast(F32)
        WVR = VV[:, :, :, :].rearrange("p a j n -> p (a j n)").bitcast(F32)
        WQT = W2H[:, E - 4:E, :].rearrange("p e n -> p (e n)").bitcast(F32)
        WKT = W2L[:, E - 4:E, :].rearrange("p e n -> p (e n)").bitcast(F32)
        BANKS = ACC + TX
        X = XBUF[:, 0:2 * JT * D].rearrange("p (b n) -> p b n", b=2)
        XF = XBUF[:, :].rearrange("p (q s n) -> p q s n", q=RING, s=SUB)
        XFT = XN[:, :, :].rearrange("p j d -> p (j d)").bitcast(F16).rearrange(
            "p (b a k n) -> p b a k n", b=2, a=2, k=KT)
        HH = RL[:, :, :].rearrange("p a n -> p (a n)").bitcast(F16).rearrange("p (b a n) -> p b a n", b=2, a=2)
        YF = XTH[:, :, :, :].rearrange("p a j n -> p (a j n)").bitcast(F32).rearrange(
            "p (b s d) -> p b s d", b=2, s=SUB)
        HB = [ACC[0], ACC[1]]
        YB = [[ACC[2], ACC[3]], [MT, RB]]
        WX = WV[:, :, :, :].rearrange("p a k n -> p (a k n)").bitcast(F32)[:, 0:NT * E].rearrange(
            "p (t e) -> p t e", e=E)
        scratch = WM[:, :, :, :].rearrange("p a k n -> p (a k n)").bitcast(F32)
        past, pastn = [scratch[:, a * NF * E:(a + 1) * NF * E].rearrange("p (t e) -> p t e", e=E) for a in range(2)]
        tin, tex, tst, trow, valid = [scratch[:, (2 * E + a) * NF:(2 * E + a + 1) * NF] for a in range(5)]
        tmpee = scratch[:, (2 * E + 6) * NF:(2 * E + 6) * NF + E * E].rearrange("p (a b) -> p a b", b=E)
        MASKB = [MT[:, :].bitcast(F16), TX[0][:, :].bitcast(F16)]

        N_TAB = 20
        N_PAD = 9
        N_WX = 8

        block = ctx.enter_context(nc.Block())

        def settle(engine):
            engine.sem_inc(s_passed, 1)

        def tokens(par):
            return X2S[:, par, :, :].bitcast(I32)[:, :, D:D + 1]

        def Xt(par, j):
            return X[:, par, j * D:(j + 1) * D]

        @block.sync
        def _(sp):
            def load_x(b, par, first=False):
                if not first:
                    sp.wait_ge(s_x2h, 4 * (b - 1))
                    settle(sp)
                    sp.wait_ge(s_x1, 16 * (b - 1))
                    settle(sp)
                sp.dma_start(X[:, par, :], x_v[b]).then_inc(s_x[par], 16)

            def load_weights(i, par, b):
                sp.wait_ge(s_el, b)
                settle(sp)
                if par == 0:
                    sp.dma_start(wraw[:, :].rearrange("p (k c) -> p k c", k=KT), w1_v[i]).then_inc(s_wr, 16)
                else:
                    sp.dma_start(wraw[:, :].rearrange("p (k c) -> p k c", k=CT), w2_v[i]).then_inc(s_wr, 16)

            def load_adj(b, first=False):
                if not first:
                    sp.wait_ge(s_mk, b)
                    settle(sp)
                sp.dma_start(ADJ[:, :], adj_v[b]).then_inc(s_adj, 16)

            load_x(0, 0, first=True)
            sp.dma_start(WQR.rearrange("p (k o) -> p k o", k=KT),
                         wq.rearrange("(k p) o -> p k o", p=P)).then_inc(s_wq, 16)
            sp.dma_start(WKR.rearrange("p (k o) -> p k o", k=KT),
                         wk.rearrange("(k p) o -> p k o", p=P)).then_inc(s_wk, 16)
            sp.dma_start(WVR.rearrange("p (k o) -> p k o", k=KT),
                         weight.rearrange("(k p) o -> p k o", p=P)).then_inc(s_wv, 16)
            sp.dma_start(wg_raw[:, :].rearrange("p (k e) -> p k e", k=KT),
                         Wg.rearrange("(k p) e -> p k e", p=P)).then_inc(s_wg, 16)
            load_adj(0, first=True)
            load_x(1, 1, first=True)
            sp.dma_start(wraw[:, :].rearrange("p (k c) -> p k c", k=KT), w1_v[0]).then_inc(s_wr, 16)
            load_adj(1)

            def graph(i, par, last=False):
                b = 2 * i + par
                if not last:
                    load_adj(b + 2)
                if not (last and par == 1):
                    if not (isinstance(b, int) and b == 0):
                        load_x(b + 1, 1 - par)
                    load_weights(i + par, 1 - par, b + 1)
                sp.wait_ge(s_res, 4 * (b + 1))
                settle(sp)
                sp.dma_start(out_v[b], X[:, par, :]).then_inc(s_x1, 16)

            graph(0, 0)
            graph(0, 1)
            graph(1, 0)
            graph(1, 1)
            with sp.Fori(2, B // 2 - 1) as i:
                graph(i, 0)
                graph(i, 1)
            graph(B // 2 - 1, 0, last=True)
            graph(B // 2 - 1, 1, last=True)
            def load_rows(n, q, free=True):
                row = sp.value_load(TAB[0:1, 1, bass.ds(n, 1)], min_val=0, max_val=E * REGION - ROWS)
                if free:
                    sp.wait_ge(s_fp, SUB * (n - RING + 1))
                    settle(sp)
                    sp.wait_ge(s_fr, 3 * (n - RING + 1))
                    settle(sp)
                src = sorted_x[bass.ds(row, ROWS), :].rearrange("(s p) n -> p s n", s=SUB)
                sp.dma_start(XF[:, q], src).then_inc(s_xf[q], 16)

            for par in range(2):
                sp.wait_ge(s_sc2[par], 2 * JT * 16 * (B // 2))
            sp.wait_ge(s_tab, N_TAB)
            for q in range(RING):
                load_rows(q, q, free=False)
            with sp.Fori(1, NF // RING) as i:
                for q in range(RING):
                    load_rows(RING * i + q, q)
            sp.wait_ge(s_pad, 2 * E * 16)
            with sp.Fori(NF // RING, NT // RING) as i:
                for q in range(RING):
                    load_rows(RING * i + q, q)

        @block.gpsimd
        def _(pool):
            pool.memset(ident[:, :], 0.0).then_inc(s_const, 1)
            pool.memset(ones16[:, :], 1.0).then_inc(s_const, 1)
            pool.memset(X2S[:, :, :, D:WIDE], 0.0).then_inc(s_const, 1)
            pool.memset(pad_rows[:, :, :], 0.0).then_inc(s_const, 1)
            pool.memset(minus_half[:, :], -0.5).then_inc(s_const, 1)
            pool.iota(expert_iota[:, :], pattern=[[1, E]], base=0, channel_multiplier=0,
                      allow_small_or_imprecise_dtypes=True).then_inc(s_const, 1)
            pool.iota(R[:, :], pattern=[[REGION, E]], base=0, channel_multiplier=0,
                      allow_small_or_imprecise_dtypes=True).then_inc(s_const, 1)
            pool.iota(base[:, :], pattern=[[REGION, E]], base=0, channel_multiplier=0,
                      allow_small_or_imprecise_dtypes=True).then_inc(s_const, 1)
            pool.iota(tile_iota[:, :], pattern=[[1, NF]], base=0, channel_multiplier=0,
                      allow_small_or_imprecise_dtypes=True).then_inc(s_const, 1)
            pool.iota(iota_p[:, :, :], pattern=[[P, 2], [0, E]], base=0, channel_multiplier=1,
                      allow_small_or_imprecise_dtypes=True).then_inc(s_const, 1)
            pool.memset(earlier[:, :, :], 1.0).then_inc(s_const, 1)
            pool.wait_ge(s_const, 11)
            for par in range(2):
                pool.iota(tokens(par), pattern=[[1, JT], [1, 1]], base=par * N,
                          channel_multiplier=JT).then_inc(s_const, 1)
            pool.iota(pad_rows[:, :, :].bitcast(I32)[:, :, D:D + 1], pattern=[[1, 2], [1, 1]], base=0,
                      channel_multiplier=JT).then_inc(s_const, 1)
            pool.affine_select(out=earlier[:, :, :], in_=earlier[:, :, :], compare_op=ALU.is_gt, fill=0.0, base=0,
                               pattern=[[1, E], [-1, E]], channel_multiplier=0).then_inc(s_const, 1)
            pool.affine_select(out=ident[:, :], in_=ident[:, :], compare_op=ALU.not_equal, fill=1.0, base=0,
                               pattern=[[-1, P]], channel_multiplier=1).then_inc(s_const, 1)
            pool.affine_select(out=before[:, :], in_=ones16[:, :], compare_op=ALU.is_gt, fill=0.0, base=0,
                               pattern=[[1, P]], channel_multiplier=-1).then_inc(s_const, 1)
            pool.wait_ge(s_const, 17)
            pool.tensor_copy(ident16[:, :], ident[:, :]).then_inc(s_const, 1)

            def layernorm_scale(b, q):
                s_m_v, s_ln, s_nb, scale = ((s_mv, s_lna, s_nba, SX), (s_mv2, s_ln2, s_nb2, SX2))[q]
                n_ln = 3 * b
                pool.wait_ge(s_m_v, 4 * (b + 1))
                settle(pool)
                pool.tensor_scalar(ve[:, q, :], mv[:, q, :, 1], 1.0, EPS, ALU.mult, ALU.add).then_inc(s_ln, 1)
                pool.tensor_scalar(nm[:, q, :], mv[:, q, :, 0], -scale, 0.0, ALU.mult, ALU.add).then_inc(s_ln, 1)
                pool.wait_ge(s_ln, n_ln + 2)
                pool.tensor_tensor(rs[:, q, :], ve[:, q, :], minus_half[:, :], ALU.pow).then_inc(s_ln, 1)
                pool.wait_ge(s_ln, n_ln + 3)
                settle(pool)
                pool.tensor_scalar(rr[:, q, :], rs[:, q, :], scale, 0.0, ALU.mult, ALU.add).then_inc(s_nb, 1)
                pool.tensor_tensor(nb[:, q, :], nm[:, q, :], rs[:, q, :], ALU.mult).then_inc(s_nb, 1)

            layernorm_scale(0, 0)
            pool.wait_ge(s_pmx, 7)
            pool.partition_all_reduce(mxa[:, :], mx[:, :], P, RMAX).then_inc(s_mxa, 1)

            def rows(r, par, turn):
                pool.wait_ge(s_nb2, 2 * (r + 1))
                if not isinstance(r, int) or r >= 2:
                    pool.wait_ge(s_sc2[par], 2 * JT * 16 * turn)
                    pool.wait_ge(s_x2p, 4 * (r - 1))
                settle(pool)
                for j in range(JT):
                    pool.tensor_scalar(X2S[:, par, j, 0:D], Xt(par, j), rr[:, 1, j:j + 1], nb[:, 1, j:j + 1],
                                       ALU.mult, ALU.add).then_inc(s_x2h, 1)

            def scatter(r, par):
                pool.wait_ge(s_slot, 2 * (r + 1))
                settle(pool)
                pool.wait_ge(s_gate, 6 * (r + 1))
                settle(pool)
                for j in range(JT):
                    for c in range(2):
                        pool.indirect_dma_start(
                            out=sorted_x, out_offset=bass.IndirectOffsetOnAxis(ap=slot[:, par, c, j:j + 1], axis=0),
                            in_=X2S[:, par, j, :], in_offset=None).then_inc(s_sc2[par], 16)

            def largest(b):
                pool.wait_ge(s_ea, b + 1)
                settle(pool)
                pool.partition_all_reduce(emxa[:, :], emx[:, :], P, RMAX).then_inc(s_eg, 1)

            largest(0)

            def graph(i, par, last=False):
                b = 2 * i + par
                r = b - 1
                static = isinstance(b, int)
                if not static or b > 0:
                    layernorm_scale(r, 1)
                    rows(r, 1 - par, i - 1 + par)
                if not (last and par == 1):
                    layernorm_scale(b + 1, 0)
                if not static or b > 0:
                    scatter(r, 1 - par)
                if not (last and par == 1):
                    largest(b + 1)

            graph(0, 0)
            graph(0, 1)
            graph(1, 0)
            graph(1, 1)
            with pool.Fori(2, B // 2 - 1) as i:
                graph(i, 0)
                graph(i, 1)
            graph(B // 2 - 1, 0, last=True)
            graph(B // 2 - 1, 1, last=True)

            layernorm_scale(B - 1, 1)
            rows(B - 1, 1, B // 2 - 1)
            scatter(B - 1, 1)

            def pad(e):
                for h in range(2):
                    pool.indirect_dma_start(
                        out=sorted_x, out_offset=bass.IndirectOffsetOnAxis(ap=padrow[:, h, e:e + 1], axis=0),
                        in_=pad_rows[:, h, :], in_offset=None).then_inc(s_pad, 16)

            def add_rows(n, q, first=False):
                pool.wait_ge(s_y0, n + 1)
                pool.wait_ge(s_y1, n + 1)
                if not first:
                    pool.wait_ge(s_add[1 - q % 2], 16 * (n - q % 2) + (0 if q % 2 == 0 else 32))
                settle(pool)
                for s in range(SUB):
                    pool.indirect_dma_start(
                        out=out_rows, out_offset=bass.IndirectOffsetOnAxis(ap=token[:, q, s:s + 1], axis=0),
                        in_=YF[:, q % 2, s, :], in_offset=None, compute_op=ALU.add).then_inc(s_add[q % 2], 16)

            pool.wait_ge(s_x1, 16 * B)
            for n in range(E):
                add_rows(n, n % RING, first=n == 0)
                if n == 0:
                    pool.wait_ge(s_pad_at, N_PAD)
                pad(n)
            with pool.Fori(E // RING, NT // RING) as i:
                for q in range(RING):
                    add_rows(RING * i + q, q)
            for par in range(2):
                pool.wait_ge(s_add[par], 32 * (NT // 2))

        @block.scalar
        def _(act):
            for t in range(0, 8, 2):
                act.wait_ge(s_wtp, t + 1)
                dst = (WQT if t < 4 else WKT)[:, (t % 4) * D:(t % 4 + 1) * D]
                act.activation(dst, BANKS[t % 6][:, :], ACT.Copy).then_inc(s_wta, 1)

            def xn_tiles(b, par, tiles=range(JT)):
                act.wait_ge(s_nba, 2 * (b + 1))
                for j in tiles:
                    if j == 0 and not isinstance(b, int):
                        act.wait_ge(s_xtp, 4 * b)
                    elif j == 0 and b > 0:
                        act.wait_ge(s_xtp, 4 * b)
                    act.activation(XN[:, j, :], Xt(par, j), ACT.Identity, scale=rr[:, 0, j:j + 1],
                                   bias=nb[:, 0, j:j + 1]).then_inc(s_xn, 1)

            def xt_high(b, par, tiles=range(JT)):
                for j in tiles:
                    act.wait_ge(s_xtp, 4 * b + j + 1)
                    act.activation(XTH[:, par, :, j * P:(j + 1) * P],
                                   TX[j % 2][:, :].rearrange("p (k n) -> p k n", k=KT), ACT.Copy).then_inc(s_xth, 1)

            def mask_t(b, halves=range(2)):
                for h in halves:
                    act.wait_ge(s_mtp, 2 * b + h + 1)
                    act.activation(MKT[:, 2 * h:2 * h + 2, :].rearrange("p j n -> p (j n)"), MASKB[h],
                                   ACT.Copy).then_inc(s_mkt, 1)

            def x2_t(r, j):
                act.wait_ge(s_x2p, 4 * r + j + 1)
                if not isinstance(r, int) or r > 0 or j >= 2:
                    act.wait_ge(s_lg, 4 * r + j - 1)
                act.activation(X2T[:, j % 2, 0:KT, :], TX[j % 2][:, :].rearrange("p (k n) -> p k n", k=KT),
                               ACT.Copy).then_inc(s_x2t, 1)

            def gate(r):
                act.wait_ge(s_dl, r + 1)
                act.activation(gx[:, :], DL[:, :], ACT.Exp, scale=k_gate[:, 0:1]).then_inc(s_gexp, 1)

            xn_tiles(0, 0)
            act.wait_ge(s_sc, 4)
            for k in range(KT):
                act.activation(WM[:, 0, k, :], ACC[k][:, :], ACT.Copy, scale=wsc[:, 0:1]).then_inc(s_whi, 1)
            for k in range(KT):
                act.activation(WV[:, 0, k, :], WVR[:, k * D:(k + 1) * D], ACT.Copy, scale=wsc[:, 1:2]).then_inc(s_whi, 1)
            act.activation(WG[:, 0, :, :].rearrange("p k e -> p (k e)"), wg_raw[:, :], ACT.Copy,
                           scale=wsc[:, 2:3]).then_inc(s_whi, 1)
            xt_high(0, 0)
            mask_t(0)

            def graph(i, par, last=False):
                b = 2 * i + par
                front = not (last and par == 1)

                def t_high(j):
                    act.wait_ge(s_tp, 4 * b + j + 1)
                    act.activation(TT[:, 0, j, :], ACC[j][:, :], ACT.Copy, scale=TO32).then_inc(s_th, 1)

                for j in range(JT):
                    t_high(j)
                act.wait_ge(s_es, 4 * (b + 1))
                settle(act)
                hi = (W1H if par == 0 else W2H)[:, bass.ds(i, 1), :].rearrange("p o n -> p (o n)")
                act.activation(hi, wraw[:, :], ACT.Copy, scale=esc[:, 0:1]).then_inc(s_eh, 1)

                def relu(j):
                    act.wait_ge(s_sp, 4 * b + j + 1)
                    act.activation(RL[:, j % 2, :], ACC[j][:, :], ACT.Relu).then_inc(s_rl, 1)

                def exp_and_high(j):
                    act.wait_ge(s_sb, 4 * b + j + 1)
                    act.activation(EX[:, j % 2, :], RL[:, j % 2, :], ACT.Exp, scale=k_pos[:, 0:1],
                                   bias=sbias[:, j:j + 1], accum_out=ssum[:, j:j + 1]).then_inc(s_ex, 1)
                    act.wait_ge(s_srs, 4 * b + j + 1)
                    act.activation(PR[:, 0, j, :], EX[:, j % 2, :], ACT.Copy, scale=srs[:, j:j + 1]).then_inc(s_ph, 1)

                routed = not isinstance(b, int) or b > 0
                relu(0)
                relu(1)
                for j in range(JT):
                    if j == JT - 1 and routed:
                        x2_t(b - 1, 0)
                        x2_t(b - 1, 1)
                    exp_and_high(j)
                    if j + 2 < JT:
                        relu(j + 2)
                for j in range(JT):
                    if j == 2 and routed:
                        x2_t(b - 1, 2)
                        x2_t(b - 1, 3)
                    if j == 3 and front:
                        xn_tiles(b + 1, 1 - par)
                    act.wait_ge(s_vp, 4 * b + j + 1)
                    act.activation(VV[:, 0, j, :], ACC[j][:, :], ACT.Copy, scale=TO32).then_inc(s_vh, 1)
                if routed:
                    gate(b - 1)
                if front:
                    xt_high(b + 1, 1 - par, [0, 1])
                    mask_t(b + 1, [0])
                    xt_high(b + 1, 1 - par, [2, 3])
                    mask_t(b + 1, [1])

            graph(0, 0)
            graph(0, 1)
            graph(1, 0)
            graph(1, 1)
            with act.Fori(2, B // 2 - 1) as i:
                graph(i, 0)
                graph(i, 1)
            graph(B // 2 - 1, 0, last=True)
            graph(B // 2 - 1, 1, last=True)

            for j in range(JT):
                x2_t(B - 1, j)

            gate(B - 1)

            def hidden(n, par):
                act.wait_ge(s_hp, n + 1)
                act.activation(HH[:, par, 0, :], HB[par][:, :], ACT.Relu).then_inc(s_hh, 1)

            def rows_high(n, par):
                for s in range(SUB):
                    act.wait_ge(s_fp, SUB * n + s + 1)
                    act.activation(XFT[:, par, 0, :, s * P:(s + 1) * P],
                                   TX[s][:, :].rearrange("p (k n) -> p k n", k=KT), ACT.Copy).then_inc(s_fh, 1)

            def result(n, q, again=True):
                if again:
                    act.wait_ge(s_add[q % 2], 16 * (n - q % 2))
                act.wait_ge(s_fr, 3 * (n + 1))
                act.wait_ge(s_yp, 2 * n + 1)
                act.activation(YF[:, q % 2, 0, :], YB[q % 2][0][:, :], ACT.Copy,
                               scale=fr[:, q, 0:1]).then_inc(s_y0, 1)

            rows_high(0, 0)
            for n in range(RING):
                rows_high(n + 1, (n + 1) % 2)
                hidden(n, n % 2)
                if n > 0:
                    result(n - 1, n - 1, again=n > 2)

            def tiles(i, last=False):
                for q in range(RING):
                    n = RING * i + q
                    if not (last and q == RING - 1):
                        rows_high(n + 1, (q + 1) % 2)
                    hidden(n, q % 2)
                    result(n - 1, (q - 1) % RING)

            with act.Fori(1, NT // RING - 1) as i:
                tiles(i)
            tiles(NT // RING - 1, last=True)
            result(NT - 1, RING - 1)

        @block.vector
        def _(dve):
            def statistics(b, par, q):
                s_b, s_m_v = ((s_bn, s_mv), (s_bn2, s_mv2))[q]
                for j in range(JT):
                    if q:
                        dve.wait_ge(s_res, 4 * b + j + 1)
                    dve.bn_stats(bs[:, q, j, :], Xt(par, j)).then_inc(s_b, 1)
                dve.wait_ge(s_b, 4 * (b + 1))
                settle(dve)
                for j in range(JT):
                    dve.bn_aggr(mv[:, q, j, :], bs[:, q, j, :]).then_inc(s_m_v, 1)

            def route(r):
                dve.wait_ge(s_lg, 4 * (r + 1))
                dve.tensor_copy(LG[:, :, :], RB[:, 0:JT * E].rearrange("p (j e) -> p j e", j=JT)).then_inc(s_lgc, 1)
                dve.wait_ge(s_lgc, r + 1)
                settle(dve)
                for j in range(JT):
                    dve.max(top[:, j, :], LG[:, j, :]).then_inc(s_top, 1)
                dve.wait_ge(s_top, 4 * (r + 1))
                settle(dve)
                for j in range(JT):
                    dve.max_index(tix[:, j, :], top[:, j, :], LG[:, j, :]).then_inc(s_tix, 1)
                dve.tensor_tensor(DL[:, :], top[:, :, 1], top[:, :, 0], ALU.subtract).then_inc(s_dl, 1)
                dve.wait_ge(s_tix, 4 * (r + 1))
                dve.tensor_copy(tixf[:, :, :], tix[:, :, 0:2].rearrange("p j c -> p c j")).then_inc(s_txf, 1)
                dve.wait_ge(s_txf, r + 1)
                for c in range(2):
                    dve.tensor_tensor(OH[:, c, :, :], tixf[:, c, :].unsqueeze(2).broadcast_to([P, JT, E]),
                                      expert_iota[:, :].unsqueeze(1).broadcast_to([P, JT, E]),
                                      ALU.is_equal).then_inc(s_oh, 1)
                dve.wait_ge(s_oh, 2 * (r + 1))
                dve.tensor_tensor(OHS[:, :, :], OH[:, 0, :, :], OH[:, 1, :, :], ALU.add).then_inc(s_ohs, 1)
                if isinstance(r, int) and r == 0:
                    dve.wait_ge(s_ohs, 1)
                    dve.tensor_copy(oh0[:, :, :], OHS[:, 0:2, :]).then_inc(s_g0, 1)

            def place(r, par, turn):
                dve.wait_ge(s_pos, r + 1)
                counts = RB[:, 64:64 + (JT + 1) * E].rearrange("p (j e) -> p j e", e=E)
                dve.tensor_tensor(row_of[:, :, :], counts[:, 0:JT, :], R[:, :].unsqueeze(1).broadcast_to([P, JT, E]),
                                  ALU.add).then_inc(s_row, 1)
                dve.wait_ge(s_row, 2 * r + 1)
                dve.tensor_tensor(R[:, :], R[:, :], counts[:, JT, :], ALU.add).then_inc(s_row, 1)
                if isinstance(r, int) and r == 0:
                    dve.tensor_tensor(cex0[:, :, :], row_of[:, 0:2, :],
                                      base[:, :].unsqueeze(1).broadcast_to([P, 2, E]), ALU.subtract).then_inc(s_g0, 1)
                for c in range(2):
                    dve.tensor_tensor(picked[:, c, :, :], OH[:, c, :, :], row_of[:, :, :], ALU.mult).then_inc(s_pick, 1)
                dve.wait_ge(s_pick, 3 * r + 2)
                dve.tensor_reduce(slotf[:, :, :], picked[:, :, :, :], AX, ALU.add).then_inc(s_pick, 1)
                dve.wait_ge(s_pick, 3 * r + 3)
                if not isinstance(r, int) or r >= 2:
                    dve.wait_ge(s_sc2[par], 2 * JT * 16 * turn)
                settle(dve)
                dve.tensor_copy(slot[:, par, :, :], slotf[:, :, :]).then_inc(s_slot, 1)
                if isinstance(r, int) and r < 2:
                    dve.sem_inc(s_slot, 1)
                else:
                    dve.tensor_scalar(tokens(par), tokens(par), float(2 * N), None, ALU.add).then_inc(s_slot, 1)
                n_g = 6 * r
                dve.wait_ge(s_gexp, r + 1)
                dve.tensor_scalar(gd[:, :], gx[:, :], 1.0, None, ALU.add).then_inc(s_gate, 1)
                dve.wait_ge(s_gate, n_g + 1)
                dve.reciprocal(gates[:, 0, :], gd[:, :]).then_inc(s_gate, 1)
                dve.wait_ge(s_gate, n_g + 2)
                dve.tensor_tensor(gates[:, 1, :], gx[:, :], gates[:, 0, :], ALU.mult).then_inc(s_gate, 1)
                dve.wait_ge(s_gate, n_g + 3)
                for c in range(2):
                    dve.tensor_tensor(gated[:, c, :, :], OH[:, c, :, :],
                                      gates[:, c, :].unsqueeze(2).broadcast_to([P, JT, E]),
                                      ALU.mult).then_inc(s_gate, 1)
                dve.wait_ge(s_gate, n_g + 5)
                dve.tensor_tensor(X2S[:, par, :, D + 1:D + 1 + E], gated[:, 0, :, :],
                                  gated[:, 1, :, :], ALU.add).then_inc(s_gate, 1)

            def mask(b):
                dve.wait_ge(s_adj, 16 * (b + 1))
                if not (isinstance(b, int) and b == 0):
                    dve.wait_ge(s_mtp, 2 * b)
                dve.tensor_scalar(MK[:, :], ADJ[:, :], 0.0, None, ALU.not_equal).then_inc(s_mk, 1)

            def xt_low(b, par, tiles=range(JT)):
                for j in tiles:
                    dve.wait_ge(s_xth, 4 * b + j + 1)
                    dve.tensor_tensor(XTL[:, par, :, j * P:(j + 1) * P],
                                      TX[j % 2][:, :].rearrange("p (k n) -> p k n", k=KT),
                                      XTH[:, par, :, j * P:(j + 1) * P], ALU.subtract).then_inc(s_xtl, 1)

            def x2_low(r, j):
                dve.wait_ge(s_x2t, 4 * r + j + 1)
                dve.tensor_tensor(X2T[:, j % 2, KT:2 * KT, :], TX[j % 2][:, :].rearrange("p (k n) -> p k n", k=KT),
                                  X2T[:, j % 2, 0:KT, :], ALU.subtract).then_inc(s_x2l, 1)

            dve.wait_ge(s_x[0], 16)
            statistics(0, 0, 0)
            for t in range(1, 8, 2):
                dve.wait_ge(s_wtp, t + 1)
                dst = (WQT if t < 4 else WKT)[:, (t % 4) * D:(t % 4 + 1) * D]
                dve.tensor_copy(dst, BANKS[t % 6][:, :]).then_inc(s_wtd, 1)
            dve.wait_ge(s_wv, 16)
            dve.tensor_reduce(mx[:, 1:2], WVR, AX, ALU.max, apply_absolute_value=True).then_inc(s_pmx, 1)
            dve.wait_ge(s_wg, 16)
            dve.tensor_reduce(mx[:, 2:3], wg_raw[:, :], AX, ALU.max, apply_absolute_value=True).then_inc(s_pmx, 1)
            mask(0)
            for k in range(KT):
                dve.wait_ge(s_m, k + 1)
                dve.tensor_reduce(mxp[:, k:k + 1], ACC[k][:, :], AX, ALU.max,
                                  apply_absolute_value=True).then_inc(s_pmx, 1)
            dve.wait_ge(s_pmx, 6)
            dve.tensor_reduce(mx[:, 0:1], mxp[:, :], AX, ALU.max).then_inc(s_pmx, 1)

            dve.wait_ge(s_mxa, 1)
            dve.tensor_scalar(mx[:, :], mxa[:, :], 2.0 ** -90, 2.0 ** 90, ALU.max, ALU.min).then_inc(s_sc, 1)
            dve.wait_ge(s_sc, 1)
            dve.tensor_scalar(ebits[:, :], mx[:, :].bitcast(I32), 0x7F800000, None, ALU.bitwise_and).then_inc(s_sc, 1)
            dve.wait_ge(s_sc, 2)
            dve.tensor_scalar(ibits[:, :], ebits[:, :], -1.0, float(254 << 23), ALU.mult, ALU.add).then_inc(s_sc, 1)
            dve.wait_ge(s_sc, 3)
            dve.tensor_scalar(wsc[:, :], ibits[:, :].bitcast(F32), SW, None, ALU.mult).then_inc(s_sc, 1)
            ef = ebits[:, :].bitcast(F32)
            dve.tensor_scalar(k_pos[:, :], ef[:, 0:1], 1.0 / (SX * 32.0), None, ALU.mult).then_inc(s_sc, 1)
            dve.tensor_scalar(k_neg[:, :], ef[:, 0:1], -1.0 / (SX * 32.0), None, ALU.mult).then_inc(s_sc, 1)
            dve.tensor_scalar(g_res[:, :], ef[:, 1:2], 1.0 / (SPROB * 32.0), None, ALU.mult).then_inc(s_sc, 1)
            dve.tensor_scalar(k_gate[:, :], ef[:, 2:3], 1.0 / (SX2 * SW), None, ALU.mult).then_inc(s_sc, 1)
            for k in range(KT):
                dve.wait_ge(s_whi, k + 1)
                if k == 0:
                    dve.wait_ge(s_sc, 8)
                dve.scalar_tensor_tensor(out=WM[:, 1, k, :], in0=ACC[k][:, :], scalar=wsc[:, 0:1],
                                         in1=WM[:, 0, k, :], op0=ALU.mult, op1=ALU.subtract).then_inc(s_wlo, 1)
            for k in range(KT):
                dve.wait_ge(s_whi, KT + k + 1)
                dve.scalar_tensor_tensor(out=WV[:, 1, k, :], in0=WVR[:, k * D:(k + 1) * D], scalar=wsc[:, 1:2],
                                         in1=WV[:, 0, k, :], op0=ALU.mult, op1=ALU.subtract).then_inc(s_wlo, 1)
            dve.wait_ge(s_whi, 2 * KT + 1)
            dve.scalar_tensor_tensor(out=WG[:, 1, :, :].rearrange("p k e -> p (k e)"), in0=wg_raw[:, :],
                                     scalar=wsc[:, 2:3], in1=WG[:, 0, :, :].rearrange("p k e -> p (k e)"),
                                     op0=ALU.mult, op1=ALU.subtract).then_inc(s_wlo, 1)
            xt_low(0, 0)

            def largest(b):
                dve.wait_ge(s_wr, 16 * (b + 1))
                dve.tensor_reduce(emx[:, :], wraw[:, :], AX, ALU.max, apply_absolute_value=True).then_inc(s_ea, 1)

            largest(0)

            def graph(i, par, last=False):
                b = 2 * i + par
                front = not (last and par == 1)
                routed = not isinstance(b, int) or b > 0

                def weight_scale():
                    dve.wait_ge(s_eg, b + 1)
                    dve.tensor_scalar(emx[:, :], emxa[:, :], 2.0 ** -60, 2.0 ** 60, ALU.max,
                                      ALU.min).then_inc(s_es, 1)
                    dve.wait_ge(s_es, 4 * b + 1)
                    eb = eebits[:, bass.ds(i + E * par, 1)]
                    dve.tensor_scalar(eb, emx[:, :].bitcast(I32), 0x7F800000, None, ALU.bitwise_and).then_inc(s_es, 1)
                    dve.wait_ge(s_es, 4 * b + 2)
                    dve.tensor_scalar(eibits[:, :], eb, -1.0, float(254 << 23), ALU.mult, ALU.add).then_inc(s_es, 1)
                    dve.wait_ge(s_es, 4 * b + 3)
                    dve.tensor_scalar(esc[:, :], eibits[:, :].bitcast(F32), SW if par else SW1, None,
                                      ALU.mult).then_inc(s_es, 1)

                for j in range(JT):
                    dve.wait_ge(s_th, 4 * b + j + 1)
                    dve.scalar_tensor_tensor(out=TT[:, 1, j, :], in0=ACC[j][:, :], scalar=TO32, in1=TT[:, 0, j, :],
                                             op0=ALU.mult, op1=ALU.subtract).then_inc(s_tl, 1)
                    if j == 1:
                        weight_scale()
                    if j == 2 and front:
                        mask(b + 1)
                dve.wait_ge(s_eh, b + 1)
                settle(dve)
                sl = bass.ds(i, 1)
                hi, lo = (W1H, W1L) if par == 0 else (W2H, W2L)
                dve.scalar_tensor_tensor(out=lo[:, sl, :].rearrange("p o n -> p (o n)"), in0=wraw[:, :],
                                         scalar=esc[:, 0:1], in1=hi[:, sl, :].rearrange("p o n -> p (o n)"),
                                         op0=ALU.mult, op1=ALU.subtract).then_inc(s_el, 1)

                def masked_max(j):
                    dve.wait_ge(s_rl, 4 * b + j + 1)
                    if j == 0:
                        dve.wait_ge(s_mkt, 2 * (b + 1))
                    settle(dve)
                    rl = RL[:, j % 2, :]
                    dve.tensor_tensor_reduce(rl, rl, MKT[:, j, :], 1.0, 0.0, ALU.mult, ALU.max,
                                             smax[:, j:j + 1]).then_inc(s_z, 1)
                    dve.wait_ge(s_z, 4 * b + j + 1)
                    dve.tensor_scalar(sbias[:, j:j + 1], smax[:, j:j + 1], k_neg[:, 0:1], None,
                                      ALU.mult).then_inc(s_sb, 1)

                def inverse_sum(j):
                    dve.wait_ge(s_ex, 4 * b + j + 1)
                    dve.reciprocal(srec[:, j:j + 1], ssum[:, j:j + 1]).then_inc(s_rec, 1)
                    dve.wait_ge(s_rec, 4 * b + j + 1)
                    dve.tensor_scalar(srs[:, j:j + 1], srec[:, j:j + 1], SPROB, None, ALU.mult).then_inc(s_srs, 1)

                def prob_low(j):
                    dve.wait_ge(s_ph, 4 * b + j + 1)
                    dve.scalar_tensor_tensor(out=PR[:, 1, j, :], in0=EX[:, j % 2, :], scalar=srs[:, j:j + 1],
                                             in1=PR[:, 0, j, :], op0=ALU.mult, op1=ALU.subtract).then_inc(s_pl, 1)

                masked_max(0)
                masked_max(1)
                for j in range(JT):
                    if j == JT - 1 and routed:
                        x2_low(b - 1, 0)
                        x2_low(b - 1, 1)
                    inverse_sum(j)
                    prob_low(j)
                    if j + 2 < JT:
                        masked_max(j + 2)

                if front:
                    dve.wait_ge(s_x[1 - par], 16 * (i + 1 + par))
                    statistics(b + 1, 1 - par, 0)
                for j in range(JT):
                    if j == 2 and routed:
                        x2_low(b - 1, 2)
                        x2_low(b - 1, 3)
                    if j == 3 and routed:
                        route(b - 1)
                    dve.wait_ge(s_vh, 4 * b + j + 1)
                    dve.scalar_tensor_tensor(out=VV[:, 1, j, :], in0=ACC[j][:, :], scalar=TO32, in1=VV[:, 0, j, :],
                                             op0=ALU.mult, op1=ALU.subtract).then_inc(s_vl, 1)
                if front:
                    xt_low(b + 1, 1 - par, [0, 1])
                for j in range(JT):
                    if j == 1 and front:
                        xt_low(b + 1, 1 - par, [2, 3])
                    dve.wait_ge(s_op, 4 * b + j + 1)
                    dve.scalar_tensor_tensor(out=Xt(par, j), in0=ACC[j][:, :], scalar=g_res[:, 0:1], in1=Xt(par, j),
                                             op0=ALU.mult, op1=ALU.add).then_inc(s_res, 1)
                    if j == 1 and routed:
                        place(b - 1, 1 - par, i - 1 + par)
                    if j == 2 and front:
                        largest(b + 1)
                statistics(b, par, 1)

            graph(0, 0)
            graph(0, 1)
            graph(1, 0)
            graph(1, 1)
            with dve.Fori(2, B // 2 - 1) as i:
                graph(i, 0)
                graph(i, 1)
            graph(B // 2 - 1, 0, last=True)
            graph(B // 2 - 1, 1, last=True)

            for j in range(JT):
                x2_low(B - 1, j)
            route(B - 1)
            place(B - 1, 1, B // 2 - 1)

            def chain(signal, count):
                done = [0]

                def step(instruction):
                    done[0] += 1
                    assert done[0] <= count
                    instruction.then_inc(signal, 1)
                    dve.wait_ge(signal, done[0])
                return step

            def over(small, outer):
                return small[:, :].unsqueeze(1).broadcast_to([P, outer, E])

            dve.wait_ge(s_row, 2 * B)
            step = chain(s_tab, N_TAB)
            step(dve.tensor_tensor(cnt[:, :], R[:, :], base[:, :], ALU.subtract))
            step(dve.tensor_copy(cnti[:, :], cnt[:, :]))
            step(dve.tensor_scalar(cnti[:, :], cnti[:, :], ROWS.bit_length() - 1, None, ALU.logical_shift_right))
            step(dve.tensor_copy(ntile[:, :], cnti[:, :]))
            step(dve.tensor_tensor(tmpee[:, :, :], earlier[:, :, :], over(ntile, E), ALU.mult))
            step(dve.tensor_reduce(tstart[:, :], tmpee[:, :, :], AX, ALU.add))
            step(dve.tensor_tensor(tend[:, :], tstart[:, :], ntile[:, :], ALU.add))
            step(dve.tensor_scalar(total1[:, :], tend[:, E - 1:E], -1.0, None, ALU.add))
            step(dve.tensor_scalar(tin[:, :], tile_iota[:, :], total1[:, 0:1], None, ALU.min))
            step(dve.tensor_tensor(past[:, :, :], tin[:, :].unsqueeze(2).broadcast_to([P, NF, E]), over(tend, NF),
                                   ALU.is_ge))
            step(dve.tensor_tensor(pastn[:, :, :], past[:, :, :], over(ntile, NF), ALU.mult))
            step(dve.tensor_reduce(tex[:, :], past[:, :, :], AX, ALU.add))
            step(dve.tensor_reduce(tst[:, :], pastn[:, :, :], AX, ALU.add))
            step(dve.tensor_tensor(trow[:, :], tin[:, :], tst[:, :], ALU.subtract))
            step(dve.tensor_scalar(trow[:, :], trow[:, :], float(ROWS), None, ALU.mult))
            step(dve.scalar_tensor_tensor(out=trow[:, :], in0=tex[:, :], scalar=float(REGION), in1=trow[:, :],
                                          op0=ALU.mult, op1=ALU.add))
            step(dve.tensor_copy(TAB[:, 0, 0:NF], tex[:, :]))
            step(dve.tensor_copy(TAB[:, 1, 0:NF], trow[:, :]))
            step(dve.tensor_copy(TAB[:, 0, NF:NT], expert_iota[:, :]))
            step(dve.scalar_tensor_tensor(out=TAB[:, 1, NF:NT], in0=ntile[:, :], scalar=float(ROWS), in1=base[:, :],
                                          op0=ALU.mult, op1=ALU.add))

            dve.wait_ge(s_g0, 2)
            step = chain(s_pad_at, N_PAD)
            step(dve.tensor_scalar(dump[:, :], iota_p[:, 0, 0:1], float(E * REGION), None, ALU.add))
            step(dve.tensor_scalar(few[:, :], cnt[:, :], float(ROWS), None, ALU.is_lt))
            step(dve.tensor_tensor(bad[:, :, :], oh0[:, :, :], over(few, 2), ALU.mult))
            step(dve.tensor_tensor(dpos[:, :, :], cex0[:, :, :], over(few, 2), ALU.mult))
            step(dve.tensor_tensor(pos0[:, :, :], iota_p[:, :, :], dpos[:, :, :], ALU.subtract))
            step(dve.tensor_tensor(pos0[:, :, :], pos0[:, :, :], over(R, 2), ALU.add))
            step(dve.tensor_scalar(dpos[:, :, :], pos0[:, :, :], -1.0, dump[:, 0:1], ALU.mult, ALU.add))
            step(dve.tensor_tensor(dpos[:, :, :], dpos[:, :, :], bad[:, :, :], ALU.mult))
            step(dve.tensor_tensor(padrow[:, :, :], pos0[:, :, :], dpos[:, :, :], ALU.add))

            ef = eebits[:, :].bitcast(F32)
            step = chain(s_wx, N_WX)
            step(dve.tensor_tensor(to_y[:, :], ef[:, 0:E], ef[:, E:2 * E], ALU.mult))
            step(dve.tensor_scalar(to_y[:, :], to_y[:, :], TO_Y, None, ALU.mult))
            step(dve.tensor_tensor(past[:, :, :], tex[:, :].unsqueeze(2).broadcast_to([P, NF, E]),
                                   over(expert_iota, NF), ALU.is_equal))
            step(dve.tensor_scalar(valid[:, :], tile_iota[:, :], total1[:, 0:1], None, ALU.is_le))
            step(dve.tensor_tensor(past[:, :, :], past[:, :, :], valid[:, :].unsqueeze(2).broadcast_to([P, NF, E]),
                                   ALU.mult))
            step(dve.tensor_tensor(WX[:, 0:NF, :], past[:, :, :], over(to_y, NF), ALU.mult))
            step(dve.tensor_tensor(tmpee[:, :, :], expert_iota[:, :].unsqueeze(2).broadcast_to([P, E, E]),
                                   over(expert_iota, E), ALU.is_equal))
            step(dve.tensor_tensor(WX[:, NF:NT, :], tmpee[:, :, :], over(to_y, E), ALU.mult))

            def hidden(n, par):
                dve.wait_ge(s_hh, n + 1)
                dve.scalar_tensor_tensor(out=HH[:, par, 1, :], in0=HB[par][:, :], scalar=0.0, in1=HH[:, par, 0, :],
                                         op0=ALU.max, op1=ALU.subtract).then_inc(s_hl, 1)

            def rows_low(n, par):
                for s in range(SUB):
                    dve.wait_ge(s_fh, SUB * n + s + 1)
                    dve.tensor_tensor(XFT[:, par, 1, :, s * P:(s + 1) * P],
                                      TX[s][:, :].rearrange("p (k n) -> p k n", k=KT),
                                      XFT[:, par, 0, :, s * P:(s + 1) * P], ALU.subtract).then_inc(s_fl, 1)

            def factors(n, q, turn):
                dve.wait_ge(s_xf[q], turn)
                if not isinstance(n, int) or n >= RING:
                    dve.wait_ge(s_y0, n - RING + 1)
                    dve.wait_ge(s_add[q % 2], 16 * (n - RING - q % 2) + 32)
                settle(dve)
                dve.tensor_copy(token[:, q, :].unsqueeze(2), XF[:, q, :, :].bitcast(I32)[:, :, D:D + 1]).then_inc(s_fr, 1)
                dve.tensor_tensor(gsel[:, q, :, :], XF[:, q, :, D + 1:D + 1 + E],
                                  WX[:, bass.ds(n, 1), :].broadcast_to([P, SUB, E]), ALU.mult).then_inc(s_fr, 1)
                dve.wait_ge(s_fr, 3 * n + 2)
                settle(dve)
                dve.tensor_reduce(fr[:, q, :], gsel[:, q, :, :], AX, ALU.add).then_inc(s_fr, 1)

            def result(n, q, again=True):
                if again:
                    dve.wait_ge(s_add[q % 2], 16 * (n - q % 2))
                dve.wait_ge(s_fr, 3 * (n + 1))
                dve.wait_ge(s_yp, 2 * n + 2)
                dve.tensor_scalar(YF[:, q % 2, 1, :], YB[q % 2][1][:, :], fr[:, q, 1:2], None,
                                  ALU.mult).then_inc(s_y1, 1)

            rows_low(0, 0)
            for n in range(RING):
                rows_low(n + 1, (n + 1) % 2)
                hidden(n, n % 2)
                if n > 0:
                    result(n - 1, n - 1, again=n > 2)
                factors(n, n, 16)

            def tiles(i, last=False):
                for q in range(RING):
                    n = RING * i + q
                    if not (last and q == RING - 1):
                        rows_low(n + 1, (q + 1) % 2)
                    hidden(n, q % 2)
                    result(n - 1, (q - 1) % RING)
                    factors(n, q, 16 * (i + 1))

            with dve.Fori(1, NT // RING - 1) as i:
                tiles(i)
            tiles(NT // RING - 1, last=True)
            result(NT - 1, RING - 1)

        @block.tensor
        def _(pe):
            def product(bank, left, right, terms, arrive=None):
                last = None
                for k in range(terms):
                    if arrive is not None:
                        arrive(k)
                    for n, (a, c) in enumerate(((0, 0), (0, 1), (1, 0))):
                        last = pe.matmul(bank, left(a, k), right(c, k), start=(k == 0 and n == 0),
                                         stop=(k == terms - 1 and n == 2))
                return last

            pe.wait_ge(s_const, 18)
            for t in range(8):
                if t == 0:
                    pe.wait_ge(s_wq, 16)
                if t == 4:
                    pe.wait_ge(s_wk, 16)
                if t >= 6:
                    pe.wait_ge(s_wta, 1)
                    pe.wait_ge(s_wtd, 1)
                raw = WQR if t < 4 else WKR
                for k in range(KT):
                    o = k * D + (t % 4) * P
                    mm = pe.transpose(BANKS[t % 6][:, k * P:(k + 1) * P], raw[:, o:o + P], ident[:, :])
                mm.then_inc(s_wtp, 1)
            pe.wait_ge(s_wta, 4)
            pe.wait_ge(s_wtd, 4)
            for m in range(KT):
                for k in range(KT):
                    mm = pe.matmul(ACC[m][:, :], WQT[:, k * D + m * P:k * D + (m + 1) * P],
                                   WKT[:, k * D:(k + 1) * D], start=(k == 0), stop=(k == KT - 1))
                mm.then_inc(s_m, 1)

            def xt(b, tiles=range(JT)):
                for j in tiles:
                    pe.wait_ge(s_xn, 4 * b + j + 1)
                    if not isinstance(b, int) or b > 0 or j >= 2:
                        pe.wait_ge(s_xtl, 4 * b + j - 1)
                    if j == 0 and not (isinstance(b, int) and b == 0):
                        pe.wait_ge(s_mkt, 2 * b)
                    if j < 2 and not (isinstance(b, int) and b < 2):
                        pe.wait_ge(s_x2l, 4 * (b - 1))
                    for k in range(KT):
                        mm = pe.transpose(TX[j % 2][:, k * P:(k + 1) * P], XN[:, j, k * P:(k + 1) * P], ident[:, :])
                    mm.then_inc(s_xtp, 1)

            def mask_t(b, halves=range(2)):
                pe.wait_ge(s_mk, b + 1)
                cols = MK[:, :].rearrange("p (n m j) -> p n j m", n=JT, j=JT)
                for h in halves:
                    if h == 1:
                        pe.wait_ge(s_xtl, 4 * (b + 1))
                    for j in range(2):
                        for n in range(JT):
                            o = j * N + n * P
                            mm = pe.transpose(MASKB[h][:, o:o + P], cols[:, n, 2 * h + j, :], ident16[:, :])
                    mm.then_inc(s_mtp, 1)

            def x2_t(r, par, j, b=None):
                pe.wait_ge(s_x2h, 4 * r + j + 1)
                if j >= 2:
                    pe.wait_ge(s_x2l, 4 * r + j - 1)
                elif b is not None:
                    pe.wait_ge(s_xtl, 4 * b + 3 + j)
                    if j == 0:
                        pe.wait_ge(s_mkt, 2 * (b + 1))
                else:
                    pe.wait_ge(s_mkt, 2 * B)
                for k in range(KT):
                    mm = pe.transpose(TX[j % 2][:, k * P:(k + 1) * P], X2S[:, par, j, k * P:(k + 1) * P], ident[:, :])
                mm.then_inc(s_x2p, 1)

            def logits(r, j):
                pe.wait_ge(s_x2l, 4 * r + j + 1)
                if j == 0 and (not isinstance(r, int) or r > 0):
                    pe.wait_ge(s_lgc, r)
                    pe.wait_ge(s_row, 2 * r)
                product(RB[:, j * E:(j + 1) * E], lambda a, k: X2T[:, j % 2, a * KT + k, :],
                        lambda c, k: WG[:, c, k, :], KT).then_inc(s_lg, 1)

            def positions(r):
                pe.wait_ge(s_ohs, r + 1)
                out0 = 64
                pe.matmul(RB[:, out0:out0 + JT * E], before[:, :], OHS[:, :, :].rearrange("p j e -> p (j e)"),
                          start=True, stop=False, skip_group_check=True)
                for j in range(JT):
                    for later in range(j + 1, JT + 1):
                        mm = pe.matmul(RB[:, out0 + later * E:out0 + (later + 1) * E], ones16[:, :], OHS[:, j, :],
                                       start=False, stop=(j == JT - 1), skip_group_check=True)
                mm.then_inc(s_pos, 1)

            xt(0)
            mask_t(0)
            pe.wait_ge(s_wlo, 2 * KT + 1)

            def graph(i, par, last=False):
                b = 2 * i + par
                front = not (last and par == 1)
                XA = (XTH[:, par], XTL[:, par])

                pe.wait_ge(s_xtl, 4 * (b + 1))
                for j in range(JT):
                    if isinstance(b, int) and b == 0:
                        pass
                    else:
                        pe.wait_ge(s_res, 4 * b - 3 + j)
                    product(ACC[j][:, :], lambda a, k: WM[:, a, k, j * P:(j + 1) * P],
                            lambda c, k: XA[c][:, k, :], KT).then_inc(s_tp, 1)
                for j in range(JT):
                    product(ACC[j][:, :], lambda a, k: XA[a][:, k, j * P:(j + 1) * P],
                            lambda c, k: TT[:, c, k, :], KT,
                            lambda k: pe.wait_ge(s_tl, 4 * b + k + 1) if j == 0 else None).then_inc(s_sp, 1)
                routed = not isinstance(b, int) or b > 0
                if routed:
                    x2_t(b - 1, 1 - par, 0, b)
                    x2_t(b - 1, 1 - par, 1, b)
                for j in range(JT):
                    pe.wait_ge(s_rl, 4 * b + j + 1)
                    product(ACC[j][:, :], lambda a, k: XA[a][:, k, j * P:(j + 1) * P],
                            lambda c, k: WV[:, c, k, :], KT).then_inc(s_vp, 1)
                    if j == 1 and routed:
                        for t in (0, 1):
                            logits(b - 1, t)
                        for t in (2, 3):
                            x2_t(b - 1, 1 - par, t, b)
                    if j == 2 and routed:
                        for t in (2, 3):
                            logits(b - 1, t)
                if front:
                    xt(b + 1, [0, 1])
                    mask_t(b + 1, [0])
                pe.wait_ge(s_pl, 4 * (b + 1))
                for j in range(JT):
                    product(ACC[j][:, :], lambda a, k: PR[:, a, k, j * P:(j + 1) * P],
                            lambda c, k: VV[:, c, k, :], JT,
                            lambda k: pe.wait_ge(s_vl, 4 * b + k + 1) if j == 0 else None).then_inc(s_op, 1)
                    if j == 0 and front:
                        xt(b + 1, [2, 3])
                    if j == 0 and routed:
                        positions(b - 1)
                    if j == 1 and front:
                        mask_t(b + 1, [1])

            graph(0, 0)
            graph(0, 1)
            graph(1, 0)
            graph(1, 1)
            with pe.Fori(2, B // 2 - 1) as i:
                graph(i, 0)
                graph(i, 1)
            graph(B // 2 - 1, 0, last=True)
            graph(B // 2 - 1, 1, last=True)
            for j in range(JT):
                x2_t(B - 1, 1, j)
                logits(B - 1, j)
            positions(B - 1)

            pe.wait_ge(s_x2l, 4 * B)
            pe.wait_ge(s_el, B)
            pe.wait_ge(s_row, 2 * B)
            pe.wait_ge(s_tab, N_TAB)

            def rows_t(n, q, turn):
                pe.wait_ge(s_xf[q], turn)
                for s in range(SUB):
                    if not isinstance(n, int) or n > 0:
                        pe.wait_ge(s_fl, SUB * (n - 1) + s + 1)
                    for k in range(KT):
                        mm = pe.transpose(TX[s][:, k * P:(k + 1) * P], XF[:, q, s, k * P:(k + 1) * P], ident[:, :])
                    mm.then_inc(s_fp, 1)

            def hidden(n, q, e):
                par = q % 2
                pe.wait_ge(s_fl, SUB * (n + 1))
                if not isinstance(n, int) or n > 1:
                    pe.wait_ge(s_hl, n - 1)
                settle(pe)
                W = (W1H, W1L)
                w = e * (KT * C)
                for m in range(CT):
                    mm = product(HB[par][:, m * ROWS:(m + 1) * ROWS],
                                 lambda a, k: W[a][:, :, :].rearrange("p e n -> p (e n)")[
                                     :, bass.ds(w + (k * C + m * P), P)],
                                 lambda c, k: XFT[:, par, c, k, :], KT)
                mm.then_inc(s_hp, 1)

            def expert_out(n, q, e):
                par = q % 2
                pe.wait_ge(s_hh, n + 1)
                pe.wait_ge(s_hl, n + 1)
                W = (W2H, W2L)
                w = e * (CT * D)
                for s in range(SUB):
                    if not isinstance(n, int) or n > 1:
                        pe.wait_ge((s_y0, s_y1)[s], n - 1)
                    product(YB[par][s][:, :],
                            lambda a, m: HH[:, par, a, m * ROWS + s * P:m * ROWS + (s + 1) * P],
                            lambda c, m: W[c][:, :, :].rearrange("p e n -> p (e n)")[:, bass.ds(w + m * D, D)],
                            CT).then_inc(s_yp, 1)

            def expert(n):
                return pe.value_load(TAB[0:1, 0, bass.ds(n, 1)], min_val=0, max_val=E - 1)

            def tiles(i, first=False, last=False):
                es = [None if first else expert(RING * i - 1)] + [expert(RING * i + q) for q in range(RING)]
                for q in range(RING):
                    n = RING * i + q
                    if not (last and q == RING - 1):
                        rows_t(n + 1, (q + 1) % RING, 16 * (i + 1) + (16 if q == RING - 1 else 0))
                    hidden(n, q, es[q + 1])
                    if not (first and q == 0):
                        expert_out(n - 1, (q - 1) % RING, es[q])
                return es[RING]

            rows_t(0, 0, 16)
            tiles(0, first=True)
            with pe.Fori(1, NT // RING - 1) as i:
                tiles(i)
            expert_out(NT - 1, RING - 1, tiles(NT // RING - 1, last=True))


_INS = ['x', 'adj', 'L0_gnn_weight', 'L0_gnn_wq', 'L0_gnn_wk', 'L0_ffn_Wg', 'L0_ffn_W1', 'L0_ffn_W2']
_OUTS = [((16, 512, 512), 'float32')]


def kernel(**inputs):
    import numpy as _np
    import concourse.bacc as _bacc
    from concourse import mybir as _mybir
    from concourse.bass_utils import run_bass_kernel_spmd as _run

    nc = _bacc.Bacc("TRN2", target_bir_lowering=False, num_devices=1)
    arrays, args = {}, []
    for name in _INS:
        a = _np.ascontiguousarray(inputs[name])
        arrays[f"in_{name}_dram"] = a
        args.append(nc.dram_tensor(f"in_{name}_dram", a.shape, _mybir.dt.from_np(a.dtype), kind="ExternalInput").ap())
    for i, (shape, dtype) in enumerate(_OUTS):
        dt = _mybir.dt.from_np(_np.dtype(dtype))
        args.append(nc.dram_tensor(f"out_{i}_dram", shape, dt, kind="ExternalOutput").ap())
    build_program(nc, *args)
    r = _run(nc, [arrays], core_ids=[0])
    got = tuple(r.results[0][f"out_{i}_dram"] for i in range(len(_OUTS)))
    return got[0]
```

```python
from contextlib import ExitStack

import concourse.bass as bass
from concourse import mybir

F32 = mybir.dt.float32
F16 = mybir.dt.float16
I32 = mybir.dt.int32
U32 = mybir.dt.uint32
ALU = mybir.AluOpType
ACT = mybir.ActivationFunctionType
AX = mybir.AxisListType.X
RMAX = bass.bass_isa.ReduceOp.max

P = 128
EPS = 1e-5
SX = 2.0 ** 8
SW = 2.0 ** 8
TO32 = 2.0 ** -11
TO_Y = 1.0 / (32.0 * SW)
SPROB = 2.0 ** 14
SX2 = 2.0 ** 3
SW1 = 2.0 ** 2


def build_program(nc, x, adj, weight, wq, wk, Wg, W1, W2, out):
    B, N, D = x.shape
    E, _, C = W1.shape
    JT = N // P
    KT = D // P
    CT = C // P
    T = B * N
    ROWS = 256
    SUB = ROWS // P
    REGION = T + ROWS
    NF = (2 * T - E * (ROWS - 1)) // ROWS
    HALVES = (2 * T + E * (P - 1)) // P - NF * SUB
    NT = NF + -(-HALVES // SUB)
    UNITS = SUB * (NT - NF)
    EARLY = 8
    RING = 5
    META = 16
    WIDE = D + META
    assert JT == 4 and KT == 4 and CT == 2 and E == 8 and B % 2 == 0
    ROUND = 2 * RING
    ROUNDS = (NT - EARLY) // ROUND
    assert RING == 5 and EARLY == 8 and NT == EARLY + ROUND * ROUNDS and NF == EARLY + 8 * ROUNDS
    assert (2 * (T - 2 * N) - E * (ROWS - 1)) // ROWS >= EARLY

    sorted_x = nc.dram_tensor("sorted_x", [E * REGION + P, WIDE], F32).ap()

    x_v = x.rearrange("b (p j) d -> b p (j d)", j=JT)
    adj_v = adj.rearrange("b (p j) m -> b p (j m)", j=JT)
    out_v = out.rearrange("b (p j) d -> b p (j d)", j=JT)
    out_rows = out.rearrange("b n d -> (b n) d")
    w1_v = W1.rearrange("e (k p) c -> e p k c", p=P)
    w2_v = W2.rearrange("e (k p) d -> e p k d", p=P)

    with ExitStack() as ctx:
        def sb(name, shape, dt):
            return ctx.enter_context(nc.sbuf_tensor(name, shape, dt))

        def pb(name, shape, dt):
            return ctx.enter_context(nc.psum_tensor(name, shape, dt))

        def sem(name):
            return ctx.enter_context(nc.semaphore(name))

        ident = sb("ident", [P, P], F32)
        ident16 = sb("ident16", [P, P], F16)
        before = sb("before", [P, P], F16)
        ones16 = sb("ones16", [P, P], F16)
        minus_half = sb("minus_half", [P, JT], F32)
        expert_iota = sb("expert_iota", [P, E], F32)
        WM = sb("WM", [P, 2, KT, D], F16)
        WV = sb("WV", [P, 2, KT, D], F16)
        WG = sb("WG", [P, KT, 2, E], F16)
        W1H = sb("W1H", [P, E, KT * C], F16)
        W1L = sb("W1L", [P, E, KT * C], F16)
        W2H = sb("W2H", [P, E, CT * D], F16)
        W2L = sb("W2L", [P, E, CT * D], F16)
        wraw = sb("wraw", [P, KT * C], F32)
        wg_raw = sb("wg_raw", [P, KT * E], F32)
        XBUF = sb("XBUF", [P, RING * SUB * WIDE], F32)
        ADJ = sb("ADJ", [P, JT * N], I32)
        MK = sb("MK", [P, JT * N], F16)
        MKT = sb("MKT", [P, JT, N], F16)
        XN = sb("XN", [P, JT, D], F32)
        XTH = sb("XTH", [P, 2, KT, N], F16)
        XTL = sb("XTL", [P, 2, KT, N], F16)
        TT = sb("TT", [P, 2, KT, N], F16)
        VV = sb("VV", [P, 2, JT, D], F16)
        PR = sb("PR", [P, 2, JT, N], F16)
        RL = sb("RL", [P, 2, N], F32)
        EX = sb("EX", [P, 2, N], F32)
        X2S = sb("X2S", [P, 2, JT, WIDE], F32)
        X2T = sb("X2T", [P, 2, 2 * KT, P], F16)
        LG = sb("LG", [P, JT, E], F32)
        top = sb("top", [P, JT, E], F32)
        tix = sb("tix", [P, JT, E], U32)
        tixf = sb("tixf", [P, 2, JT], F32)
        OH = sb("OH", [P, 2, JT, E], F32)
        OHS = sb("OHS", [P, JT, E], F16)
        row_of = sb("row_of", [P, JT, E], F32)
        picked = sb("picked", [P, 2, JT, E], F32)
        slot = sb("slot", [P, 2, 2, JT], I32)
        DL = sb("DL", [P, JT], F32)
        gx = sb("gx", [P, JT], F32)
        gd = sb("gd", [P, JT], F32)
        gates = sb("gates", [P, 2, JT], F32)
        gated = sb("gated", [P, 2, JT, E], F32)
        slotf = sb("slotf", [P, 2, JT], F32)
        R = sb("R", [P, E], F32)
        base = sb("base", [P, E], F32)
        earlier = sb("earlier", [P, E, E], F32)
        cnt = sb("cnt", [P, E], F32)
        taken = sb("taken", [P, E], F32)
        rest = sb("rest", [P, E], F32)
        few = sb("few", [P, E], F32)
        oh0 = sb("oh0", [P, E], F32)
        cex0 = sb("cex0", [P, E], F32)
        dump = sb("dump", [P, 1], F32)
        pos0 = sb("pos0", [P, E], F32)
        dpos = sb("dpos", [P, E], F32)
        bad = sb("bad", [P, E], F32)
        total1 = sb("total1", [P, 1], F32)
        cnti = sb("cnti", [P, E], I32)
        ntile = sb("ntile", [P, E], F32)
        tend = sb("tend", [P, E], F32)
        tstart = sb("tstart", [P, E], F32)
        tile_iota = sb("tile_iota", [P, NF], F32)
        TAB = sb("TAB", [P, 2, NF], I32)
        TABU = sb("TABU", [P, 2, SUB + UNITS], I32)
        used = sb("used", [P, E], F32)
        padrow = sb("padrow", [P, E], I32)
        iota_p = sb("iota_p", [P, E], F32)
        pad_rows = sb("pad_rows", [P, WIDE], F32)
        token = sb("token", [P, RING, SUB], I32)
        gsel = sb("gsel", [P, RING, SUB, E], F32)
        to_y = sb("to_y", [P, E], F32)
        fr = sb("fr", [P, RING, SUB], F32)
        k_gate = sb("k_gate", [P, 1], F32)
        bs = sb("bs", [P, 2, JT, 6], F32)
        mv = sb("mv", [P, 2, JT, 2], F32)
        ve = sb("ve", [P, 2, JT], F32)
        rs = sb("rs", [P, 2, JT], F32)
        rr = sb("rr", [P, 2, JT], F32)
        nm = sb("nm", [P, 2, JT], F32)
        nb = sb("nb", [P, 2, JT], F32)
        smax = sb("smax", [P, JT], F32)
        sbias = sb("sbias", [P, JT], F32)
        ssum = sb("ssum", [P, JT], F32)
        srec = sb("srec", [P, JT], F32)
        srs = sb("srs", [P, JT], F32)
        mxp = sb("mxp", [P, KT], F32)
        mx = sb("mx", [P, 3], F32)
        mxa = sb("mxa", [P, 3], F32)
        ebits = sb("ebits", [P, 3], I32)
        ibits = sb("ibits", [P, 3], I32)
        wsc = sb("wsc", [P, 3], F32)
        k_pos = sb("k_pos", [P, 1], F32)
        k_neg = sb("k_neg", [P, 1], F32)
        g_res = sb("g_res", [P, 1], F32)
        emx = sb("emx", [P, 1], F32)
        emxa = sb("emxa", [P, 1], F32)
        eebits = sb("eebits", [P, 2 * E], I32)
        eibits = sb("eibits", [P, 1], I32)
        esc = sb("esc", [P, 1], F32)

        ACC = [pb(f"ACC{j}", [P, 512], F32) for j in range(4)]
        TX = [pb(f"TX{j}", [P, 512], F32) for j in range(2)]
        MT = pb("MT", [P, 512], F32)
        RB = pb("RB", [P, 512], F32)

        constants_ready = sem("constants_ready")
        passed = sem("passed")
        wq_loaded = sem("wq_loaded")
        wk_loaded = sem("wk_loaded")
        weight_loaded = sem("weight_loaded")
        wg_loaded = sem("wg_loaded")
        wt_transposed = sem("wt_transposed")
        wt_copied_act = sem("wt_copied_act")
        wt_copied_dve = sem("wt_copied_dve")
        m_ready = sem("m_ready")
        part_max = sem("part_max")
        all_max = sem("all_max")
        scale_steps = sem("scale_steps")
        w_high = sem("w_high")
        w_low = sem("w_low")
        x_loaded = [sem(f"x_loaded{i}") for i in range(2)]
        adj_loaded = sem("adj_loaded")
        chunk_loaded = sem("chunk_loaded")
        stats1 = sem("stats1")
        meanvar1 = sem("meanvar1")
        ln1_steps = sem("ln1_steps")
        ln1_scale = sem("ln1_scale")
        xn_ready = sem("xn_ready")
        xnt_psum = sem("xnt_psum")
        xnt_high = sem("xnt_high")
        xnt_low = sem("xnt_low")
        mask_ready = sem("mask_ready")
        mask_psum = sem("mask_psum")
        maskt_ready = sem("maskt_ready")
        t_psum = sem("t_psum")
        t_high_ready = sem("t_high_ready")
        t_low_ready = sem("t_low_ready")
        scores_psum = sem("scores_psum")
        relu_ready = sem("relu_ready")
        score_max = sem("score_max")
        exp_bias = sem("exp_bias")
        exp_ready = sem("exp_ready")
        sum_inverse = sem("sum_inverse")
        prob_scale = sem("prob_scale")
        prob_high = sem("prob_high")
        prob_low_ready = sem("prob_low_ready")
        v_psum = sem("v_psum")
        v_high = sem("v_high")
        v_low = sem("v_low")
        attention_psum = sem("attention_psum")
        x1_ready = sem("x1_ready")
        x1_stored = sem("x1_stored")
        stats2 = sem("stats2")
        meanvar2 = sem("meanvar2")
        ln2_steps = sem("ln2_steps")
        ln2_scale = sem("ln2_scale")
        x2_ready = sem("x2_ready")
        x2t_psum = sem("x2t_psum")
        x2t_high = sem("x2t_high")
        x2t_low = sem("x2t_low")
        logits_psum = sem("logits_psum")
        logits_read = sem("logits_read")
        top_ready = sem("top_ready")
        top_index = sem("top_index")
        index_float = sem("index_float")
        onehot = sem("onehot")
        onehot_sum = sem("onehot_sum")
        logit_gap = sem("logit_gap")
        positions_psum = sem("positions_psum")
        positions_read = sem("positions_read")
        pick_steps = sem("pick_steps")
        slot_ready = sem("slot_ready")
        rows_scattered = [sem(f"rows_scattered{i}") for i in range(2)]
        table_steps = sem("table_steps")
        pads_scattered = sem("pads_scattered")
        pad_steps = sem("pad_steps")
        tile_loaded = [sem(f"tile_loaded{i}") for i in range(RING)]
        tile_psum = sem("tile_psum")
        tile_high = sem("tile_high")
        tile_low = sem("tile_low")
        factor_steps = sem("factor_steps")
        row_factors = sem("row_factors")
        hidden_psum = sem("hidden_psum")
        hidden_high = sem("hidden_high")
        hidden_low = sem("hidden_low")
        y_psum = sem("y_psum")
        y_first = sem("y_first")
        y_second = sem("y_second")
        y_added = [sem(f"y_added{i}") for i in range(2)]
        gate_exp = sem("gate_exp")
        gate_steps = sem("gate_steps")
        first_tokens = sem("first_tokens")
        chunk_max = sem("chunk_max")
        chunk_max_all = sem("chunk_max_all")
        chunk_scale = sem("chunk_scale")
        chunk_high = sem("chunk_high")
        chunk_low = sem("chunk_low")

        WQR = PR[:, :, :, :].rearrange("p a j n -> p (a j n)").bitcast(F32)
        WKR = TT[:, :, :, :].rearrange("p a j n -> p (a j n)").bitcast(F32)
        WVR = VV[:, :, :, :].rearrange("p a j n -> p (a j n)").bitcast(F32)
        WQT = W2H[:, E - 4:E, :].rearrange("p e n -> p (e n)").bitcast(F32)
        WKT = W2L[:, E - 4:E, :].rearrange("p e n -> p (e n)").bitcast(F32)
        BANKS = ACC + TX
        X = XBUF[:, :].rearrange("p (b n) -> p b n", b=2)[:, :, 0:JT * D]
        XF = XBUF[:, :].rearrange("p (q s n) -> p q s n", q=RING, s=SUB)
        XFT = XN[:, :, :].rearrange("p j d -> p (j d)").bitcast(F16).rearrange(
            "p (b a k n) -> p b a k n", b=2, a=2, k=KT)
        HH = RL[:, :, :].rearrange("p a n -> p (a n)").bitcast(F16).rearrange("p (b a n) -> p b a n", b=2, a=2)
        YF = XTH[:, :, :, :].rearrange("p a j n -> p (a j n)").bitcast(F32).rearrange(
            "p (b s d) -> p b s d", b=2, s=SUB)
        HB = [ACC[0], ACC[1]]
        YB = [[ACC[2], ACC[3]], [MT, RB]]
        WX = WV[:, :, :, :].rearrange("p a k n -> p (a k n)").bitcast(F32)[:, 0:(NF + UNITS) * E].rearrange(
            "p (t e) -> p t e", e=E)
        scratch = WM[:, :, :, :].rearrange("p a k n -> p (a k n)").bitcast(F32)
        past, pastn = [scratch[:, a * NF * E:(a + 1) * NF * E].rearrange("p (t e) -> p t e", e=E) for a in range(2)]
        tin, tex, tst, trow, valid = [scratch[:, (2 * E + a) * NF:(2 * E + a + 1) * NF] for a in range(5)]
        tmpee = scratch[:, (2 * E + 6) * NF:(2 * E + 6) * NF + E * E].rearrange("p (a b) -> p a b", b=E)
        MASKB = [MT[:, :].bitcast(F16), TX[0][:, :].bitcast(F16)]

        N_EARLY = 15
        N_TAB = N_EARLY + 18
        N_EARLY_WX = 7
        N_PAD = 9
        N_COUNTS = N_EARLY_WX + 12
        N_HALVES = N_COUNTS + 13
        N_WX = N_HALVES + 3

        block = ctx.enter_context(nc.Block())

        def settle(engine):
            engine.sem_inc(passed, 1)

        def halved(t):
            return t % RING == RING - 1

        def slot_of(i, t):
            return 2 * i + t // RING if halved(t) else EARLY + 8 * i + t - t // RING

        def loaded(i, t):
            before = (EARLY + RING - 1 - (EARLY + t) % RING) // RING
            turns = 2 * i + t // RING + 1
            return 16 * before + (16 * SUB if halved(t) else 16) * turns

        def tokens(par):
            return X2S[:, par, :, :].bitcast(I32)[:, :, D:D + 1]

        def Xt(par, j):
            return X[:, par, j * D:(j + 1) * D]

        @block.sync
        def _(sp):
            def load_x(b, par, first=False):
                if not first:
                    sp.wait_ge(x2_ready, 4 * (b - 1))
                    settle(sp)
                    sp.wait_ge(x1_stored, 16 * (b - 1))
                    settle(sp)
                sp.dma_start(X[:, par, :], x_v[b]).then_inc(x_loaded[par], 16)

            def load_weights(i, par, b):
                sp.wait_ge(chunk_low, b)
                settle(sp)
                if par == 0:
                    sp.dma_start(wraw[:, :].rearrange("p (k c) -> p k c", k=KT), w1_v[i]).then_inc(chunk_loaded, 16)
                else:
                    sp.dma_start(wraw[:, :].rearrange("p (k c) -> p k c", k=CT), w2_v[i]).then_inc(chunk_loaded, 16)

            def load_adj(b, first=False):
                if not first:
                    sp.wait_ge(mask_ready, b)
                    settle(sp)
                sp.dma_start(ADJ[:, :], adj_v[b]).then_inc(adj_loaded, 16)

            sp.dma_start(WQR.rearrange("p (k o) -> p k o", k=KT),
                         wq.rearrange("(k p) o -> p k o", p=P)).then_inc(wq_loaded, 16)
            sp.dma_start(WKR.rearrange("p (k o) -> p k o", k=KT),
                         wk.rearrange("(k p) o -> p k o", p=P)).then_inc(wk_loaded, 16)
            load_x(0, 0, first=True)
            sp.dma_start(WVR.rearrange("p (k o) -> p k o", k=KT),
                         weight.rearrange("(k p) o -> p k o", p=P)).then_inc(weight_loaded, 16)
            sp.dma_start(wg_raw[:, :].rearrange("p (k e) -> p k e", k=KT),
                         Wg.rearrange("(k p) e -> p k e", p=P)).then_inc(wg_loaded, 16)
            load_adj(0, first=True)
            load_x(1, 1, first=True)
            sp.dma_start(wraw[:, :].rearrange("p (k c) -> p k c", k=KT), w1_v[0]).then_inc(chunk_loaded, 16)
            load_adj(1)

            def load_rows(n, q, slot, free=True):
                row = sp.value_load(TAB[0:1, 1, bass.ds(slot, 1)], min_val=0, max_val=E * REGION - ROWS)
                if free:
                    sp.wait_ge(tile_psum, SUB * (n - RING + 1))
                    settle(sp)
                    sp.wait_ge(row_factors, 3 * (n - RING + 1))
                    settle(sp)
                src = sorted_x[bass.ds(row, ROWS), :].rearrange("(s p) n -> p s n", s=SUB)
                sp.dma_start(XF[:, q], src).then_inc(tile_loaded[q], 16)

            def load_halves(n, q, slot):
                sp.wait_ge(tile_psum, SUB * (n - RING + 1))
                settle(sp)
                sp.wait_ge(row_factors, 3 * (n - RING + 1))
                settle(sp)
                for s in range(SUB):
                    row = sp.value_load(TABU[0:1, 1, bass.ds(SUB * slot + (SUB + s), 1)],
                                        min_val=0, max_val=E * REGION - P)
                    sp.dma_start(XF[:, q, s, :], sorted_x[bass.ds(row, P), :]).then_inc(tile_loaded[q], 16)

            def graph(i, par, last=False):
                b = 2 * i + par
                if not last:
                    load_adj(b + 2)
                if not (last and par == 1):
                    if not (isinstance(b, int) and b == 0):
                        load_x(b + 1, 1 - par)
                    load_weights(i + par, 1 - par, b + 1)
                if last and par == 1:
                    sp.wait_ge(x2_ready, 4 * (B - 1))
                    sp.wait_ge(x1_stored, 16 * (B - 1))
                    sp.wait_ge(table_steps, N_EARLY)
                    for h in range(2):
                        sp.wait_ge(rows_scattered[h], 2 * JT * 16 * (B // 2 - 1))
                    load_rows(0, 0, 0, free=False)
                    load_rows(1, 1, 1, free=False)
                sp.wait_ge(x1_ready, 4 * (b + 1))
                settle(sp)
                sp.dma_start(out_v[b], X[:, par, :]).then_inc(x1_stored, 16)

            graph(0, 0)
            graph(0, 1)
            graph(1, 0)
            graph(1, 1)
            with sp.Fori(2, B // 2 - 1) as i:
                graph(i, 0)
                graph(i, 1)
            graph(B // 2 - 1, 0, last=True)
            graph(B // 2 - 1, 1, last=True)
            sp.wait_ge(x2_ready, 4 * B)
            sp.wait_ge(x1_stored, 16 * B)
            for n in range(2, EARLY):
                load_rows(n, n % RING, n, free=n >= RING)
            for par in range(2):
                sp.wait_ge(rows_scattered[par], 2 * JT * 16 * (B // 2))
            sp.wait_ge(table_steps, N_TAB)
            with sp.Fori(0, ROUNDS) as i:
                for t in range(ROUND):
                    n, q = EARLY + ROUND * i + t, (EARLY + t) % RING
                    if halved(t):
                        sp.wait_ge(pads_scattered, E * 16)
                        sp.wait_ge(factor_steps, N_HALVES)
                        load_halves(n, q, slot_of(i, t))
                    else:
                        load_rows(n, q, slot_of(i, t))

        @block.gpsimd
        def _(pool):
            pool.memset(ident[:, :], 0.0).then_inc(constants_ready, 1)
            pool.memset(ones16[:, :], 1.0).then_inc(constants_ready, 1)
            pool.memset(X2S[:, :, :, D:WIDE], 0.0).then_inc(constants_ready, 1)
            pool.memset(pad_rows[:, :], 0.0).then_inc(constants_ready, 1)
            pool.memset(minus_half[:, :], -0.5).then_inc(constants_ready, 1)
            pool.iota(expert_iota[:, :], pattern=[[1, E]], base=0, channel_multiplier=0,
                      allow_small_or_imprecise_dtypes=True).then_inc(constants_ready, 1)
            pool.iota(R[:, :], pattern=[[REGION, E]], base=0, channel_multiplier=0,
                      allow_small_or_imprecise_dtypes=True).then_inc(constants_ready, 1)
            pool.iota(base[:, :], pattern=[[REGION, E]], base=0, channel_multiplier=0,
                      allow_small_or_imprecise_dtypes=True).then_inc(constants_ready, 1)
            pool.iota(tile_iota[:, :], pattern=[[1, NF]], base=0, channel_multiplier=0,
                      allow_small_or_imprecise_dtypes=True).then_inc(constants_ready, 1)
            pool.iota(iota_p[:, :], pattern=[[0, E]], base=0, channel_multiplier=1,
                      allow_small_or_imprecise_dtypes=True).then_inc(constants_ready, 1)
            pool.memset(earlier[:, :, :], 1.0).then_inc(constants_ready, 1)
            pool.wait_ge(constants_ready, 11)
            for par in range(2):
                pool.iota(tokens(par), pattern=[[1, JT], [1, 1]], base=par * N,
                          channel_multiplier=JT).then_inc(constants_ready, 1)
            pool.iota(pad_rows[:, :].bitcast(I32)[:, D:D + 1], pattern=[[1, 1]], base=0,
                      channel_multiplier=JT).then_inc(constants_ready, 1)
            pool.affine_select(out=earlier[:, :, :], in_=earlier[:, :, :], compare_op=ALU.is_gt, fill=0.0, base=0,
                               pattern=[[1, E], [-1, E]], channel_multiplier=0).then_inc(constants_ready, 1)
            pool.affine_select(out=ident[:, :], in_=ident[:, :], compare_op=ALU.not_equal, fill=1.0, base=0,
                               pattern=[[-1, P]], channel_multiplier=1).then_inc(constants_ready, 1)
            pool.affine_select(out=before[:, :], in_=ones16[:, :], compare_op=ALU.is_gt, fill=0.0, base=0,
                               pattern=[[1, P]], channel_multiplier=-1).then_inc(constants_ready, 1)
            pool.wait_ge(constants_ready, 17)
            pool.tensor_copy(ident16[:, :], ident[:, :]).then_inc(constants_ready, 1)

            def layernorm_scale(b, q):
                s_m_v, s_ln, s_nb, scale = ((meanvar1, ln1_steps, ln1_scale, SX), (meanvar2, ln2_steps, ln2_scale, SX2))[q]
                n_ln = 3 * b
                pool.wait_ge(s_m_v, 4 * (b + 1))
                settle(pool)
                pool.tensor_scalar(ve[:, q, :], mv[:, q, :, 1], 1.0, EPS, ALU.mult, ALU.add).then_inc(s_ln, 1)
                pool.tensor_scalar(nm[:, q, :], mv[:, q, :, 0], -scale, 0.0, ALU.mult, ALU.add).then_inc(s_ln, 1)
                pool.wait_ge(s_ln, n_ln + 2)
                pool.tensor_tensor(rs[:, q, :], ve[:, q, :], minus_half[:, :], ALU.pow).then_inc(s_ln, 1)
                pool.wait_ge(s_ln, n_ln + 3)
                settle(pool)
                pool.tensor_scalar(rr[:, q, :], rs[:, q, :], scale, 0.0, ALU.mult, ALU.add).then_inc(s_nb, 1)
                pool.tensor_tensor(nb[:, q, :], nm[:, q, :], rs[:, q, :], ALU.mult).then_inc(s_nb, 1)

            layernorm_scale(0, 0)
            pool.wait_ge(part_max, 2)
            pool.partition_all_reduce(mxa[:, 1:3], mx[:, 1:3], P, RMAX).then_inc(all_max, 1)
            pool.wait_ge(part_max, 7)
            pool.partition_all_reduce(mxa[:, 0:1], mx[:, 0:1], P, RMAX).then_inc(all_max, 1)

            def rows(r, par, turn):
                pool.wait_ge(ln2_scale, 2 * (r + 1))
                if not isinstance(r, int) or r >= 2:
                    pool.wait_ge(rows_scattered[par], 2 * JT * 16 * turn)
                    pool.wait_ge(x2t_psum, 4 * (r - 1))
                settle(pool)
                for j in range(JT):
                    pool.tensor_scalar(X2S[:, par, j, 0:D], Xt(par, j), rr[:, 1, j:j + 1], nb[:, 1, j:j + 1],
                                       ALU.mult, ALU.add).then_inc(x2_ready, 1)

            def scatter(r, par):
                pool.wait_ge(slot_ready, 2 * (r + 1))
                settle(pool)
                pool.wait_ge(gate_steps, 6 * (r + 1))
                settle(pool)
                for j in range(JT):
                    for c in range(2):
                        pool.indirect_dma_start(
                            out=sorted_x, out_offset=bass.IndirectOffsetOnAxis(ap=slot[:, par, c, j:j + 1], axis=0),
                            in_=X2S[:, par, j, :], in_offset=None).then_inc(rows_scattered[par], 16)

            def largest(b):
                pool.wait_ge(chunk_max, b + 1)
                settle(pool)
                pool.partition_all_reduce(emxa[:, :], emx[:, :], P, RMAX).then_inc(chunk_max_all, 1)

            largest(0)

            def graph(i, par, last=False):
                b = 2 * i + par
                r = b - 1
                static = isinstance(b, int)
                if not static or b > 0:
                    layernorm_scale(r, 1)
                    rows(r, 1 - par, i - 1 + par)
                if not (last and par == 1):
                    layernorm_scale(b + 1, 0)
                if not static or b > 0:
                    scatter(r, 1 - par)
                if not (last and par == 1):
                    largest(b + 1)

            graph(0, 0)
            graph(0, 1)
            graph(1, 0)
            graph(1, 1)
            with pool.Fori(2, B // 2 - 1) as i:
                graph(i, 0)
                graph(i, 1)
            graph(B // 2 - 1, 0, last=True)
            graph(B // 2 - 1, 1, last=True)

            layernorm_scale(B - 1, 1)
            rows(B - 1, 1, B // 2 - 1)

            def pad(e):
                pool.indirect_dma_start(
                    out=sorted_x, out_offset=bass.IndirectOffsetOnAxis(ap=padrow[:, e:e + 1], axis=0),
                    in_=pad_rows[:, :], in_offset=None).then_inc(pads_scattered, 16)

            def add_rows(n, q, par, first=False, halves=False):
                pool.wait_ge(y_first, n + 1)
                pool.wait_ge(y_second, n + 1)
                if not first:
                    pool.wait_ge(y_added[1 - par], 16 * (n - par) + (0 if par == 0 else 32))
                settle(pool)
                for s in range(SUB):
                    if halves and s == 1:
                        pool.wait_ge(y_added[par], 16 * (n - par) + 16)
                        settle(pool)
                    pool.indirect_dma_start(
                        out=out_rows, out_offset=bass.IndirectOffsetOnAxis(ap=token[:, q, s:s + 1], axis=0),
                        in_=YF[:, par, s, :], in_offset=None, compute_op=ALU.add).then_inc(y_added[par], 16)

            pool.wait_ge(x1_stored, 16 * B)
            add_rows(0, 0, 0, first=True)
            scatter(B - 1, 1)
            for n in range(1, EARLY):
                add_rows(n, n % RING, n % 2)
                if n >= EARLY // 2:
                    if n == EARLY // 2:
                        pool.wait_ge(pad_steps, N_PAD)
                    pad(2 * n - EARLY)
                    pad(2 * n - EARLY + 1)
            with pool.Fori(0, ROUNDS) as i:
                for t in range(ROUND):
                    add_rows(EARLY + ROUND * i + t, (EARLY + t) % RING, t % 2, halves=halved(t))
            for par in range(2):
                pool.wait_ge(y_added[par], 32 * (NT // 2))

        @block.scalar
        def _(act):
            for t in range(0, 8, 2):
                act.wait_ge(wt_transposed, t + 1)
                dst = (WQT if t < 4 else WKT)[:, (t % 4) * D:(t % 4 + 1) * D]
                act.activation(dst, BANKS[t % 6][:, :], ACT.Copy).then_inc(wt_copied_act, 1)

            def xn_tiles(b, par, tiles=range(JT)):
                act.wait_ge(ln1_scale, 2 * (b + 1))
                for j in tiles:
                    if j == 0 and not isinstance(b, int):
                        act.wait_ge(xnt_psum, 4 * b)
                    elif j == 0 and b > 0:
                        act.wait_ge(xnt_psum, 4 * b)
                    act.activation(XN[:, j, :], Xt(par, j), ACT.Identity, scale=rr[:, 0, j:j + 1],
                                   bias=nb[:, 0, j:j + 1]).then_inc(xn_ready, 1)

            def xt_high(b, par, tiles=range(JT)):
                for j in tiles:
                    act.wait_ge(xnt_psum, 4 * b + j + 1)
                    act.activation(XTH[:, par, :, j * P:(j + 1) * P],
                                   TX[j % 2][:, :].rearrange("p (k n) -> p k n", k=KT), ACT.Copy).then_inc(xnt_high, 1)

            def mask_t(b, halves=range(2)):
                for h in halves:
                    act.wait_ge(mask_psum, 2 * b + h + 1)
                    act.activation(MKT[:, 2 * h:2 * h + 2, :].rearrange("p j n -> p (j n)"), MASKB[h],
                                   ACT.Copy).then_inc(maskt_ready, 1)

            def x2_t(r, j):
                act.wait_ge(x2t_psum, 4 * r + j + 1)
                if not isinstance(r, int) or r > 0 or j >= 2:
                    act.wait_ge(logits_psum, 4 * r + j - 1)
                act.activation(X2T[:, j % 2, 0:KT, :], TX[j % 2][:, :].rearrange("p (k n) -> p k n", k=KT),
                               ACT.Copy).then_inc(x2t_high, 1)

            def gate(r):
                act.wait_ge(logit_gap, r + 1)
                act.activation(gx[:, :], DL[:, :], ACT.Exp, scale=k_gate[:, 0:1]).then_inc(gate_exp, 1)

            def rows_high(n, par):
                for s in range(SUB):
                    act.wait_ge(tile_psum, SUB * n + s + 1)
                    act.activation(XFT[:, par, 0, :, s * P:(s + 1) * P],
                                   TX[s][:, :].rearrange("p (k n) -> p k n", k=KT), ACT.Copy).then_inc(tile_high, 1)

            xn_tiles(0, 0)
            xt_high(0, 0, [0, 1])
            act.wait_ge(scale_steps, 4)
            for k in range(KT):
                act.activation(WV[:, 0, k, :], WVR[:, k * D:(k + 1) * D], ACT.Copy, scale=wsc[:, 1:2]).then_inc(w_high, 1)
            act.activation(WG[:, :, 0, :], wg_raw[:, :].rearrange("p (k e) -> p k e", k=KT), ACT.Copy,
                           scale=wsc[:, 2:3]).then_inc(w_high, 1)
            xt_high(0, 0, [2, 3])
            mask_t(0)
            act.wait_ge(scale_steps, 10)
            for k in range(KT):
                act.activation(WM[:, 0, k, :], ACC[k][:, :], ACT.Copy, scale=wsc[:, 0:1]).then_inc(w_high, 1)

            def graph(i, par, last=False):
                b = 2 * i + par
                front = not (last and par == 1)

                def t_high(j):
                    act.wait_ge(t_psum, 4 * b + j + 1)
                    act.activation(TT[:, 0, j, :], ACC[j][:, :], ACT.Copy, scale=TO32).then_inc(t_high_ready, 1)

                for j in range(JT):
                    t_high(j)
                act.wait_ge(chunk_scale, 4 * (b + 1))
                settle(act)
                hi = (W1H if par == 0 else W2H)[:, bass.ds(i, 1), :].rearrange("p o n -> p (o n)")
                act.activation(hi, wraw[:, :], ACT.Copy, scale=esc[:, 0:1]).then_inc(chunk_high, 1)

                def relu(j):
                    act.wait_ge(scores_psum, 4 * b + j + 1)
                    act.activation(RL[:, j % 2, :], ACC[j][:, :], ACT.Relu).then_inc(relu_ready, 1)

                def exp_and_high(j):
                    act.wait_ge(exp_bias, 4 * b + j + 1)
                    act.activation(EX[:, j % 2, :], RL[:, j % 2, :], ACT.Exp, scale=k_pos[:, 0:1],
                                   bias=sbias[:, j:j + 1], accum_out=ssum[:, j:j + 1]).then_inc(exp_ready, 1)
                    act.wait_ge(prob_scale, 4 * b + j + 1)
                    act.activation(PR[:, 0, j, :], EX[:, j % 2, :], ACT.Copy, scale=srs[:, j:j + 1]).then_inc(prob_high, 1)

                routed = not isinstance(b, int) or b > 0
                relu(0)
                relu(1)
                for j in range(JT):
                    if j == JT - 1 and routed:
                        x2_t(b - 1, 0)
                        x2_t(b - 1, 1)
                    exp_and_high(j)
                    if j + 2 < JT:
                        relu(j + 2)
                for j in range(JT):
                    if j == 2 and routed:
                        x2_t(b - 1, 2)
                        x2_t(b - 1, 3)
                    if j == 3 and front:
                        xn_tiles(b + 1, 1 - par)
                    act.wait_ge(v_psum, 4 * b + j + 1)
                    act.activation(VV[:, 0, j, :], ACC[j][:, :], ACT.Copy, scale=TO32).then_inc(v_high, 1)
                if front:
                    xt_high(b + 1, 1 - par, [0, 1])
                    mask_t(b + 1, [0])
                if routed:
                    gate(b - 1)
                if front:
                    xt_high(b + 1, 1 - par, [2, 3])
                    mask_t(b + 1, [1])
                else:
                    rows_high(0, 0)

            graph(0, 0)
            graph(0, 1)
            graph(1, 0)
            graph(1, 1)
            with act.Fori(2, B // 2 - 1) as i:
                graph(i, 0)
                graph(i, 1)
            graph(B // 2 - 1, 0, last=True)
            graph(B // 2 - 1, 1, last=True)

            def hidden(n, par):
                act.wait_ge(hidden_psum, n + 1)
                act.activation(HH[:, par, 0, :], HB[par][:, :], ACT.Relu).then_inc(hidden_high, 1)

            def result(n, q, par, again=True):
                if again:
                    act.wait_ge(y_added[par], 16 * (n - par))
                act.wait_ge(row_factors, 3 * (n + 1))
                act.wait_ge(y_psum, 2 * n + 1)
                act.activation(YF[:, par, 0, :], YB[par][0][:, :], ACT.Copy,
                               scale=fr[:, q, 0:1]).then_inc(y_first, 1)

            rows_high(1, 1)
            hidden(0, 0)
            hidden(1, 1)
            x2_t(B - 1, 0)
            x2_t(B - 1, 1)
            result(0, 0, 0, again=False)
            x2_t(B - 1, 2)
            x2_t(B - 1, 3)
            rows_high(2, 0)
            rows_high(3, 1)
            gate(B - 1)
            hidden(2, 0)
            rows_high(4, 0)
            result(1, 1, 1, again=False)
            act.wait_ge(y_psum, 4)
            hidden(3, 1)
            result(2, 2, 0)

            def step(n, q, par, last=False):
                if not last:
                    rows_high(n + 1, 1 - par)
                hidden(n, par)
                result(n - 1, (q - 1) % RING, 1 - par)

            def steps(i, last=False):
                for t in range(ROUND):
                    step(EARLY + ROUND * i + t, (EARLY + t) % RING, t % 2, last=last and t == ROUND - 1)

            for n in range(4, EARLY):
                step(n, n % RING, n % 2)
            with act.Fori(0, ROUNDS - 1) as i:
                steps(i)
            steps(ROUNDS - 1, last=True)
            result(NT - 1, (NT - 1) % RING, 1)

        @block.vector
        def _(dve):
            def statistics(b, par, q):
                s_b, s_m_v = ((stats1, meanvar1), (stats2, meanvar2))[q]
                for j in range(JT):
                    if q:
                        dve.wait_ge(x1_ready, 4 * b + j + 1)
                    dve.bn_stats(bs[:, q, j, :], Xt(par, j)).then_inc(s_b, 1)
                dve.wait_ge(s_b, 4 * (b + 1))
                settle(dve)
                for j in range(JT):
                    dve.bn_aggr(mv[:, q, j, :], bs[:, q, j, :]).then_inc(s_m_v, 1)

            def route(r):
                dve.wait_ge(logits_psum, 4 * (r + 1))
                both = RB[:, 0:JT * 2 * E].rearrange("p (j c e) -> p j e c", j=JT, c=2)
                dve.tensor_reduce(LG[:, :, :], both, AX, ALU.add).then_inc(logits_read, 1)
                dve.wait_ge(logits_read, r + 1)
                settle(dve)
                for j in range(JT):
                    dve.max(top[:, j, :], LG[:, j, :]).then_inc(top_ready, 1)
                dve.wait_ge(top_ready, 4 * (r + 1))
                settle(dve)
                for j in range(JT):
                    dve.max_index(tix[:, j, :], top[:, j, :], LG[:, j, :]).then_inc(top_index, 1)
                dve.tensor_tensor(DL[:, :], top[:, :, 1], top[:, :, 0], ALU.subtract).then_inc(logit_gap, 1)
                dve.wait_ge(top_index, 4 * (r + 1))
                dve.tensor_copy(tixf[:, :, :], tix[:, :, 0:2].rearrange("p j c -> p c j")).then_inc(index_float, 1)
                dve.wait_ge(index_float, r + 1)
                for c in range(2):
                    dve.tensor_tensor(OH[:, c, :, :], tixf[:, c, :].unsqueeze(2).broadcast_to([P, JT, E]),
                                      expert_iota[:, :].unsqueeze(1).broadcast_to([P, JT, E]),
                                      ALU.is_equal).then_inc(onehot, 1)
                dve.wait_ge(onehot, 2 * (r + 1))
                dve.tensor_tensor(OHS[:, :, :], OH[:, 0, :, :], OH[:, 1, :, :], ALU.add).then_inc(onehot_sum, 1)
                if isinstance(r, int) and r == 0:
                    dve.wait_ge(onehot_sum, 1)
                    dve.tensor_copy(oh0[:, :], OHS[:, 0, :]).then_inc(first_tokens, 1)

            def place(r, par, turn):
                dve.wait_ge(positions_psum, r + 1)
                counts = RB[:, 64:64 + (JT + 1) * E].rearrange("p (j e) -> p j e", e=E)
                dve.tensor_tensor(row_of[:, :, :], counts[:, 0:JT, :], R[:, :].unsqueeze(1).broadcast_to([P, JT, E]),
                                  ALU.add).then_inc(positions_read, 1)
                dve.wait_ge(positions_read, 2 * r + 1)
                dve.tensor_tensor(R[:, :], R[:, :], counts[:, JT, :], ALU.add).then_inc(positions_read, 1)
                if isinstance(r, int) and r == 0:
                    dve.tensor_tensor(cex0[:, :], row_of[:, 0, :], base[:, :], ALU.subtract).then_inc(first_tokens, 1)
                for c in range(2):
                    dve.tensor_tensor(picked[:, c, :, :], OH[:, c, :, :], row_of[:, :, :], ALU.mult).then_inc(pick_steps, 1)
                dve.wait_ge(pick_steps, 3 * r + 2)
                dve.tensor_reduce(slotf[:, :, :], picked[:, :, :, :], AX, ALU.add).then_inc(pick_steps, 1)
                dve.wait_ge(pick_steps, 3 * r + 3)
                if not isinstance(r, int) or r >= 2:
                    dve.wait_ge(rows_scattered[par], 2 * JT * 16 * turn)
                settle(dve)
                dve.tensor_copy(slot[:, par, :, :], slotf[:, :, :]).then_inc(slot_ready, 1)
                if isinstance(r, int) and r < 2:
                    dve.sem_inc(slot_ready, 1)
                else:
                    dve.tensor_scalar(tokens(par), tokens(par), float(2 * N), None, ALU.add).then_inc(slot_ready, 1)
                n_g = 6 * r
                dve.wait_ge(gate_exp, r + 1)
                dve.tensor_scalar(gd[:, :], gx[:, :], 1.0, None, ALU.add).then_inc(gate_steps, 1)
                dve.wait_ge(gate_steps, n_g + 1)
                dve.reciprocal(gates[:, 0, :], gd[:, :]).then_inc(gate_steps, 1)
                dve.wait_ge(gate_steps, n_g + 2)
                dve.tensor_tensor(gates[:, 1, :], gx[:, :], gates[:, 0, :], ALU.mult).then_inc(gate_steps, 1)
                dve.wait_ge(gate_steps, n_g + 3)
                for c in range(2):
                    dve.tensor_tensor(gated[:, c, :, :], OH[:, c, :, :],
                                      gates[:, c, :].unsqueeze(2).broadcast_to([P, JT, E]),
                                      ALU.mult).then_inc(gate_steps, 1)
                dve.wait_ge(gate_steps, n_g + 5)
                dve.tensor_tensor(X2S[:, par, :, D + 1:D + 1 + E], gated[:, 0, :, :],
                                  gated[:, 1, :, :], ALU.add).then_inc(gate_steps, 1)

            def mask(b):
                dve.wait_ge(adj_loaded, 16 * (b + 1))
                if not (isinstance(b, int) and b == 0):
                    dve.wait_ge(mask_psum, 2 * b)
                dve.tensor_scalar(MK[:, :], ADJ[:, :], 0.0, None, ALU.not_equal).then_inc(mask_ready, 1)

            def xt_low(b, par, tiles=range(JT)):
                for j in tiles:
                    dve.wait_ge(xnt_high, 4 * b + j + 1)
                    dve.tensor_tensor(XTL[:, par, :, j * P:(j + 1) * P],
                                      TX[j % 2][:, :].rearrange("p (k n) -> p k n", k=KT),
                                      XTH[:, par, :, j * P:(j + 1) * P], ALU.subtract).then_inc(xnt_low, 1)

            def x2_low(r, j):
                dve.wait_ge(x2t_high, 4 * r + j + 1)
                dve.tensor_tensor(X2T[:, j % 2, KT:2 * KT, :], TX[j % 2][:, :].rearrange("p (k n) -> p k n", k=KT),
                                  X2T[:, j % 2, 0:KT, :], ALU.subtract).then_inc(x2t_low, 1)

            for t in range(1, 8, 2):
                dve.wait_ge(wt_transposed, t + 1)
                dst = (WQT if t < 4 else WKT)[:, (t % 4) * D:(t % 4 + 1) * D]
                dve.tensor_copy(dst, BANKS[t % 6][:, :]).then_inc(wt_copied_dve, 1)
            dve.wait_ge(x_loaded[0], 16)
            statistics(0, 0, 0)
            dve.wait_ge(weight_loaded, 16)
            dve.tensor_reduce(mx[:, 1:2], WVR, AX, ALU.max, apply_absolute_value=True).then_inc(part_max, 1)
            dve.wait_ge(wg_loaded, 16)
            dve.tensor_reduce(mx[:, 2:3], wg_raw[:, :], AX, ALU.max, apply_absolute_value=True).then_inc(part_max, 1)
            mask(0)

            def scales(lo, hi, n, back):
                m, e = mx[:, lo:hi], ebits[:, lo:hi]
                dve.tensor_scalar(m, mxa[:, lo:hi], 2.0 ** -90, 2.0 ** 90, ALU.max, ALU.min).then_inc(scale_steps, 1)
                dve.wait_ge(scale_steps, n + 1)
                dve.tensor_scalar(e, m.bitcast(I32), 0x7F800000, None, ALU.bitwise_and).then_inc(scale_steps, 1)
                dve.wait_ge(scale_steps, n + 2)
                dve.tensor_scalar(ibits[:, lo:hi], e, -1.0, float(254 << 23), ALU.mult, ALU.add).then_inc(scale_steps, 1)
                dve.wait_ge(scale_steps, n + 3)
                dve.tensor_scalar(wsc[:, lo:hi], ibits[:, lo:hi].bitcast(F32), SW, None, ALU.mult).then_inc(scale_steps, 1)
                for to, of, factor in back:
                    dve.tensor_scalar(to[:, :], ebits[:, of:of + 1].bitcast(F32), factor, None,
                                      ALU.mult).then_inc(scale_steps, 1)

            dve.wait_ge(all_max, 1)
            scales(1, 3, 0, ((g_res, 1, 1.0 / (SPROB * 32.0)), (k_gate, 2, 1.0 / (SX2 * SW))))
            xt_low(0, 0, [0, 1])
            dve.wait_ge(scale_steps, 6)
            for k in range(KT):
                dve.wait_ge(w_high, k + 1)
                dve.scalar_tensor_tensor(out=WV[:, 1, k, :], in0=WVR[:, k * D:(k + 1) * D], scalar=wsc[:, 1:2],
                                         in1=WV[:, 0, k, :], op0=ALU.mult, op1=ALU.subtract).then_inc(w_low, 1)
            dve.wait_ge(w_high, KT + 1)
            dve.scalar_tensor_tensor(out=WG[:, :, 1, :], in0=wg_raw[:, :].rearrange("p (k e) -> p k e", k=KT),
                                     scalar=wsc[:, 2:3], in1=WG[:, :, 0, :],
                                     op0=ALU.mult, op1=ALU.subtract).then_inc(w_low, 1)
            xt_low(0, 0, [2, 3])
            for k in range(KT):
                dve.wait_ge(m_ready, k + 1)
                dve.tensor_reduce(mxp[:, k:k + 1], ACC[k][:, :], AX, ALU.max,
                                  apply_absolute_value=True).then_inc(part_max, 1)
            dve.wait_ge(part_max, 6)
            dve.tensor_reduce(mx[:, 0:1], mxp[:, :], AX, ALU.max).then_inc(part_max, 1)
            dve.wait_ge(all_max, 2)
            scales(0, 1, 6, ((k_pos, 0, 1.0 / (SX * 32.0)), (k_neg, 0, -1.0 / (SX * 32.0))))
            dve.wait_ge(scale_steps, 12)
            for k in range(KT):
                dve.wait_ge(w_high, KT + k + 2)
                dve.scalar_tensor_tensor(out=WM[:, 1, k, :], in0=ACC[k][:, :], scalar=wsc[:, 0:1],
                                         in1=WM[:, 0, k, :], op0=ALU.mult, op1=ALU.subtract).then_inc(w_low, 1)

            def rows_low(n, par):
                for s in range(SUB):
                    dve.wait_ge(tile_high, SUB * n + s + 1)
                    dve.tensor_tensor(XFT[:, par, 1, :, s * P:(s + 1) * P],
                                      TX[s][:, :].rearrange("p (k n) -> p k n", k=KT),
                                      XFT[:, par, 0, :, s * P:(s + 1) * P], ALU.subtract).then_inc(tile_low, 1)

            def chain(signal, count, done=0):
                at = [done]

                def step(instruction):
                    at[0] += 1
                    assert at[0] <= count
                    instruction.then_inc(signal, 1)
                    dve.wait_ge(signal, at[0])
                return step

            def over(small, outer):
                return small[:, :].unsqueeze(1).broadcast_to([P, outer, E])

            def along(t, count):
                return t[:, 0:count].unsqueeze(2).broadcast_to([P, count, E])

            def full_tiles(step):
                step(dve.tensor_tensor(cnt[:, :], R[:, :], base[:, :], ALU.subtract))
                step(dve.tensor_copy(cnti[:, :], cnt[:, :]))
                step(dve.tensor_scalar(cnti[:, :], cnti[:, :], ROWS.bit_length() - 1, None, ALU.logical_shift_right))
                step(dve.tensor_copy(ntile[:, :], cnti[:, :]))

            def first_tiles(step):
                step(dve.tensor_tensor(tmpee[:, :, :], earlier[:, :, :], over(ntile, E), ALU.mult))
                step(dve.tensor_reduce(tstart[:, :], tmpee[:, :, :], AX, ALU.add))
                step(dve.tensor_tensor(tend[:, :], tstart[:, :], ntile[:, :], ALU.add))

            def tiles_experts(step, tiles, count):
                few_past, few_pastn = past[:, 0:count, :], pastn[:, 0:count, :]
                step(dve.tensor_tensor(few_past, along(tiles, count), over(tend, count), ALU.is_ge))
                step(dve.tensor_tensor(few_pastn, few_past, over(ntile, count), ALU.mult))
                step(dve.tensor_reduce(tex[:, 0:count], few_past, AX, ALU.add))
                step(dve.tensor_reduce(tst[:, 0:count], few_pastn, AX, ALU.add))

            def early_table():
                dve.wait_ge(positions_read, 2 * (B - 2))
                step = chain(table_steps, N_EARLY)
                full_tiles(step)
                first_tiles(step)
                tiles_experts(step, tile_iota, EARLY)
                step(dve.tensor_tensor(trow[:, 0:EARLY], tile_iota[:, 0:EARLY], tst[:, 0:EARLY], ALU.subtract))
                step(dve.tensor_scalar(trow[:, 0:EARLY], trow[:, 0:EARLY], float(ROWS), None, ALU.mult))
                step(dve.scalar_tensor_tensor(out=TAB[:, 1, 0:EARLY], in0=tex[:, 0:EARLY], scalar=float(REGION),
                                              in1=trow[:, 0:EARLY], op0=ALU.mult, op1=ALU.add))
                step(dve.tensor_copy(TAB[:, 0, 0:EARLY], tex[:, 0:EARLY]))

            def early_factors():
                step = chain(factor_steps, N_EARLY_WX)
                dve.wait_ge(chunk_scale, 4 * B)
                ef = eebits[:, :].bitcast(F32)
                step(dve.tensor_tensor(to_y[:, :], ef[:, 0:E], ef[:, E:2 * E], ALU.mult))
                step(dve.tensor_scalar(to_y[:, :], to_y[:, :], TO_Y, None, ALU.mult))
                step(dve.tensor_tensor(past[:, 0:EARLY, :], along(tex, EARLY), over(expert_iota, EARLY), ALU.is_equal))
                step(dve.tensor_tensor(WX[:, 0:EARLY, :], past[:, 0:EARLY, :], over(to_y, EARLY), ALU.mult))
                step(dve.tensor_reduce(taken[:, :], past[:, 0:EARLY, :].rearrange("p t e -> p e t"), AX, ALU.add))
                step(dve.tensor_scalar(rest[:, :], taken[:, :], float(ROWS), None, ALU.mult))
                step(dve.tensor_tensor(rest[:, :], rest[:, :], base[:, :], ALU.add))

            def table():
                dve.wait_ge(positions_read, 2 * B)
                late = NF - EARLY
                step = chain(table_steps, N_TAB, N_EARLY)
                full_tiles(step)
                step(dve.tensor_tensor(ntile[:, :], ntile[:, :], taken[:, :], ALU.subtract))
                first_tiles(step)
                tiles_experts(step, tile_iota, late)
                step(dve.tensor_tensor(trow[:, 0:late], tile_iota[:, 0:late], tst[:, 0:late], ALU.subtract))
                step(dve.tensor_tensor(past[:, 0:late, :], along(tex, late), over(expert_iota, late), ALU.is_equal))
                step(dve.tensor_tensor(pastn[:, 0:late, :], past[:, 0:late, :], over(rest, late), ALU.mult))
                step(dve.tensor_reduce(tst[:, 0:late], pastn[:, 0:late, :], AX, ALU.add))
                step(dve.scalar_tensor_tensor(out=TAB[:, 1, EARLY:NF], in0=trow[:, 0:late], scalar=float(ROWS),
                                              in1=tst[:, 0:late], op0=ALU.mult, op1=ALU.add))
                step(dve.tensor_copy(TAB[:, 0, EARLY:NF], tex[:, 0:late]))

            def padding():
                dve.wait_ge(first_tokens, 2)
                step = chain(pad_steps, N_PAD)
                step(dve.tensor_scalar(dump[:, :], iota_p[:, 0:1], float(E * REGION), None, ALU.add))
                step(dve.tensor_scalar(few[:, :], cnt[:, :], float(P), None, ALU.is_lt))
                step(dve.tensor_tensor(bad[:, :], oh0[:, :], few[:, :], ALU.mult))
                step(dve.tensor_tensor(dpos[:, :], cex0[:, :], few[:, :], ALU.mult))
                step(dve.tensor_tensor(pos0[:, :], iota_p[:, :], dpos[:, :], ALU.subtract))
                step(dve.tensor_tensor(pos0[:, :], pos0[:, :], R[:, :], ALU.add))
                step(dve.tensor_scalar(dpos[:, :], pos0[:, :], -1.0, dump[:, 0:1], ALU.mult, ALU.add))
                step(dve.tensor_tensor(dpos[:, :], dpos[:, :], bad[:, :], ALU.mult))
                step(dve.tensor_tensor(padrow[:, :], pos0[:, :], dpos[:, :], ALU.add))

            def halves_counts():
                late = NF - EARLY
                step = chain(factor_steps, N_COUNTS, N_EARLY_WX)
                step(dve.tensor_tensor(WX[:, EARLY:NF, :], past[:, 0:late, :], over(to_y, late), ALU.mult))
                step(dve.tensor_reduce(used[:, :], past[:, 0:late, :].rearrange("p t e -> p e t"), AX, ALU.add))
                step(dve.scalar_tensor_tensor(out=rest[:, :], in0=used[:, :], scalar=float(ROWS), in1=rest[:, :],
                                              op0=ALU.mult, op1=ALU.add))
                step(dve.tensor_tensor(used[:, :], used[:, :], taken[:, :], ALU.add))
                step(dve.tensor_scalar(ntile[:, :], cnt[:, :], float(P - 1), None, ALU.add))
                step(dve.tensor_copy(cnti[:, :], ntile[:, :]))
                step(dve.tensor_scalar(cnti[:, :], cnti[:, :], P.bit_length() - 1, None, ALU.logical_shift_right))
                step(dve.tensor_copy(ntile[:, :], cnti[:, :]))
                step(dve.scalar_tensor_tensor(out=ntile[:, :], in0=used[:, :], scalar=-float(SUB), in1=ntile[:, :],
                                              op0=ALU.mult, op1=ALU.add))
                first_tiles(step)

            def halves_table():
                step = chain(factor_steps, N_HALVES, N_COUNTS)
                step(dve.tensor_scalar(total1[:, :], tend[:, E - 1:E], -1.0, None, ALU.add))
                step(dve.tensor_scalar(tin[:, 0:UNITS], tile_iota[:, 0:UNITS], total1[:, 0:1], None, ALU.min))
                tiles_experts(step, tin, UNITS)
                units, unitsn = past[:, 0:UNITS, :], pastn[:, 0:UNITS, :]
                step(dve.tensor_tensor(trow[:, 0:UNITS], tin[:, 0:UNITS], tst[:, 0:UNITS], ALU.subtract))
                step(dve.tensor_tensor(units, along(tex, UNITS), over(expert_iota, UNITS), ALU.is_equal))
                step(dve.tensor_tensor(unitsn, units, over(rest, UNITS), ALU.mult))
                step(dve.tensor_reduce(tst[:, 0:UNITS], unitsn, AX, ALU.add))
                step(dve.scalar_tensor_tensor(out=TABU[:, 1, SUB:], in0=trow[:, 0:UNITS], scalar=float(P),
                                              in1=tst[:, 0:UNITS], op0=ALU.mult, op1=ALU.add))
                step(dve.tensor_copy(TABU[:, 0, SUB:], tex[:, 0:UNITS]))
                step(dve.tensor_copy(TABU[:, 0, 0:SUB], TAB[:, 0, EARLY - 1:EARLY].broadcast_to([P, SUB])))

            def halves_factors():
                units, unitsn = past[:, 0:UNITS, :], pastn[:, 0:UNITS, :]
                step = chain(factor_steps, N_WX, N_HALVES)
                step(dve.tensor_scalar(valid[:, 0:UNITS], tile_iota[:, 0:UNITS], total1[:, 0:1], None, ALU.is_le))
                step(dve.tensor_tensor(unitsn, units, along(valid, UNITS), ALU.mult))
                step(dve.tensor_tensor(WX[:, NF:, :], unitsn, over(to_y, UNITS), ALU.mult))

            def largest(b):
                dve.wait_ge(chunk_loaded, 16 * (b + 1))
                dve.tensor_reduce(emx[:, :], wraw[:, :], AX, ALU.max, apply_absolute_value=True).then_inc(chunk_max, 1)

            largest(0)

            def graph(i, par, last=False):
                b = 2 * i + par
                front = not (last and par == 1)
                routed = not isinstance(b, int) or b > 0

                def weight_scale():
                    dve.wait_ge(chunk_max_all, b + 1)
                    dve.tensor_scalar(emx[:, :], emxa[:, :], 2.0 ** -60, 2.0 ** 60, ALU.max,
                                      ALU.min).then_inc(chunk_scale, 1)
                    dve.wait_ge(chunk_scale, 4 * b + 1)
                    eb = eebits[:, bass.ds(i + E * par, 1)]
                    dve.tensor_scalar(eb, emx[:, :].bitcast(I32), 0x7F800000, None, ALU.bitwise_and).then_inc(chunk_scale, 1)
                    dve.wait_ge(chunk_scale, 4 * b + 2)
                    dve.tensor_scalar(eibits[:, :], eb, -1.0, float(254 << 23), ALU.mult, ALU.add).then_inc(chunk_scale, 1)
                    dve.wait_ge(chunk_scale, 4 * b + 3)
                    dve.tensor_scalar(esc[:, :], eibits[:, :].bitcast(F32), SW if par else SW1, None,
                                      ALU.mult).then_inc(chunk_scale, 1)

                for j in range(JT):
                    dve.wait_ge(t_high_ready, 4 * b + j + 1)
                    dve.scalar_tensor_tensor(out=TT[:, 1, j, :], in0=ACC[j][:, :], scalar=TO32, in1=TT[:, 0, j, :],
                                             op0=ALU.mult, op1=ALU.subtract).then_inc(t_low_ready, 1)
                    if j == 1:
                        weight_scale()
                    if j == 2 and front:
                        mask(b + 1)
                dve.wait_ge(chunk_high, b + 1)
                settle(dve)
                sl = bass.ds(i, 1)
                hi, lo = (W1H, W1L) if par == 0 else (W2H, W2L)
                dve.scalar_tensor_tensor(out=lo[:, sl, :].rearrange("p o n -> p (o n)"), in0=wraw[:, :],
                                         scalar=esc[:, 0:1], in1=hi[:, sl, :].rearrange("p o n -> p (o n)"),
                                         op0=ALU.mult, op1=ALU.subtract).then_inc(chunk_low, 1)

                def masked_max(j):
                    dve.wait_ge(relu_ready, 4 * b + j + 1)
                    if j == 0:
                        dve.wait_ge(maskt_ready, 2 * (b + 1))
                    settle(dve)
                    rl = RL[:, j % 2, :]
                    dve.tensor_tensor_reduce(rl, rl, MKT[:, j, :], 1.0, 0.0, ALU.mult, ALU.max,
                                             smax[:, j:j + 1]).then_inc(score_max, 1)
                    dve.wait_ge(score_max, 4 * b + j + 1)
                    dve.tensor_scalar(sbias[:, j:j + 1], smax[:, j:j + 1], k_neg[:, 0:1], None,
                                      ALU.mult).then_inc(exp_bias, 1)

                def inverse_sum(j):
                    dve.wait_ge(exp_ready, 4 * b + j + 1)
                    dve.reciprocal(srec[:, j:j + 1], ssum[:, j:j + 1]).then_inc(sum_inverse, 1)
                    dve.wait_ge(sum_inverse, 4 * b + j + 1)
                    dve.tensor_scalar(srs[:, j:j + 1], srec[:, j:j + 1], SPROB, None, ALU.mult).then_inc(prob_scale, 1)

                def prob_low(j):
                    dve.wait_ge(prob_high, 4 * b + j + 1)
                    dve.scalar_tensor_tensor(out=PR[:, 1, j, :], in0=EX[:, j % 2, :], scalar=srs[:, j:j + 1],
                                             in1=PR[:, 0, j, :], op0=ALU.mult, op1=ALU.subtract).then_inc(prob_low_ready, 1)

                masked_max(0)
                masked_max(1)
                for j in range(JT):
                    if j == JT - 1 and routed:
                        x2_low(b - 1, 0)
                        x2_low(b - 1, 1)
                    inverse_sum(j)
                    prob_low(j)
                    if j + 2 < JT:
                        masked_max(j + 2)

                if front:
                    dve.wait_ge(x_loaded[1 - par], 16 * (i + 1 + par))
                    statistics(b + 1, 1 - par, 0)
                if routed:
                    x2_low(b - 1, 2)
                    x2_low(b - 1, 3)
                for j in range(JT):
                    if j == 2 and not front:
                        early_table()
                    dve.wait_ge(v_high, 4 * b + j + 1)
                    dve.scalar_tensor_tensor(out=VV[:, 1, j, :], in0=ACC[j][:, :], scalar=TO32, in1=VV[:, 0, j, :],
                                             op0=ALU.mult, op1=ALU.subtract).then_inc(v_low, 1)
                if front:
                    xt_low(b + 1, 1 - par, [0, 1])
                if routed:
                    route(b - 1)
                if not front:
                    early_factors()
                for j in range(JT):
                    if j == 1 and front:
                        xt_low(b + 1, 1 - par, [2, 3])
                    if j == 2 and not front:
                        rows_low(0, 0)
                    dve.wait_ge(attention_psum, 4 * b + j + 1)
                    dve.scalar_tensor_tensor(out=Xt(par, j), in0=ACC[j][:, :], scalar=g_res[:, 0:1], in1=Xt(par, j),
                                             op0=ALU.mult, op1=ALU.add).then_inc(x1_ready, 1)
                    if j == 1 and routed:
                        place(b - 1, 1 - par, i - 1 + par)
                    if j == 2 and front:
                        largest(b + 1)
                statistics(b, par, 1)

            graph(0, 0)
            graph(0, 1)
            graph(1, 0)
            graph(1, 1)
            with dve.Fori(2, B // 2 - 1) as i:
                graph(i, 0)
                graph(i, 1)
            graph(B // 2 - 1, 0, last=True)
            graph(B // 2 - 1, 1, last=True)

            def hidden(n, par):
                dve.wait_ge(hidden_high, n + 1)
                dve.scalar_tensor_tensor(out=HH[:, par, 1, :], in0=HB[par][:, :], scalar=0.0, in1=HH[:, par, 0, :],
                                         op0=ALU.max, op1=ALU.subtract).then_inc(hidden_low, 1)

            def factors(n, q, par, slot, turn, halves=False):
                dve.wait_ge(tile_loaded[q], turn)
                if not isinstance(n, int) or n >= RING:
                    dve.wait_ge(y_first, n - RING + 1)
                    dve.wait_ge(y_added[1 - par], 16 * (n - RING - (1 - par)) + 32)
                settle(dve)
                dve.tensor_copy(token[:, q, :].unsqueeze(2), XF[:, q, :, :].bitcast(I32)[:, :, D:D + 1]).then_inc(row_factors, 1)
                wx = WX[:, bass.ds(SUB * slot + NF, SUB), :] if halves else WX[
                    :, bass.ds(slot, 1), :].broadcast_to([P, SUB, E])
                dve.tensor_tensor(gsel[:, q, :, :], XF[:, q, :, D + 1:D + 1 + E], wx, ALU.mult).then_inc(row_factors, 1)
                dve.wait_ge(row_factors, 3 * n + 2)
                settle(dve)
                dve.tensor_reduce(fr[:, q, :], gsel[:, q, :, :], AX, ALU.add).then_inc(row_factors, 1)

            def result(n, q, par, again=True):
                if again:
                    dve.wait_ge(y_added[par], 16 * (n - par))
                dve.wait_ge(row_factors, 3 * (n + 1))
                dve.wait_ge(y_psum, 2 * n + 2)
                dve.tensor_scalar(YF[:, par, 1, :], YB[par][1][:, :], fr[:, q, 1:2], None,
                                  ALU.mult).then_inc(y_second, 1)

            rows_low(1, 1)
            hidden(0, 0)
            hidden(1, 1)
            x2_low(B - 1, 0)
            x2_low(B - 1, 1)
            factors(0, 0, 0, 0, 16)
            result(0, 0, 0, again=False)
            x2_low(B - 1, 2)
            x2_low(B - 1, 3)
            factors(1, 1, 1, 1, 16)
            rows_low(2, 0)
            route(B - 1)
            rows_low(3, 1)
            factors(2, 2, 0, 2, 16)
            factors(3, 3, 1, 3, 16)
            hidden(2, 0)
            place(B - 1, 1, B // 2 - 1)
            rows_low(4, 0)
            result(1, 1, 1, again=False)
            hidden(3, 1)
            table()
            result(2, 2, 0)

            def step(n, q, par, slot, turn, halves=False, last=False):
                if not last:
                    rows_low(n + 1, 1 - par)
                hidden(n, par)
                result(n - 1, (q - 1) % RING, 1 - par)
                factors(n, q, par, slot, turn, halves)

            def steps(i, last=False):
                for t in range(ROUND):
                    step(EARLY + ROUND * i + t, (EARLY + t) % RING, t % 2, slot_of(i, t), loaded(i, t),
                         halves=halved(t), last=last and t == ROUND - 1)

            for n in range(4, EARLY):
                step(n, n % RING, n % 2, n, 16 * (n // RING + 1))
                if n == 4:
                    padding()
                if n == 5:
                    halves_counts()
                if n == 6:
                    halves_table()
                if n == 7:
                    halves_factors()
            with dve.Fori(0, ROUNDS - 1) as i:
                steps(i)
            steps(ROUNDS - 1, last=True)
            result(NT - 1, (NT - 1) % RING, 1)

        @block.tensor
        def _(pe):
            def product(bank, left, right, terms, arrive=None):
                last = None
                for k in range(terms):
                    if arrive is not None:
                        arrive(k)
                    for n, (a, c) in enumerate(((0, 0), (0, 1), (1, 0))):
                        last = pe.matmul(bank, left(a, k), right(c, k), start=(k == 0 and n == 0),
                                         stop=(k == terms - 1 and n == 2))
                return last

            pe.wait_ge(constants_ready, 18)
            for t in range(8):
                if t == 0:
                    pe.wait_ge(wq_loaded, 16)
                if t == 4:
                    pe.wait_ge(wk_loaded, 16)
                if t >= 6:
                    pe.wait_ge(wt_copied_act, 1)
                    pe.wait_ge(wt_copied_dve, 1)
                raw = WQR if t < 4 else WKR
                for k in range(KT):
                    o = k * D + (t % 4) * P
                    mm = pe.transpose(BANKS[t % 6][:, k * P:(k + 1) * P], raw[:, o:o + P], ident[:, :])
                mm.then_inc(wt_transposed, 1)
            pe.wait_ge(wt_copied_act, 4)
            pe.wait_ge(wt_copied_dve, 4)
            def xt(b, tiles=range(JT)):
                for j in tiles:
                    pe.wait_ge(xn_ready, 4 * b + j + 1)
                    if not isinstance(b, int) or b > 0 or j >= 2:
                        pe.wait_ge(xnt_low, 4 * b + j - 1)
                    if j == 0 and not (isinstance(b, int) and b == 0):
                        pe.wait_ge(maskt_ready, 2 * b)
                    if j < 2 and not (isinstance(b, int) and b < 2):
                        pe.wait_ge(x2t_low, 4 * (b - 1))
                    for k in range(KT):
                        mm = pe.transpose(TX[j % 2][:, k * P:(k + 1) * P], XN[:, j, k * P:(k + 1) * P], ident[:, :])
                    mm.then_inc(xnt_psum, 1)

            def mask_t(b, halves=range(2)):
                pe.wait_ge(mask_ready, b + 1)
                cols = MK[:, :].rearrange("p (n m j) -> p n j m", n=JT, j=JT)
                for h in halves:
                    if h == 1:
                        pe.wait_ge(xnt_low, 4 * (b + 1))
                    for j in range(2):
                        for n in range(JT):
                            o = j * N + n * P
                            mm = pe.transpose(MASKB[h][:, o:o + P], cols[:, n, 2 * h + j, :], ident16[:, :])
                    mm.then_inc(mask_psum, 1)

            def x2_t(r, par, j, b=None):
                pe.wait_ge(x2_ready, 4 * r + j + 1)
                if j >= 2:
                    pe.wait_ge(x2t_low, 4 * r + j - 1)
                elif b is not None:
                    pe.wait_ge(xnt_low, 4 * b + 3 + j)
                    if j == 0:
                        pe.wait_ge(maskt_ready, 2 * (b + 1))
                else:
                    pe.wait_ge(tile_low, SUB * 2)
                for k in range(KT):
                    mm = pe.transpose(TX[j % 2][:, k * P:(k + 1) * P], X2S[:, par, j, k * P:(k + 1) * P], ident[:, :])
                mm.then_inc(x2t_psum, 1)

            def logits(r, j):
                pe.wait_ge(x2t_low, 4 * r + j + 1)
                if j == 0 and (not isinstance(r, int) or r > 0):
                    pe.wait_ge(logits_read, r)
                    pe.wait_ge(positions_read, 2 * r)
                o = j * 2 * E
                for k in range(KT):
                    pe.matmul(RB[:, o:o + 2 * E], X2T[:, j % 2, k, :], WG[:, k, :, :].rearrange("p c e -> p (c e)"),
                              start=(k == 0), stop=(k == KT - 1), skip_group_check=True)
                for k in range(KT):
                    mm = pe.matmul(RB[:, o:o + E], X2T[:, j % 2, KT + k, :], WG[:, k, 0, :],
                                   start=False, stop=(k == KT - 1), skip_group_check=True)
                mm.then_inc(logits_psum, 1)

            def positions(r):
                pe.wait_ge(onehot_sum, r + 1)
                out0 = 64
                pe.matmul(RB[:, out0:out0 + JT * E], before[:, :], OHS[:, :, :].rearrange("p j e -> p (j e)"),
                          start=True, stop=False, skip_group_check=True)
                for j in range(JT):
                    mm = pe.matmul(RB[:, out0 + (j + 1) * E:out0 + (JT + 1) * E], ones16[:, :],
                                   OHS[:, j, :].unsqueeze(1).broadcast_to([P, JT - j, E]),
                                   start=False, stop=(j == JT - 1), skip_group_check=True)
                mm.then_inc(positions_psum, 1)

            def rows_t(n, q, turn):
                pe.wait_ge(tile_loaded[q], turn)
                for s in range(SUB):
                    if not isinstance(n, int) or n > 0:
                        pe.wait_ge(tile_low, SUB * (n - 1) + s + 1)
                    for k in range(KT):
                        mm = pe.transpose(TX[s][:, k * P:(k + 1) * P], XF[:, q, s, k * P:(k + 1) * P], ident[:, :])
                    mm.then_inc(tile_psum, 1)

            for m in range(KT):
                for k in range(KT):
                    mm = pe.matmul(ACC[m][:, :], WQT[:, k * D + m * P:k * D + (m + 1) * P],
                                   WKT[:, k * D:(k + 1) * D], start=(k == 0), stop=(k == KT - 1))
                mm.then_inc(m_ready, 1)
                if m in (1, 2):
                    xt(0, [2 * m - 2, 2 * m - 1])
            mask_t(0)

            def graph(i, par, last=False):
                b = 2 * i + par
                front = not (last and par == 1)
                XA = (XTH[:, par], XTL[:, par])

                pe.wait_ge(xnt_low, 4 * (b + 1))
                for j in range(JT):
                    if not isinstance(b, int) or b > 0:
                        pe.wait_ge(x1_ready, 4 * b - 3 + j)
                    first = isinstance(b, int) and b == 0 and j == 0
                    product(ACC[j][:, :], lambda a, k: WM[:, a, k, j * P:(j + 1) * P],
                            lambda c, k: XA[c][:, k, :], KT,
                            lambda k: pe.wait_ge(w_low, KT + k + 2) if first else None).then_inc(t_psum, 1)
                for j in range(JT):
                    product(ACC[j][:, :], lambda a, k: XA[a][:, k, j * P:(j + 1) * P],
                            lambda c, k: TT[:, c, k, :], KT,
                            lambda k: pe.wait_ge(t_low_ready, 4 * b + k + 1) if j == 0 else None).then_inc(scores_psum, 1)
                routed = not isinstance(b, int) or b > 0
                if routed:
                    x2_t(b - 1, 1 - par, 0, b)
                    x2_t(b - 1, 1 - par, 1, b)
                for j in range(JT):
                    pe.wait_ge(relu_ready, 4 * b + j + 1)
                    product(ACC[j][:, :], lambda a, k: XA[a][:, k, j * P:(j + 1) * P],
                            lambda c, k: WV[:, c, k, :], KT).then_inc(v_psum, 1)
                    if j == 1 and routed:
                        for t in (0, 1):
                            logits(b - 1, t)
                        for t in (2, 3):
                            x2_t(b - 1, 1 - par, t, b)
                    if j == 3 and routed:
                        for t in (2, 3):
                            logits(b - 1, t)
                if front:
                    xt(b + 1, [0, 1])
                    mask_t(b + 1, [0])
                pe.wait_ge(prob_low_ready, 4 * (b + 1))
                for j in range(JT):
                    product(ACC[j][:, :], lambda a, k: PR[:, a, k, j * P:(j + 1) * P],
                            lambda c, k: VV[:, c, k, :], JT,
                            lambda k: pe.wait_ge(v_low, 4 * b + k + 1) if j == 0 else None).then_inc(attention_psum, 1)
                    if j == 0 and front:
                        xt(b + 1, [2, 3])
                    if j == 1 and routed:
                        positions(b - 1)
                    if j == 1 and front:
                        mask_t(b + 1, [1])
                    if j == 2 and not front:
                        pe.wait_ge(xnt_low, 4 * B)
                        pe.wait_ge(maskt_ready, 2 * B)
                        pe.wait_ge(x2t_low, 4 * (B - 1))
                        rows_t(0, 0, 16)

            graph(0, 0)
            graph(0, 1)
            graph(1, 0)
            graph(1, 1)
            with pe.Fori(2, B // 2 - 1) as i:
                graph(i, 0)
                graph(i, 1)
            graph(B // 2 - 1, 0, last=True)
            graph(B // 2 - 1, 1, last=True)
            def hidden(n, par, experts):
                pe.wait_ge(tile_low, SUB * (n + 1))
                if not isinstance(n, int) or n > 1:
                    pe.wait_ge(hidden_low, n - 1)
                settle(pe)
                W = (W1H, W1L)
                width = ROWS // len(experts)
                for h, e in enumerate(experts):
                    w = e * (KT * C)
                    o = h * width
                    for m in range(CT):
                        mm = product(HB[par][:, m * ROWS + o:m * ROWS + o + width],
                                     lambda a, k: W[a][:, :, :].rearrange("p e n -> p (e n)")[
                                         :, bass.ds(w + (k * C + m * P), P)],
                                     lambda c, k: XFT[:, par, c, k, o:o + width], KT)
                mm.then_inc(hidden_psum, 1)

            def expert_out(n, par, experts):
                pe.wait_ge(hidden_high, n + 1)
                pe.wait_ge(hidden_low, n + 1)
                W = (W2H, W2L)
                for s in range(SUB):
                    w = experts[s % len(experts)] * (CT * D)
                    if not isinstance(n, int) or n > 1:
                        pe.wait_ge((y_first, y_second)[s], n - 1)
                    product(YB[par][s][:, :],
                            lambda a, m: HH[:, par, a, m * ROWS + s * P:m * ROWS + (s + 1) * P],
                            lambda c, m: W[c][:, :, :].rearrange("p e n -> p (e n)")[:, bass.ds(w + m * D, D)],
                            CT).then_inc(y_psum, 1)

            def expert(slot):
                return [pe.value_load(TAB[0:1, 0, bass.ds(slot, 1)], min_val=0, max_val=E - 1)]

            def experts_of_halves(slot):
                return [pe.value_load(TABU[0:1, 0, bass.ds(SUB * slot + (SUB + s), 1)],
                                      min_val=0, max_val=E - 1) for s in range(SUB)]

            def steps(i, last=False):
                es = [experts_of_halves(2 * i - 1)]
                for t in range(ROUND):
                    n, par = EARLY + ROUND * i + t, t % 2
                    es.append((experts_of_halves if halved(t) else expert)(slot_of(i, t)))
                    if not (last and t == ROUND - 1):
                        turn = loaded(i, t + 1) if t < ROUND - 1 else loaded(i + 1, 0)
                        rows_t(n + 1, (EARLY + t + 1) % RING, turn)
                    hidden(n, par, es[t + 1])
                    expert_out(n - 1, 1 - par, es[t])
                return es[ROUND]

            pe.wait_ge(chunk_low, B)
            pe.wait_ge(table_steps, N_EARLY)
            e0, e1, e2, e3 = [expert(n) for n in range(4)]
            rows_t(1, 1, 16)
            pe.wait_ge(x1_ready, 4 * (B - 1) + 2)
            hidden(0, 0, e0)
            hidden(1, 1, e1)
            x2_t(B - 1, 1, 0)
            x2_t(B - 1, 1, 1)
            pe.wait_ge(x1_ready, 4 * B)
            expert_out(0, 0, e0)
            logits(B - 1, 0)
            logits(B - 1, 1)
            x2_t(B - 1, 1, 2)
            x2_t(B - 1, 1, 3)
            logits(B - 1, 2)
            logits(B - 1, 3)
            rows_t(2, 2, 16)
            rows_t(3, 3, 16)
            hidden(2, 0, e2)
            positions(B - 1)
            hidden(3, 1, e3)
            rows_t(4, 4, 16)
            pe.wait_ge(positions_read, 2 * B)
            expert_out(1, 1, e1)
            expert_out(2, 0, e2)
            e_before = e3
            for n in range(4, EARLY):
                e = expert(n)
                rows_t(n + 1, (n + 1) % RING, 16 * ((n + 1) // RING + 1))
                hidden(n, n % 2, e)
                expert_out(n - 1, 1 - n % 2, e_before)
                e_before = e
            pe.wait_ge(table_steps, N_TAB)
            pe.wait_ge(factor_steps, N_HALVES)
            with pe.Fori(0, ROUNDS - 1) as i:
                steps(i)
            expert_out(NT - 1, 1, steps(ROUNDS - 1, last=True))


_INS = ['x', 'adj', 'L0_gnn_weight', 'L0_gnn_wq', 'L0_gnn_wk', 'L0_ffn_Wg', 'L0_ffn_W1', 'L0_ffn_W2']
_OUTS = [((16, 512, 512), 'float32')]


def kernel(**inputs):
    import numpy as _np
    import concourse.bacc as _bacc
    from concourse import mybir as _mybir
    from concourse.bass_utils import run_bass_kernel_spmd as _run

    nc = _bacc.Bacc("TRN2", target_bir_lowering=False, num_devices=1)
    arrays, args = {}, []
    for name in _INS:
        a = _np.ascontiguousarray(inputs[name])
        arrays[f"in_{name}_dram"] = a
        args.append(nc.dram_tensor(f"in_{name}_dram", a.shape, _mybir.dt.from_np(a.dtype), kind="ExternalInput").ap())
    for i, (shape, dtype) in enumerate(_OUTS):
        dt = _mybir.dt.from_np(_np.dtype(dtype))
        args.append(nc.dram_tensor(f"out_{i}_dram", shape, dt, kind="ExternalOutput").ap())
    build_program(nc, *args)
    r = _run(nc, [arrays], core_ids=[0])
    got = tuple(r.results[0][f"out_{i}_dram"] for i in range(len(_OUTS)))
    return got[0]
```
